# Optimizing a Trainium2 kernel written in Bass

```python
import numpy as np
import jax
import jax.numpy as jnp

def _softmax(x, axis=-1):
    return jax.nn.softmax(x, axis=axis)

def _gelu(x):
    return jax.nn.gelu(x, approximate=True)

def _silu(x):
    return jax.nn.silu(x)

def _sigmoid(x):
    return jax.nn.sigmoid(x)

def _layernorm(x, axis=-1, eps=1e-05):
    m = jnp.mean(x, axis=axis, keepdims=True)
    v = jnp.var(x, axis=axis, keepdims=True)
    return (x - m) / jnp.sqrt(v + eps)

def _scatter_add(tgt, idx, src, axis=0):
    return tgt.at[idx].add(src)

def _segment_sum(src, seg, n):
    return jax.ops.segment_sum(src, seg, n)
kernel_name = 'mk_xattn_seq_d4_seqx_r8_674bad'

def setup_inputs(seed: int=0):
    np.random.seed(seed)
    _w = jnp.asarray

    def _rec_inputs():
        import jax
        import jax.numpy as jnp
        _rk = jax.random.key(seed)
        x = 7.22e-05 + 1 * jax.random.normal(jax.random.fold_in(_rk, 1), (8, 256, 256), jnp.float32)
        _lenS = 256 - jax.random.randint(jax.random.fold_in(_rk, 7), (8,), 0, max(1, 256 // 4) + 1, jnp.int32)
        _lenS2 = 64 - jax.random.randint(jax.random.fold_in(_rk, 8), (8,), 0, max(1, 64 // 4) + 1, jnp.int32)
        _ctx_2048P = jax.random.normal(jax.random.fold_in(_rk, 11), (8, 16, 256), jnp.float32)
        _ctx_2048c = jax.random.dirichlet(jax.random.fold_in(_rk, 511), 0.3 * jnp.ones((16,), jnp.float32), (8, 64))
        _ctx_2048t = jnp.einsum('bsk,bkd->bsd', _ctx_2048c, _ctx_2048P)
        _ctx_2048t = _ctx_2048t * jax.lax.rsqrt(jnp.mean(jnp.square(_ctx_2048t)) + 1e-12) * 0.953939
        ctx_2048 = 4.13588e-05 + 0.999923 * (_ctx_2048t + 0.3 * jax.random.normal(jax.random.fold_in(_rk, 611), (8, 64, 256), jnp.float32))
        _validS = jnp.arange(256)[None, :] < _lenS[:, None]
        _validS2 = jnp.arange(64)[None, :] < _lenS2[:, None]
        _causal = jnp.tril(jnp.ones((256, 256), dtype=bool))
        mask_Bx1xSxS2_ff0 = jnp.where(jnp.ones((8, 1, 256, 64), dtype=bool), 0.0, -1000000000.0).astype(jnp.float32)
        mask_BxS2_ik0 = jnp.where(jnp.broadcast_to(_validS2[:, :], (8, 64)), 0, 1).astype(jnp.int32)
        return (x, ctx_2048, mask_Bx1xSxS2_ff0, mask_BxS2_ik0)
    x, ctx_2048, mask_Bx1xSxS2_ff0, mask_BxS2_ik0 = _rec_inputs()

    def _L0_xattn_setup():
        import jax, jax.numpy as jnp
        import numpy as np
        H = 256
        NH = 32
        KVH = 8
        HD = H // NH
        GROUPS = NH // KVH
        EPS = 1e-06
        B, L, S = (4, 128, 128)

        def _gqa_forward(hidden_state, encoder_hidden_state, encoder_attention_mask, Wq, bq, Wk, bk, Wv, bv, Wo, bo, gamma, beta):
            b, l, _ = hidden_state.shape
            s = encoder_hidden_state.shape[1]
            q = hidden_state @ Wq + bq
            k = encoder_hidden_state @ Wk + bk
            v = encoder_hidden_state @ Wv + bv
            q = q.reshape(b, l, KVH, GROUPS, HD).transpose(0, 2, 3, 1, 4)
            k = k.reshape(b, s, KVH, HD).transpose(0, 2, 1, 3)
            v = v.reshape(b, s, KVH, HD).transpose(0, 2, 1, 3)
            scale = 1.0 / jnp.sqrt(jnp.asarray(HD, q.dtype))
            scores = jnp.einsum('bkgld,bksd->bkgls', q, k) * scale
            scores = scores + encoder_attention_mask[:, :, None, :, :]
            attn = jax.nn.softmax(scores, axis=-1)
            out = jnp.einsum('bkgls,bksd->bkgld', attn, v)
            out = out.transpose(0, 3, 1, 2, 4).reshape(b, l, H)
            out = out @ Wo + bo
            x = out + hidden_state
            mu = jnp.mean(x, axis=-1, keepdims=True)
            var = jnp.var(x, axis=-1, keepdims=True)
            return (x - mu) * jax.lax.rsqrt(var + EPS) * gamma + beta
        key = jax.random.key(seed)
        ks = jax.random.split(key, 12)
        sd = 0.02
        return {'hidden_state': jax.random.normal(ks[0], (B, L, H), jnp.float32), 'encoder_hidden_state': jax.random.normal(ks[1], (B, S, H), jnp.float32), 'encoder_attention_mask': jnp.zeros((B, 1, L, S), jnp.float32), 'Wq': jax.random.normal(ks[2], (H, H), jnp.float32) * sd, 'bq': jnp.zeros((H,), jnp.float32), 'Wk': jax.random.normal(ks[3], (H, KVH * HD), jnp.float32) * sd, 'bk': jnp.zeros((KVH * HD,), jnp.float32), 'Wv': jax.random.normal(ks[4], (H, KVH * HD), jnp.float32) * sd, 'bv': jnp.zeros((KVH * HD,), jnp.float32), 'Wo': jax.random.normal(ks[5], (H, H), jnp.float32) * sd, 'bo': jnp.zeros((H,), jnp.float32), 'gamma': jnp.ones((H,), jnp.float32), 'beta': jnp.zeros((H,), jnp.float32)}
    _L0_xattn_all = _L0_xattn_setup()
    _L0_xattn_in = {k: v for k, v in _L0_xattn_all.items() if k in ('Wq', 'bq', 'Wk', 'bk', 'Wv', 'bv', 'Wo', 'bo', 'gamma', 'beta')}
    del _L0_xattn_all

    def _L1_xattn_setup():
        import jax, jax.numpy as jnp
        import numpy as np
        B, P, K, H, NH = (4, 256, 32, 256, 16)
        DH = H // NH
        EPS = 1e-06

        def rmsnorm(x, w):
            var = jnp.mean(jnp.square(x), axis=-1, keepdims=True)
            return x * jax.lax.rsqrt(var + EPS) * w
        key = jax.random.key(seed)
        ks = jax.random.split(key, 12)
        s = 0.02
        return {'x': jax.random.normal(ks[0], (B, P, H), jnp.float32), 'latents': jax.random.normal(ks[1], (B, K, H), jnp.float32), 'attention_mask': jax.random.randint(ks[2], (B, P), 0, 2, jnp.int32), 'q_w': s * jax.random.normal(ks[3], (H, H), jnp.float32), 'q_b': jnp.zeros((H,), jnp.float32), 'kv_w': s * jax.random.normal(ks[4], (H, 2 * H), jnp.float32), 'kv_b': jnp.zeros((2 * H,), jnp.float32), 'out_w': s * jax.random.normal(ks[5], (H, H), jnp.float32), 'out_b': jnp.zeros((H,), jnp.float32), 'postnorm_w': jnp.ones((H,), jnp.float32), 'mlp_w1': s * jax.random.normal(ks[6], (H, 4 * H), jnp.float32), 'mlp_b1': jnp.zeros((4 * H,), jnp.float32), 'mlp_w2': s * jax.random.normal(ks[7], (4 * H, H), jnp.float32), 'mlp_b2': jnp.zeros((H,), jnp.float32)}
    _L1_xattn_all = _L1_xattn_setup()
    _L1_xattn_in = {k: v for k, v in _L1_xattn_all.items() if k in ('q_w', 'q_b', 'kv_w', 'kv_b', 'out_w', 'out_b', 'postnorm_w', 'mlp_w1', 'mlp_b1', 'mlp_w2', 'mlp_b2')}
    del _L1_xattn_all

    def _L2_xattn_setup():
        import jax, jax.numpy as jnp
        import numpy as np
        H = 256
        B, L, S = (4, 512, 10)
        key = jax.random.key(seed)
        k1, k2, k3, k4, k5, k6 = jax.random.split(key, 6)
        scale = 1.0 / np.sqrt(H)
        return {'h_english': jax.random.normal(k1, (B, L, H), dtype=jnp.float32), 'h_lojban': jax.random.normal(k2, (B, S, H), dtype=jnp.float32), 'w_q': jax.random.normal(k3, (H, H), dtype=jnp.float32) * scale, 'w_k': jax.random.normal(k4, (H, H), dtype=jnp.float32) * scale, 'w_v': jax.random.normal(k5, (H, H), dtype=jnp.float32) * scale, 'w_o': jax.random.normal(k6, (H, H), dtype=jnp.float32) * scale, 'alpha': jnp.float32(0.1)}
    _L2_xattn_all = _L2_xattn_setup()
    _L2_xattn_in = {k: v for k, v in _L2_xattn_all.items() if k in ('w_q', 'w_k', 'w_v', 'w_o', 'alpha')}
    del _L2_xattn_all

    def _L3_xattn_setup():
        import jax, jax.numpy as jnp
        import numpy as np
        B, Q, S1, S2 = (4, 32, 256, 256)
        D, H, K, F = (256, 16, 128, 1024)
        LN_EPS = 1e-05

        def _layer_norm(x, scale, offset):
            mu = jnp.mean(x, axis=-1, keepdims=True)
            var = jnp.var(x, axis=-1, keepdims=True)
            return (x - mu) * jax.lax.rsqrt(var + LN_EPS) * scale + offset

        def _cross_attention(q_in, kv_in, wq, bq, wk, bk, wv, bv, wo, bo, bias_k, bias_v):
            b, q_len, _ = q_in.shape
            t = kv_in.shape[1]
            qh = (q_in @ wq + bq).reshape(b, q_len, H, K)
            kh = (kv_in @ wk + bk).reshape(b, t, H, K)
            vh = (kv_in @ wv + bv).reshape(b, t, H, K)
            kh = jnp.concatenate([kh, jnp.broadcast_to(bias_k, (b, 1, H, K))], axis=1)
            vh = jnp.concatenate([vh, jnp.broadcast_to(bias_v, (b, 1, H, K))], axis=1)
            scale = jnp.sqrt(jnp.asarray(K, q_in.dtype))
            logits = jnp.einsum('bqhk,bthk->bhqt', qh, kh) / scale
            weights = jax.nn.softmax(logits, axis=-1)
            ctx = jnp.einsum('bhqt,bthk->bqhk', weights, vh).reshape(b, q_len, H * K)
            return ctx @ wo + bo

        def _forward(x, xf_1, xf_2, ln1_scale, ln1_offset, wq1, bq1, wk1, bk1, wv1, bv1, wo1, bo1, bias_k1, bias_v1, ln2_scale, ln2_offset, wq2, bq2, wk2, bk2, wv2, bv2, wo2, bo2, bias_k2, bias_v2, ln_mlp_scale, ln_mlp_offset, w_fc1, b_fc1, w_fc2, b_fc2):
            res = x
            h = _layer_norm(x, ln1_scale, ln1_offset)
            x = res + _cross_attention(h, xf_1, wq1, bq1, wk1, bk1, wv1, bv1, wo1, bo1, bias_k1, bias_v1)
            res = x
            h = _layer_norm(x, ln2_scale, ln2_offset)
            x = res + _cross_attention(h, xf_2, wq2, bq2, wk2, bk2, wv2, bv2, wo2, bo2, bias_k2, bias_v2)
            h = _layer_norm(x, ln_mlp_scale, ln_mlp_offset)
            h = jax.nn.gelu(h @ w_fc1 + b_fc1, approximate=False) @ w_fc2 + b_fc2
            return x + h
        key = jax.random.key(seed)
        ks = iter(jax.random.split(key, 64))

        def rn(shape, s=0.02):
            return jax.random.normal(next(ks), shape, jnp.float32) * s
        inp = {'x': rn((B, Q, D), 1.0), 'xf_1': rn((B, S1, D), 1.0), 'xf_2': rn((B, S2, D), 1.0)}
        for i in (1, 2):
            inp[f'ln{i}_scale'] = jnp.ones((D,), jnp.float32)
            inp[f'ln{i}_offset'] = jnp.zeros((D,), jnp.float32)
            inp[f'wq{i}'] = rn((D, H * K))
            inp[f'bq{i}'] = jnp.zeros((H * K,), jnp.float32)
            inp[f'wk{i}'] = rn((D, H * K))
            inp[f'bk{i}'] = jnp.zeros((H * K,), jnp.float32)
            inp[f'wv{i}'] = rn((D, H * K))
            inp[f'bv{i}'] = jnp.zeros((H * K,), jnp.float32)
            inp[f'wo{i}'] = rn((H * K, D))
            inp[f'bo{i}'] = jnp.zeros((D,), jnp.float32)
            inp[f'bias_k{i}'] = rn((1, 1, H, K))
            inp[f'bias_v{i}'] = rn((1, 1, H, K))
        inp['ln_mlp_scale'] = jnp.ones((D,), jnp.float32)
        inp['ln_mlp_offset'] = jnp.zeros((D,), jnp.float32)
        inp['w_fc1'] = rn((D, F))
        inp['b_fc1'] = jnp.zeros((F,), jnp.float32)
        inp['w_fc2'] = rn((F, D))
        inp['b_fc2'] = jnp.zeros((D,), jnp.float32)
        return inp
    _L3_xattn_all = _L3_xattn_setup()
    _L3_xattn_in = {k: v for k, v in _L3_xattn_all.items() if k in ('ln1_scale', 'ln1_offset', 'wq1', 'bq1', 'wk1', 'bk1', 'wv1', 'bv1', 'wo1', 'bo1', 'bias_k1', 'bias_v1', 'ln2_scale', 'ln2_offset', 'wq2', 'bq2', 'wk2', 'bk2', 'wv2', 'bv2', 'wo2', 'bo2', 'bias_k2', 'bias_v2', 'ln_mlp_scale', 'ln_mlp_offset', 'w_fc1', 'b_fc1', 'w_fc2', 'b_fc2')}
    del _L3_xattn_all
    return {'x': x, 'ctx_2048': ctx_2048, 'mask_Bx1xSxS2_ff0': mask_Bx1xSxS2_ff0, 'mask_BxS2_ik0': mask_BxS2_ik0, 'L0_xattn_Wq': _L0_xattn_in['Wq'], 'L0_xattn_bq': _L0_xattn_in['bq'], 'L0_xattn_Wk': _L0_xattn_in['Wk'], 'L0_xattn_bk': _L0_xattn_in['bk'], 'L0_xattn_Wv': _L0_xattn_in['Wv'], 'L0_xattn_bv': _L0_xattn_in['bv'], 'L0_xattn_Wo': _L0_xattn_in['Wo'], 'L0_xattn_bo': _L0_xattn_in['bo'], 'L0_xattn_gamma': _L0_xattn_in['gamma'], 'L0_xattn_beta': _L0_xattn_in['beta'], 'L1_xattn_q_w': _L1_xattn_in['q_w'], 'L1_xattn_q_b': _L1_xattn_in['q_b'], 'L1_xattn_kv_w': _L1_xattn_in['kv_w'], 'L1_xattn_kv_b': _L1_xattn_in['kv_b'], 'L1_xattn_out_w': _L1_xattn_in['out_w'], 'L1_xattn_out_b': _L1_xattn_in['out_b'], 'L1_xattn_postnorm_w': _L1_xattn_in['postnorm_w'], 'L1_xattn_mlp_w1': _L1_xattn_in['mlp_w1'], 'L1_xattn_mlp_b1': _L1_xattn_in['mlp_b1'], 'L1_xattn_mlp_w2': _L1_xattn_in['mlp_w2'], 'L1_xattn_mlp_b2': _L1_xattn_in['mlp_b2'], 'L2_xattn_w_q': _L2_xattn_in['w_q'], 'L2_xattn_w_k': _L2_xattn_in['w_k'], 'L2_xattn_w_v': _L2_xattn_in['w_v'], 'L2_xattn_w_o': _L2_xattn_in['w_o'], 'L2_xattn_alpha': _L2_xattn_in['alpha'], 'L3_xattn_ln1_scale': _L3_xattn_in['ln1_scale'], 'L3_xattn_ln1_offset': _L3_xattn_in['ln1_offset'], 'L3_xattn_wq1': _L3_xattn_in['wq1'], 'L3_xattn_bq1': _L3_xattn_in['bq1'], 'L3_xattn_wk1': _L3_xattn_in['wk1'], 'L3_xattn_bk1': _L3_xattn_in['bk1'], 'L3_xattn_wv1': _L3_xattn_in['wv1'], 'L3_xattn_bv1': _L3_xattn_in['bv1'], 'L3_xattn_wo1': _L3_xattn_in['wo1'], 'L3_xattn_bo1': _L3_xattn_in['bo1'], 'L3_xattn_bias_k1': _L3_xattn_in['bias_k1'], 'L3_xattn_bias_v1': _L3_xattn_in['bias_v1'], 'L3_xattn_ln2_scale': _L3_xattn_in['ln2_scale'], 'L3_xattn_ln2_offset': _L3_xattn_in['ln2_offset'], 'L3_xattn_wq2': _L3_xattn_in['wq2'], 'L3_xattn_bq2': _L3_xattn_in['bq2'], 'L3_xattn_wk2': _L3_xattn_in['wk2'], 'L3_xattn_bk2': _L3_xattn_in['bk2'], 'L3_xattn_wv2': _L3_xattn_in['wv2'], 'L3_xattn_bv2': _L3_xattn_in['bv2'], 'L3_xattn_wo2': _L3_xattn_in['wo2'], 'L3_xattn_bo2': _L3_xattn_in['bo2'], 'L3_xattn_bias_k2': _L3_xattn_in['bias_k2'], 'L3_xattn_bias_v2': _L3_xattn_in['bias_v2'], 'L3_xattn_ln_mlp_scale': _L3_xattn_in['ln_mlp_scale'], 'L3_xattn_ln_mlp_offset': _L3_xattn_in['ln_mlp_offset'], 'L3_xattn_w_fc1': _L3_xattn_in['w_fc1'], 'L3_xattn_b_fc1': _L3_xattn_in['b_fc1'], 'L3_xattn_w_fc2': _L3_xattn_in['w_fc2'], 'L3_xattn_b_fc2': _L3_xattn_in['b_fc2']}

def reference(x, ctx_2048, mask_Bx1xSxS2_ff0, mask_BxS2_ik0, L0_xattn_Wq, L0_xattn_bq, L0_xattn_Wk, L0_xattn_bk, L0_xattn_Wv, L0_xattn_bv, L0_xattn_Wo, L0_xattn_bo, L0_xattn_gamma, L0_xattn_beta, L1_xattn_q_w, L1_xattn_q_b, L1_xattn_kv_w, L1_xattn_kv_b, L1_xattn_out_w, L1_xattn_out_b, L1_xattn_postnorm_w, L1_xattn_mlp_w1, L1_xattn_mlp_b1, L1_xattn_mlp_w2, L1_xattn_mlp_b2, L2_xattn_w_q, L2_xattn_w_k, L2_xattn_w_v, L2_xattn_w_o, L2_xattn_alpha, L3_xattn_ln1_scale, L3_xattn_ln1_offset, L3_xattn_wq1, L3_xattn_bq1, L3_xattn_wk1, L3_xattn_bk1, L3_xattn_wv1, L3_xattn_bv1, L3_xattn_wo1, L3_xattn_bo1, L3_xattn_bias_k1, L3_xattn_bias_v1, L3_xattn_ln2_scale, L3_xattn_ln2_offset, L3_xattn_wq2, L3_xattn_bq2, L3_xattn_wk2, L3_xattn_bk2, L3_xattn_wv2, L3_xattn_bv2, L3_xattn_wo2, L3_xattn_bo2, L3_xattn_bias_k2, L3_xattn_bias_v2, L3_xattn_ln_mlp_scale, L3_xattn_ln_mlp_offset, L3_xattn_w_fc1, L3_xattn_b_fc1, L3_xattn_w_fc2, L3_xattn_b_fc2):
    import jax
    import jax.numpy as jnp

    def _L0_xattn_ref(hidden_state, encoder_hidden_state, encoder_attention_mask, Wq, bq, Wk, bk, Wv, bv, Wo, bo, gamma, beta):
        import jax, jax.numpy as jnp
        import numpy as np
        H = 256
        NH = 32
        KVH = 8
        HD = H // NH
        GROUPS = NH // KVH
        EPS = 1e-06
        B, L, S = (4, 128, 128)

        def _gqa_forward(hidden_state, encoder_hidden_state, encoder_attention_mask, Wq, bq, Wk, bk, Wv, bv, Wo, bo, gamma, beta):
            b, l, _ = hidden_state.shape
            s = encoder_hidden_state.shape[1]
            q = hidden_state @ Wq + bq
            k = encoder_hidden_state @ Wk + bk
            v = encoder_hidden_state @ Wv + bv
            q = q.reshape(b, l, KVH, GROUPS, HD).transpose(0, 2, 3, 1, 4)
            k = k.reshape(b, s, KVH, HD).transpose(0, 2, 1, 3)
            v = v.reshape(b, s, KVH, HD).transpose(0, 2, 1, 3)
            scale = 1.0 / jnp.sqrt(jnp.asarray(HD, q.dtype))
            scores = jnp.einsum('bkgld,bksd->bkgls', q, k) * scale
            scores = scores + encoder_attention_mask[:, :, None, :, :]
            attn = jax.nn.softmax(scores, axis=-1)
            out = jnp.einsum('bkgls,bksd->bkgld', attn, v)
            out = out.transpose(0, 3, 1, 2, 4).reshape(b, l, H)
            out = out @ Wo + bo
            x = out + hidden_state
            mu = jnp.mean(x, axis=-1, keepdims=True)
            var = jnp.var(x, axis=-1, keepdims=True)
            return (x - mu) * jax.lax.rsqrt(var + EPS) * gamma + beta
        return _gqa_forward(hidden_state, encoder_hidden_state, encoder_attention_mask, Wq, bq, Wk, bk, Wv, bv, Wo, bo, gamma, beta)

    def _L1_xattn_ref(x, latents, attention_mask, q_w, q_b, kv_w, kv_b, out_w, out_b, postnorm_w, mlp_w1, mlp_b1, mlp_w2, mlp_b2):
        import jax, jax.numpy as jnp
        import numpy as np
        B, P, K, H, NH = (4, 256, 32, 256, 16)
        DH = H // NH
        EPS = 1e-06

        def rmsnorm(x, w):
            var = jnp.mean(jnp.square(x), axis=-1, keepdims=True)
            return x * jax.lax.rsqrt(var + EPS) * w
        b, p, _ = x.shape
        k_len = latents.shape[1]
        residual = latents
        h = jnp.concatenate([x, latents], axis=1)
        q = (latents @ q_w + q_b).reshape(b, k_len, NH, DH)
        kv = (h @ kv_w + kv_b).reshape(b, p + k_len, NH, DH, 2)
        kmat, v = (kv[..., 0], kv[..., 1])
        attn = jnp.einsum('bkhd,bnhd->bhkn', q, kmat) / DH
        full_mask = jnp.concatenate([attention_mask.astype(bool), jnp.ones((b, k_len), bool)], axis=-1)
        attn = jnp.where(full_mask[:, None, None, :], attn, -jnp.inf)
        attn = jax.nn.softmax(attn.astype(jnp.float32), axis=-1).astype(q.dtype)
        attn_out = jnp.einsum('bhkn,bnhd->bkhd', attn, v).reshape(b, k_len, H)
        attn_out = attn_out @ out_w + out_b + residual
        out = rmsnorm(attn_out, postnorm_w)
        out = jax.nn.gelu(out @ mlp_w1 + mlp_b1) @ mlp_w2 + mlp_b2
        return out + residual

    def _L2_xattn_ref(h_english, h_lojban, w_q, w_k, w_v, w_o, alpha):
        import jax, jax.numpy as jnp
        import numpy as np
        H = 256
        B, L, S = (4, 512, 10)
        h = h_english.shape[-1]
        q = jnp.einsum('blh,oh->blo', h_english, w_q)
        k = jnp.einsum('bsh,oh->bso', h_lojban, w_k)
        v = jnp.einsum('bsh,oh->bso', h_lojban, w_v)
        scores = jnp.einsum('blh,bsh->bls', q, k) / jnp.sqrt(jnp.float32(h))
        probs = jax.nn.softmax(scores, axis=-1)
        context = jnp.einsum('bls,bsh->blh', probs, v)
        delta = jnp.einsum('blh,oh->blo', context, w_o)
        return h_english + alpha * delta

    def _L3_xattn_ref(x, xf_1, xf_2, ln1_scale, ln1_offset, wq1, bq1, wk1, bk1, wv1, bv1, wo1, bo1, bias_k1, bias_v1, ln2_scale, ln2_offset, wq2, bq2, wk2, bk2, wv2, bv2, wo2, bo2, bias_k2, bias_v2, ln_mlp_scale, ln_mlp_offset, w_fc1, b_fc1, w_fc2, b_fc2):
        import jax, jax.numpy as jnp
        import numpy as np
        B, Q, S1, S2 = (4, 32, 256, 256)
        D, H, K, F = (256, 16, 128, 1024)
        LN_EPS = 1e-05

        def _layer_norm(x, scale, offset):
            mu = jnp.mean(x, axis=-1, keepdims=True)
            var = jnp.var(x, axis=-1, keepdims=True)
            return (x - mu) * jax.lax.rsqrt(var + LN_EPS) * scale + offset

        def _cross_attention(q_in, kv_in, wq, bq, wk, bk, wv, bv, wo, bo, bias_k, bias_v):
            b, q_len, _ = q_in.shape
            t = kv_in.shape[1]
            qh = (q_in @ wq + bq).reshape(b, q_len, H, K)
            kh = (kv_in @ wk + bk).reshape(b, t, H, K)
            vh = (kv_in @ wv + bv).reshape(b, t, H, K)
            kh = jnp.concatenate([kh, jnp.broadcast_to(bias_k, (b, 1, H, K))], axis=1)
            vh = jnp.concatenate([vh, jnp.broadcast_to(bias_v, (b, 1, H, K))], axis=1)
            scale = jnp.sqrt(jnp.asarray(K, q_in.dtype))
            logits = jnp.einsum('bqhk,bthk->bhqt', qh, kh) / scale
            weights = jax.nn.softmax(logits, axis=-1)
            ctx = jnp.einsum('bhqt,bthk->bqhk', weights, vh).reshape(b, q_len, H * K)
            return ctx @ wo + bo

        def _forward(x, xf_1, xf_2, ln1_scale, ln1_offset, wq1, bq1, wk1, bk1, wv1, bv1, wo1, bo1, bias_k1, bias_v1, ln2_scale, ln2_offset, wq2, bq2, wk2, bk2, wv2, bv2, wo2, bo2, bias_k2, bias_v2, ln_mlp_scale, ln_mlp_offset, w_fc1, b_fc1, w_fc2, b_fc2):
            res = x
            h = _layer_norm(x, ln1_scale, ln1_offset)
            x = res + _cross_attention(h, xf_1, wq1, bq1, wk1, bk1, wv1, bv1, wo1, bo1, bias_k1, bias_v1)
            res = x
            h = _layer_norm(x, ln2_scale, ln2_offset)
            x = res + _cross_attention(h, xf_2, wq2, bq2, wk2, bk2, wv2, bv2, wo2, bo2, bias_k2, bias_v2)
            h = _layer_norm(x, ln_mlp_scale, ln_mlp_offset)
            h = jax.nn.gelu(h @ w_fc1 + b_fc1, approximate=False) @ w_fc2 + b_fc2
            return x + h
        return _forward(x, xf_1, xf_2, ln1_scale, ln1_offset, wq1, bq1, wk1, bk1, wv1, bv1, wo1, bo1, bias_k1, bias_v1, ln2_scale, ln2_offset, wq2, bq2, wk2, bk2, wv2, bv2, wo2, bo2, bias_k2, bias_v2, ln_mlp_scale, ln_mlp_offset, w_fc1, b_fc1, w_fc2, b_fc2)
    x = _L0_xattn_ref(x, ctx_2048, mask_Bx1xSxS2_ff0, L0_xattn_Wq, L0_xattn_bq, L0_xattn_Wk, L0_xattn_bk, L0_xattn_Wv, L0_xattn_bv, L0_xattn_Wo, L0_xattn_bo, L0_xattn_gamma, L0_xattn_beta)
    x = _L1_xattn_ref(ctx_2048, x, mask_BxS2_ik0, L1_xattn_q_w, L1_xattn_q_b, L1_xattn_kv_w, L1_xattn_kv_b, L1_xattn_out_w, L1_xattn_out_b, L1_xattn_postnorm_w, L1_xattn_mlp_w1, L1_xattn_mlp_b1, L1_xattn_mlp_w2, L1_xattn_mlp_b2)
    x = _L2_xattn_ref(x, ctx_2048, L2_xattn_w_q, L2_xattn_w_k, L2_xattn_w_v, L2_xattn_w_o, L2_xattn_alpha)
    x = _L3_xattn_ref(x, ctx_2048, ctx_2048, L3_xattn_ln1_scale, L3_xattn_ln1_offset, L3_xattn_wq1, L3_xattn_bq1, L3_xattn_wk1, L3_xattn_bk1, L3_xattn_wv1, L3_xattn_bv1, L3_xattn_wo1, L3_xattn_bo1, L3_xattn_bias_k1, L3_xattn_bias_v1, L3_xattn_ln2_scale, L3_xattn_ln2_offset, L3_xattn_wq2, L3_xattn_bq2, L3_xattn_wk2, L3_xattn_bk2, L3_xattn_wv2, L3_xattn_bv2, L3_xattn_wo2, L3_xattn_bo2, L3_xattn_bias_k2, L3_xattn_bias_v2, L3_xattn_ln_mlp_scale, L3_xattn_ln_mlp_offset, L3_xattn_w_fc1, L3_xattn_b_fc1, L3_xattn_w_fc2, L3_xattn_b_fc2)
    return x

_drawn_inputs = setup_inputs


def setup_inputs(seed=0):
    import zlib

    import numpy as np

    out = dict(_drawn_inputs(seed))
    spreads = {'L0_xattn_bq': (0.0, 0.8),
     'L0_xattn_bk': (0.0, 2.0),
     'L0_xattn_bv': (0.0, 0.1),
     'L0_xattn_bo': (0.0, 0.1),
     'L0_xattn_gamma': (1.0, 0.2),
     'L0_xattn_beta': (0.0, 0.1),
     'L1_xattn_q_b': (0.0, 0.8),
     'L1_xattn_kv_b': (0.0, 0.8),
     'L1_xattn_out_b': (0.0, 0.8),
     'L1_xattn_postnorm_w': (1.0, 0.6),
     'L1_xattn_mlp_b1': (0.0, 0.1),
     'L1_xattn_mlp_b2': (0.0, 0.1),
     'L3_xattn_ln1_scale': (1.0, 0.6),
     'L3_xattn_ln1_offset': (0.0, 0.8),
     'L3_xattn_bq1': (0.0, 0.8),
     'L3_xattn_bk1': (0.0, 2.0),
     'L3_xattn_bv1': (0.0, 0.1),
     'L3_xattn_bo1': (0.0, 0.1),
     'L3_xattn_ln2_scale': (1.0, 0.6),
     'L3_xattn_ln2_offset': (0.0, 0.8),
     'L3_xattn_bq2': (0.0, 0.8),
     'L3_xattn_bk2': (0.0, 2.0),
     'L3_xattn_bv2': (0.0, 0.1),
     'L3_xattn_bo2': (0.0, 0.1),
     'L3_xattn_ln_mlp_scale': (1.0, 0.6),
     'L3_xattn_ln_mlp_offset': (0.0, 0.8),
     'L3_xattn_b_fc1': (0.0, 0.1),
     'L3_xattn_b_fc2': (0.0, 0.1)}
    factors = {'L0_xattn_Wq': 8.0,
     'L0_xattn_Wk': 8.0,
     'L1_xattn_q_w': 8.0,
     'L1_xattn_kv_w': 8.0,
     'L1_xattn_out_w': 8.0,
     'L2_xattn_w_q': 2.735,
     'L2_xattn_w_k': 2.751,
     'L3_xattn_wq1': 8.0,
     'L3_xattn_wk1': 8.0,
     'L3_xattn_bias_k1': 64.0,
     'L3_xattn_bias_v1': 64.0,
     'L3_xattn_wq2': 8.0,
     'L3_xattn_wk2': 8.0,
     'L3_xattn_bias_k2': 64.0,
     'L3_xattn_bias_v2': 64.0}
    for name, (base, spread) in spreads.items():
        noise = np.random.default_rng([zlib.crc32(name.encode()), seed]).standard_normal(out[name].shape)
        drawn = base * np.exp(spread * noise) if base else spread * noise
        out[name] = jnp.asarray(drawn.astype(out[name].dtype))
    for name, factor in factors.items():
        out[name] = (out[name] * factor).astype(out[name].dtype)
    return out
```

```python
from contextlib import ExitStack

import numpy as np

import concourse.bass as bass
from concourse import mybir

F32 = mybir.dt.float32
I32 = mybir.dt.int32
ALU = mybir.AluOpType
ACT = mybir.ActivationFunctionType
X = mybir.AxisListType.X

P = 128
D = 256
KT = D // P
B = 8
S = 256
SC = 64
QT_B = S // P
NQ = B * QT_B
T = B * S
C = B * SC
HALF = P // 2

H0, G0, D0 = 32, 8, 8
SCALE0 = float(1.0 / np.sqrt(np.float32(D0)))
EPS0 = 1e-6
H1, D1 = 16, 16
KEYS1 = S + SC
SCALE1 = 1.0 / D1
EPS1 = 1e-6
MASKED = -3.0e38
F = 1024
FT = F // P
CH = 512
NCH = T // CH
QC = CH // P
SCALE2 = float(1.0 / np.sqrt(np.float32(D)))
H3, D3 = 16, 128
SCALE3 = float(1.0 / np.sqrt(np.float32(D3)))
EPS3 = 1e-5
HP = H3 // 2
KEYS3 = H3 * SC

CONST = dict(ident=(0, P), quarter=(128, 4), parity=(132, 2), half=(134, 2), minus_half=(136, 1))
NCONST = 137
VECS = ["L0_bq", "L0_bk", "L0_bv", "L0_gamma", "L0_beta", "L1_bq", "L1_bk", "L1_bv", "L1_norm",
        "ln1_s", "ln1_o", "ln2_s", "ln2_o", "lnm_s", "lnm_o"]
NVEC = len(VECS) * KT + 2 * FT
ROWS = ["L0_bo", "L0_gamma", "L0_beta", "L1_bo", "L1_b2", "bo1", "bo2", "b_fc2"]
W0 = dict(wq=(0, 512), wk=(512, 512), wo=(1024, 512), wv=(1536, 128))
W1 = dict(wq=(0, 512), wk=(512, 512), wv=(1024, 512), wo=(1536, 512))
W2 = dict(wq=(0, 512), wkT=(512, 512), wvT=(1024, 512), woT=(1536, 512))
BUN = 4 * D + 4 + H3


class Steps:

    def __init__(self, sem, name, steps):
        self.sem, self.steps, self.per, self.k = sem(name), list(steps), len(steps), 0
        assert len(set(self.steps)) == self.per, name

    def now(self, i, step):
        return (i + 1) * self.per + (self.steps.index(step) + 1)

    def prev(self, i, step):
        return i * self.per + (self.steps.index(step) + 1)

    def end(self, iterations):
        return (iterations + 1) * self.per

    def did(self, step):
        assert self.steps[self.k % self.per] == step, (step, self.steps[self.k % self.per])
        self.k += 1
        return 1


def spread(lead, per_unit, extra, tail):
    out = list(lead)
    for u in range(16):
        out += per_unit(u) + extra.get(u, [])
    return out + list(tail)


def build(nc, io, out, stop=99):
    ctx = ExitStack()
    with ctx:
        def sem(name):
            return ctx.enter_context(nc.semaphore(name))

        def sb(name, shape, dt=F32, where=ctx):
            return where.enter_context(nc.sbuf_tensor(name, shape, dt))

        ps = ctx.enter_context(nc.psum_tensor("ps", [P, 8, 512], F32))

        xr = sb("xr", [P, NQ, D])
        cT = sb("cT", [P, KT, C])
        cst = sb("cst", [P, NCONST])
        vec = sb("vec", [P, NVEC])
        row3 = sb("row3", [P, 3, D])
        alpha = sb("alpha", [P, 1])
        ident = cst[:, 0:P]

        def const(name, k=0):
            return cst[:, CONST[name][0] + k:CONST[name][0] + k + 1]

        def pvec(name, kt):
            c = VECS.index(name) * KT + kt
            return vec[:, c:c + 1]

        def fvec(which, ft):
            c = len(VECS) * KT + which * FT + ft
            return vec[:, c:c + 1]

        def prow(name):
            k = ROWS.index(name)
            return row1[:, k, :] if k < len(ROWS) - 3 else row3[:, k - (len(ROWS) - 3), :]

        def wt(tile, cols, name):
            a, n = cols[name]
            return tile[:, a:a + n].rearrange("p (k n) -> p k n", k=KT)

        upto2 = ExitStack()
        w2 = sb("w2", [P, 2048], where=upto2)
        row1 = sb("row1", [P, len(ROWS) - 3, D], where=upto2)
        early = ExitStack()
        xT = sb("xT", [P, KT, T], where=early)
        nT = sb("nT", [P, KT, T], where=early)
        attn01 = ExitStack()
        w0 = sb("w0", [P, 1664], where=attn01)
        w1 = sb("w1", [P, 2048], where=attn01)
        kbd = sb("kbd", [P, KT, B, 4 * SC], where=attn01)
        vbd = sb("vbd", [P, B * G0, 2, D0 + 1], where=attn01)
        vc1 = sb("vc1", [P, B, H1, D1 + 1], where=attn01)
        mask0 = sb("mask0", [P, NQ, SC], where=attn01)
        maski = sb("maski", [P, B * SC], I32, where=attn01)
        mask1 = sb("mask1", [P, B * SC], where=attn01)
        ones = sb("ones", [P, P], where=attn01)

        l0 = ExitStack()
        q0 = sb("q0", [P, KT, S], where=l0)
        kb0 = sb("kb0", [P, KT, 4 * SC], where=l0)
        p0 = [sb(f"p0_{t}", [P, 2048], where=l0) for t in range(2)]
        pt0 = [sb(f"pt0_{t}", [P, 512], where=l0) for t in range(2)]
        mx0 = [sb(f"mx0_{t}", [P, H0], where=l0) for t in range(2)]
        ri0 = sb("ri0", [P, H0], where=l0)
        ao0 = sb("ao0", [P, D], where=l0)
        aoT0 = sb("aoT0", [P, KT, P], where=l0)
        xb0 = [sb(f"xb0_{t}", [P, D], where=l0) for t in range(2)]
        y0 = sb("y0", [P, D], where=l0)
        st0 = sb("st0", [P, 6], where=l0)
        mv0 = [sb(f"mv0_{t}", [P, 4], where=l0) for t in range(2)]
        xn0 = [sb(f"xn0_{t}", [P, D], where=l0) for t in range(2)]
        xg0 = sb("xg0", [P, D], where=l0)
        l0.close()

        l1 = ExitStack()
        xb1T = sb("xb1T", [P, KT, S], where=l1)
        q1 = sb("q1", [P, KT, S], where=l1)
        vb1 = sb("vb1", [P, H1, D1 + 1], where=l1)
        k1 = sb("k1", [P, KT, 2, SC + KEYS1], where=l1)
        v1 = sb("v1", [P, QT_B, H1, D1 + 1], where=l1)
        nm1 = sb("nm1", [P, 16, 2], where=l1)
        p1 = [sb(f"p1_{t}", [P, 2 * KEYS1], where=l1) for t in range(2)]
        pt1 = [sb(f"pt1_{t}", [P, 4, P], where=l1) for t in range(2)]
        pc1 = [sb(f"pc1_{t}", [P, P], where=l1) for t in range(2)]
        ri1 = sb("ri1", [P, H1], where=l1)
        ao1 = sb("ao1", [P, D], where=l1)
        aoT1 = sb("aoT1", [P, KT, P], where=l1)
        xb1 = [sb(f"xb1_{t}", [P, D], where=l1) for t in range(2)]
        y1 = [sb(f"y1_{t}", [P, D], where=l1) for t in range(2)]
        sq1 = sb("sq1", [P, D], where=l1)
        ms1 = [sb(f"ms1_{t}", [P, 4], where=l1) for t in range(2)]
        n1 = sb("n1", [P, D], where=l1)
        l1.close()
        attn01.close()

        mlp1 = ExitStack()
        m1 = dict(wa=sb("m1a", [P, KT, F], where=mlp1), wb=sb("m1b", [P, FT, D], where=mlp1),
                  h=sb("hid1", [P, FT, CH], where=mlp1), xb=[sb(f"xbm1_{t}", [P, D], where=mlp1) for t in range(2)])
        mlp1.close()
        early.close()

        l2 = ExitStack()
        k2 = sb("k2", [P, KT, B, SC], where=l2)
        v2 = sb("v2", [SC, B, D], where=l2)
        t2 = sb("t2", [P, 2, KT, C], where=l2)
        x2 = [sb(f"x2_{t}", [P, D], where=l2) for t in range(2)]
        x2T = [sb(f"x2T{t}", [P, KT, P], where=l2) for t in range(2)]
        p2 = [sb(f"p2_{t}", [P, SC], where=l2) for t in range(2)]
        pT2 = [sb(f"pT2_{t}", [SC, P], where=l2) for t in range(2)]
        sm2 = [sb(f"sm2_{t}", [P, 4], where=l2) for t in range(2)]
        l2.close()
        upto2.close()

        late = ExitStack()
        g3 = sb("g3", [P, KT, B, KEYS3], where=late)
        v3 = sb("v3", [P, B, HP, D], where=late)
        gb3 = sb("gb3", [P, KT, H3], where=late)
        vb3 = sb("vb3", [H3, D], where=late)
        bt3 = sb("bt3", [1, B, KEYS3], where=late)
        bb3 = sb("bb3", [1, H3], where=late)
        one3 = sb("one3", [1, P], where=late)
        prep = ExitStack()
        bun = [sb(f"bun{t}", [P, BUN], where=prep) for t in range(2)]
        kh = sb("kh", [P, C], where=prep)
        vh = sb("vh", [P, C], where=prep)
        prep.close()
        at3 = ExitStack()
        hn = [sb(f"hn{t}", [P, D], where=at3) for t in range(2)]
        hT = [sb(f"hT_{t}", [P, KT, P], where=at3) for t in range(2)]
        st3 = sb("st3", [P, 6], where=at3)
        mv3 = [sb(f"mv3_{t}", [P, 4], where=at3) for t in range(2)]
        mx3 = [sb(f"mx3_{t}", [P, H3], where=at3) for t in range(2)]
        sm3 = [sb(f"sm3_{t}", [P, H3], where=at3) for t in range(2)]
        p3 = [sb(f"p3_{t}", [P, KEYS3 + H3], where=at3) for t in range(2)]
        pT3 = [sb(f"pT3_{t}", [P, 4, P], where=at3) for t in range(2)]
        pb3 = sb("pb3", [H3, P], where=at3)
        xb3 = [sb(f"xb3_{t}", [P, D], where=at3) for t in range(2)]
        at3.close()
        late.close()

        fin = ExitStack()
        m3 = dict(wa=sb("m3a", [P, KT, F], where=fin), wb=sb("m3b", [P, FT, D], where=fin),
                  h=sb("hid3", [P, FT, CH], where=fin), xb=[sb(f"xbm3_{t}", [P, D], where=fin) for t in range(2)])
        xc3 = sb("xc3", [P, KT, CH], where=fin)
        hnm = [sb(f"hnm{t}", [P, D], where=fin) for t in range(2)]
        stm = sb("stm", [P, 6], where=fin)
        mvm = [sb(f"mvm{t}", [P, 4], where=fin) for t in range(2)]
        fin.close()

        dma_x, dma_xT, dma_c, dma_w0, dma_w1, dma_w2, dma_m, dma_k, dma_m1, dma_m3 = [
            sem(f"loaded_{n}") for n in ("x", "xT", "ctx", "w0", "w1", "w2", "masks", "consts", "mlp1", "mlp3")]
        dma_bun = [[sem(f"loaded_heads{a}_{t}") for t in range(2)] for a in range(2)]
        dma_out = sem("stored_out")

        ppe = Steps(sem, "prep_pe", ["k0", "v0", "v1"])
        pdv = Steps(sem, "prep_dve", ["ones", "k0", "v0", "v1", "m1"])
        ppo = Steps(sem, "prep_pool", ["ones"])

        e0 = Steps(sem, "l0_pe", ["q", "s0", "s1", "t00", "t01", "v00", "t02", "v01", "t03", "v02", "v03", "t10", "t11",
                                  "aot0", "v10", "t12", "v11", "out0", "t13", "v12", "v13", "xt0", "aot1", "out1", "xt1"])
        tails0 = [["inv%d", "ao%d", "y%d", "bn%d", "mv%d", "eps%d", "xn%d"]] * 2
        d0 = Steps(sem, "l0_dve", ["q", "mask0", "max0", "mask1", "max1"] + [n % t for t in range(2) for n in tails0[t]])
        a0 = Steps(sem, "l0_act", ["exp0", "c00", "c01", "c02", "c03", "exp1", "c10", "c11", "aot0", "c12", "c13",
                                   "xt0", "aot1", "xt1"])
        g0 = Steps(sem, "l0_pool", ["kb", "xb0", "xb1", "sh0", "sh1", "rs0", "xg0", "xr0", "rs1", "xg1", "xr1"])

        e1 = Steps(sem, "l1_pe", spread(
            ["q", "k", "v", "s0"],
            lambda u: ([f"s{u + 1}"] if u < 15 else []) + [f"t{u}"] + ([f"a{u - 1}"] if u else []),
            {9: ["aot0"], 10: ["out0"], 13: ["nt0"]}, ["a15", "aot1", "out1", "nt1"]))
        d1 = Steps(sem, "l1_dve", spread(
            ["q", "k", "mk0", "mx0", "mk1", "mx1"],
            lambda u: [f"pt{u}"] + ([f"mk{u + 2}", f"mx{u + 2}"] if u < 14 else []),
            {8: ["inv0", "ao0"], 10: ["y0", "sq0", "eps0"], 12: ["n0"]}, ["inv1", "ao1", "y1", "sq1", "eps1", "n1"]))
        a1 = Steps(sem, "l1_act", spread(
            ["v", "e0"],
            lambda u: ([f"e{u + 1}"] if u < 15 else []) + [f"c{u}"],
            {9: ["aot0"], 13: ["nt0"]}, ["aot1", "nt1"]))
        g1 = Steps(sem, "l1_pool", ["xT", "vb", "xb0", "xb1", "rs0", "rs1"])

        hs, os_ = [f"h{f}" for f in range(FT)], [f"o{t}" for t in range(QC)]
        em = [Steps(sem, "mlp1_pe", hs + os_), Steps(sem, "mlp3_pe", [f"x{t}" for t in range(QC)] + hs + os_)]
        am = [Steps(sem, "mlp1_act", hs), Steps(sem, "mlp3_act", [f"x{t}" for t in range(QC)] + hs)]
        ln4 = [n % t for t in range(QC) for n in ("bn%d", "mv%d", "eps%d", "xn%d")]
        dm = [Steps(sem, "mlp1_dve", os_), Steps(sem, "mlp3_dve", ln4 + os_)]
        gm = [Steps(sem, "mlp1_pool", [f"xb{t}" for t in range(QC)]),
              Steps(sem, "mlp3_pool", [f"rs{t}" for t in range(QC)] + [f"xb{t}" for t in range(QC)])]

        pe2p = Steps(sem, "l2_prep_pe", ["k", "kq", "v", "vo"])
        dv2p = Steps(sem, "l2_prep_dve", ["k", "kq", "v", "vo"])
        two = lambda *names: [n % t for n in names for t in range(2)]
        e2 = Steps(sem, "l2_pe", two("xt%d", "s%d", "pt%d", "o%d"))
        a2 = Steps(sem, "l2_act", two("xt%d", "exp%d", "pt%d"))
        d2 = Steps(sem, "l2_dve", [n % t for t in range(2) for n in ("m%d", "max%d")]
                   + [n % t for t in range(2) for n in ("s%d", "sum%d")] + two("y%d"))
        vbz = [sem(f"bias_values_zero{a}") for a in range(2)]
        g2 = Steps(sem, "l2_pool", two("x%d"))

        ep = [Steps(sem, f"heads{a}_pe", [n % t for t in range(2) for n in ("k%d", "g%d", "b%d", "v%d", "w%d", "r%d")])
              for a in range(2)]
        dp = [Steps(sem, f"heads{a}_dve", [n % t for t in range(2) for n in ("k%d", "w%d", "m%d", "vb%d")])
              for a in range(2)]
        ap_ = [Steps(sem, f"heads{a}_act", [n % t for t in range(2) for n in ("g%d", "b%d", "v%d", "w%d")])
               for a in range(2)]

        e3 = [Steps(sem, f"attn{a}_pe", two("h%d") + ["sb"] + two("s%d")
                    + [n % t for t in range(2) for n in ("ta%d", "tb%d", "tc%d", "o%d")])
              for a in range(2)]
        d3 = [Steps(sem, f"attn{a}_dve", [n % t for t in range(2) for n in ("bn%d", "mv%d", "eps%d", "hn%d")]
                    + [n % t for t in range(2) for n in ("mx%d", "mb%d", "sub%d", "subb%d")]
                    + [n % t for t in range(2) for n in ("sum%d", "sumb%d", "inv%d", "nb%d")] + two("y%d")) for a in range(2)]
        a3 = [Steps(sem, f"attn{a}_act", two("h%d", "exp%d") + [n % t for t in range(2) for n in ("ca%d", "cb%d", "cc%d")])
              for a in range(2)]
        g3s = [Steps(sem, f"attn{a}_pool", two("rs%d", "xb%d", "nrm%d")) for a in range(2)]

        def settle(eng):
            eng.nop(nofuse=True)

        x_rows = io["x"].rearrange("b (t p) d -> p (b t) d", p=P)
        out_rows = out.rearrange("b (t p) d -> p (b t) d", p=P)

        block = ctx.enter_context(nc.Block())

        def unit1(u):
            v = u % 8
            return u // 8, v // 4, (v // 2) % 2, v % 2

        def head1(u, e):
            _, kt, par, jp = unit1(u)
            return 8 * kt + 2 * (2 * jp + e) + par

        @block.sync
        def _(sp):
            sp.dma_start(cT[:, :, :], io["ctxT"]).then_inc(dma_c, 16)
            sp.dma_start(w0[:, :], io["w0"]).then_inc(dma_w0, 16)
            sp.dma_start(cst[:, :], io["const"]).then_inc(dma_k, 16)
            sp.dma_start(vec[:, :], io["vecs"]).then_inc(dma_k, 16)
            sp.dma_start(alpha[:, :], io["alpha"].partition_broadcast(P)).then_inc(dma_k, 16)
            sp.dma_start(xT[:, :, :], io["xT"]).then_inc(dma_xT, 16)
            sp.dma_start(row1[:, :, :], io["rows"][0:len(ROWS) - 3, :].partition_broadcast(P)).then_inc(dma_k, 16)
            sp.dma_start(row3[:, :, :], io["rows"][len(ROWS) - 3:, :].partition_broadcast(P)).then_inc(dma_k, 16)
            sp.dma_start(xr[:, :, :], x_rows).then_inc(dma_x, 16)
            sp.dma_start(mask0[:, :, :], io["mask0"].rearrange("b o (t p) k -> p (b o t) k", p=P)).then_inc(dma_m, 16)
            sp.dma_start(maski[:, :], io["mask1"].partition_broadcast(P)).then_inc(dma_m, 16)
            sp.dma_start(w1[:, :], io["w1"]).then_inc(dma_w1, 16)
            sp.dma_start(w2[:, :], io["w2"]).then_inc(dma_w2, 16)
            if stop >= 2:
                sp.wait_ge(e1.sem, e1.end(B))
                sp.wait_ge(a1.sem, a1.end(B))
                sp.dma_start(m1["wa"][:, :, :], io["m1a"]).then_inc(dma_m1, 16)
                sp.dma_start(m1["wb"][:, :, :], io["m1b"]).then_inc(dma_m1, 16)
            for a in range(2):
                if stop >= 4 + 2 * a:
                    if a == 0:
                        sp.wait_ge(d2.sem, d2.end(B))
                        sp.wait_ge(e2.sem, e2.end(B))
                    else:
                        sp.wait_ge(d3[0].sem, d3[0].end(B))
                    with sp.Fori(0, HP) as i:
                        for t in range(2):
                            sp.wait_ge(ep[a].sem, ep[a].prev(i, f"r{t}"))
                            settle(sp)
                            sp.wait_ge(ap_[a].sem, ap_[a].prev(i, f"v{t}"))
                            settle(sp)
                            sp.dma_start(bun[t][:, :], io[f"heads{a}"][bass.ds(2 * i + t, 1), :, :].rearrange(
                                "o p n -> p (o n)")).then_inc(dma_bun[a][t], 16)
            if stop >= 8:
                sp.wait_ge(d3[1].sem, d3[1].end(B))
                sp.dma_start(m3["wa"][:, :, :], io["m3a"]).then_inc(dma_m3, 16)
                sp.dma_start(m3["wb"][:, :, :], io["m3b"]).then_inc(dma_m3, 16)
            last = [(g0, B), (d1, B), (dm[0], NCH), (d2, B), (d2, B), (d3[0], B), (d3[0], B), (d3[1], B), (dm[1], NCH)][min(stop, 8)]
            sp.wait_ge(last[0].sem, last[0].end(last[1]))
            sp.dma_start(out_rows, xr[:, :, :]).then_inc(dma_out, 16)
            sp.wait_ge(dma_out, 16)

        @block.tensor
        def _(pe):
            mm, tr = nc.tensor.matmul, nc.tensor.transpose
            for s in [ppe, e0, e1, pe2p, e2] + em + ep + e3:
                pe.sem_inc(s.sem, s.per)

            pe.wait_ge(dma_c, 16)
            pe.wait_ge(dma_w0, 16)
            for mt in range(KT):
                for kt in range(KT):
                    last = mm(ps[:, mt, :], wt(w0, W0, "wk")[:, kt, mt * P:(mt + 1) * P], cT[:, kt, :],
                              start=kt == 0, stop=kt == KT - 1)
            last.then_inc(ppe.sem, ppe.did("k0"))
            for b in range(B):
                for hf in range(2):
                    for kt in range(KT):
                        last = mm(ps[HALF * hf:HALF * (hf + 1), 2, b * SC:(b + 1) * SC],
                                  cT[:, kt, b * SC:(b + 1) * SC], wt(w0, W0, "wv")[:, kt, :],
                                  start=kt == 0, stop=kt == KT - 1)
            last.then_inc(ppe.sem, ppe.did("v0"))
            pe.wait_ge(dma_w1, 16)
            for b in range(B):
                for hf in range(2):
                    for kt in range(KT):
                        last = mm(ps[HALF * hf:HALF * (hf + 1), 3 + b // 2, (b % 2) * D:(b % 2 + 1) * D],
                                  cT[:, kt, b * SC:(b + 1) * SC], wt(w1, W1, "wv")[:, kt, :],
                                  start=kt == 0, stop=kt == KT - 1)
            last.then_inc(ppe.sem, ppe.did("v1"))
            pe.wait_ge(pdv.sem, pdv.now(0, "v1"))
            pe.wait_ge(dma_k, 80)
            pe.wait_ge(dma_xT, 16)

            with pe.Fori(0, B) as i:
                pe.wait_ge(d0.sem, d0.prev(i, "y1"))
                for mt in range(KT):
                    for kt in range(KT):
                        last = mm(ps[:, 7, mt * S:(mt + 1) * S], wt(w0, W0, "wq")[:, kt, mt * P:(mt + 1) * P],
                                  xT[:, kt, bass.ds(i * S, S)], start=kt == 0, stop=kt == KT - 1)
                last.then_inc(e0.sem, e0.did("q"))
                pe.wait_ge(d0.sem, d0.now(i, "q"))
                pe.wait_ge(g0.sem, g0.now(i, "kb"))
                for t in range(2):
                    pe.wait_ge(d0.sem, d0.now(i, "mask0") if t else d0.prev(i, "mask1"))
                    for kt in range(KT):
                        for j in range(4):
                            last = mm(ps[:, j, kt * 256:(kt + 1) * 256], q0[32 * j:32 * j + 32, kt, t * P:(t + 1) * P],
                                      kb0[32 * j:32 * j + 32, kt, :], start=True, stop=True)
                    last.then_inc(e0.sem, e0.did(f"s{t}"))

                def turn(t, c, bank, freed):
                    if c == 0:
                        pe.wait_ge(a0.sem, a0.now(i, f"exp{t}"))
                    pe.wait_ge(a0.sem, freed)
                    for k in range(4):
                        blk = 4 * c + k
                        last = tr(ps[:, bank, k * P:(k + 1) * P], p0[t][:, blk * P:(blk + 1) * P], ident)
                    last.then_inc(e0.sem, e0.did(f"t{t}{c}"))

                def av(t, c):
                    if c == 0:
                        pe.wait_ge(d0.sem, d0.now(i, "ao0") if t else d0.prev(i, "ao1"))
                    pe.wait_ge(a0.sem, a0.now(i, f"c{t}{c}"))
                    for k in range(4):
                        blk = 4 * c + k
                        g = 4 * ((blk // 2) % 2) + blk // 4
                        last = mm(ps[:, 6, blk * 18:blk * 18 + 18], pt0[c % 2][:, k * P:(k + 1) * P],
                                  vbd[:, bass.ds(i * G0 + g, 1), :, :], start=True, stop=True)
                    last.then_inc(e0.sem, e0.did(f"v{t}{c}"))

                def turn_out(t, freed):
                    pe.wait_ge(d0.sem, d0.now(i, f"ao{t}"))
                    pe.wait_ge(a0.sem, freed)
                    for kt in range(KT):
                        last = tr(ps[:, 4, kt * P:(kt + 1) * P], ao0[:, kt * P:(kt + 1) * P], ident)
                    last.then_inc(e0.sem, e0.did(f"aot{t}"))

                def project(t):
                    pe.wait_ge(a0.sem, a0.now(i, f"aot{t}"))
                    if t:
                        pe.wait_ge(d0.sem, d0.now(i, "y0"))
                    for kt in range(KT):
                        last = mm(ps[:, 7, 0:D], aoT0[:, kt, :], wt(w0, W0, "wo")[:, kt, :], start=kt == 0, stop=kt == KT - 1)
                    last.then_inc(e0.sem, e0.did(f"out{t}"))

                def turn_x(t, freed):
                    pe.wait_ge(d0.sem, d0.now(i, f"xn{t}"))
                    pe.wait_ge(a0.sem, freed)
                    for kt in range(KT):
                        last = tr(ps[:, 5, kt * P:(kt + 1) * P], xn0[t][:, kt * P:(kt + 1) * P], ident)
                    last.then_inc(e0.sem, e0.did(f"xt{t}"))

                turn(0, 0, 4, a0.prev(i, "aot1"))
                turn(0, 1, 5, a0.prev(i, "xt1"))
                av(0, 0)
                turn(0, 2, 4, a0.now(i, "c00"))
                av(0, 1)
                turn(0, 3, 5, a0.now(i, "c01"))
                av(0, 2)
                av(0, 3)
                turn(1, 0, 4, a0.now(i, "c02"))
                turn(1, 1, 5, a0.now(i, "c03"))
                turn_out(0, a0.now(i, "c10"))
                av(1, 0)
                turn(1, 2, 5, a0.now(i, "c11"))
                av(1, 1)
                project(0)
                turn(1, 3, 4, a0.now(i, "aot0"))
                av(1, 2)
                av(1, 3)
                turn_x(0, a0.now(i, "c12"))
                turn_out(1, a0.now(i, "c13"))
                project(1)
                turn_x(1, a0.now(i, "xt0"))

            if stop >= 1:
                pe.wait_ge(a0.sem, a0.end(B))
                pe.wait_ge(d0.sem, d0.end(B))
                with pe.Fori(0, B) as i:
                    pe.wait_ge(g1.sem, g1.now(i, "xT"))
                    pe.wait_ge(d1.sem, d1.prev(i, "pt14"))
                    for mt in range(KT):
                        for kt in range(KT):
                            last = mm(ps[:, 4, mt * S:(mt + 1) * S], wt(w1, W1, "wq")[:, kt, mt * P:(mt + 1) * P],
                                      xb1T[:, kt, :], start=kt == 0, stop=kt == KT - 1)
                    last.then_inc(e1.sem, e1.did("q"))
                    pe.wait_ge(a1.sem, a1.prev(i, "e14"))
                    for mt in range(KT):
                        lhs = wt(w1, W1, "wk")
                        for lo, hi, rhs in ((0, SC, None), (SC, SC + S, xb1T), (SC + S, SC + S + SC, None)):
                            for kt in range(KT):
                                r = rhs[:, kt, :] if rhs is not None else cT[:, kt, bass.ds(i * SC, SC)]
                                last = mm(ps[:, mt, lo:hi], lhs[:, kt, mt * P:(mt + 1) * P], r,
                                          start=kt == 0, stop=kt == KT - 1)
                    last.then_inc(e1.sem, e1.did("k"))
                    pe.wait_ge(d1.sem, d1.prev(i, "pt15"))
                    for t in range(QT_B):
                        for kt in range(KT):
                            last = mm(ps[:, 5, t * D:(t + 1) * D], xb1T[:, kt, t * P:(t + 1) * P],
                                      wt(w1, W1, "wv")[:, kt, :], start=kt == 0, stop=kt == KT - 1)
                    last.then_inc(e1.sem, e1.did("v"))

                    bank6 = [(a1, a1.prev(i, "nt1"))]

                    def take_bank6(reader, count):
                        s, n = bank6.pop()
                        pe.wait_ge(s.sem, n)
                        bank6.append((reader, count))

                    def scores(u):
                        t, kt, par, jp = unit1(u)
                        if u == 0:
                            pe.wait_ge(d1.sem, d1.now(i, "k"))
                        elif u == 1:
                            pe.wait_ge(a1.sem, a1.prev(i, "e15"))
                        else:
                            pe.wait_ge(a1.sem, a1.now(i, f"e{u - 2}"))
                        for e in range(2):
                            r = 32 * (2 * jp + e)
                            first = 0 if e else SC
                            last = mm(ps[:, 2 * (u % 2) + e, 0:KEYS1], q1[r:r + 32, kt, t * P:(t + 1) * P],
                                      k1[r:r + 32, kt, par, first:first + KEYS1], start=True, stop=True)
                        last.then_inc(e1.sem, e1.did(f"s{u}"))

                    def turn(u):
                        pe.wait_ge(a1.sem, a1.now(i, f"e{u}"))
                        if u < 2:
                            pe.wait_ge(d1.sem, d1.now(i, "q") if u == 0 else d1.prev(i, "pt15"))
                            if u == 1:
                                pe.wait_ge(a1.sem, a1.now(i, "v"))
                        else:
                            pe.wait_ge(d1.sem, d1.now(i, f"pt{u - 2}"))
                        for k, blk in enumerate((0, 1, 3, 4)):
                            tr(ps[:, 4 + u % 2, k * P:(k + 1) * P], p1[u % 2][:, blk * P:(blk + 1) * P], ident)
                        take_bank6(a1, a1.now(i, f"c{u}"))
                        tr(ps[:, 6, 0:P], p1[u % 2][:, 2 * P:3 * P],
                           ident).then_inc(e1.sem, e1.did(f"t{u}"))

                    def av(u):
                        if u == 0:
                            pe.wait_ge(d1.sem, d1.prev(i, "ao1"))
                            pe.wait_ge(g1.sem, g1.now(i, "vb"))
                        if u == 8:
                            pe.wait_ge(d1.sem, d1.now(i, "ao0"))
                        pe.wait_ge(d1.sem, d1.now(i, f"pt{u}"))
                        pe.wait_ge(a1.sem, a1.now(i, f"c{u}"))
                        for e in range(2):
                            h = head1(u, e)
                            o = ps[:, 7, h * (D1 + 1):(h + 1) * (D1 + 1)]
                            for c in range(2):
                                mm(o, pt1[u % 2][:, 2 * e + c, :], v1[:, c, h, :], start=c == 0, stop=False)
                            last = mm(o, pc1[u % 2][:, :], vb1[:, h, :], start=False, stop=True)
                        last.then_inc(e1.sem, e1.did(f"a{u}"))

                    def turn_out(t):
                        pe.wait_ge(d1.sem, d1.now(i, f"ao{t}"))
                        take_bank6(a1, a1.now(i, f"aot{t}"))
                        for kt in range(KT):
                            last = tr(ps[:, 6, 256 + kt * P:256 + (kt + 1) * P], ao1[:, kt * P:(kt + 1) * P], ident)
                        last.then_inc(e1.sem, e1.did(f"aot{t}"))

                    def project(t):
                        pe.wait_ge(a1.sem, a1.now(i, f"aot{t}"))
                        take_bank6(d1, d1.now(i, f"y{t}"))
                        for kt in range(KT):
                            last = mm(ps[:, 6, 256:512], aoT1[:, kt, :], wt(w1, W1, "wo")[:, kt, :],
                                      start=kt == 0, stop=kt == KT - 1)
                        last.then_inc(e1.sem, e1.did(f"out{t}"))

                    def turn_n(t):
                        pe.wait_ge(d1.sem, d1.now(i, f"n{t}"))
                        take_bank6(a1, a1.now(i, f"nt{t}"))
                        for kt in range(KT):
                            last = tr(ps[:, 6, 256 + kt * P:256 + (kt + 1) * P], n1[:, kt * P:(kt + 1) * P], ident)
                        last.then_inc(e1.sem, e1.did(f"nt{t}"))

                    scores(0)
                    for u in range(16):
                        if u < 15:
                            scores(u + 1)
                        turn(u)
                        if u:
                            av(u - 1)
                        if u == 9:
                            turn_out(0)
                        if u == 10:
                            project(0)
                        if u == 13:
                            turn_n(0)
                    av(15)
                    turn_out(1)
                    project(1)
                    turn_n(1)

            def mlp_products(m, w, loaded, cols):
                pe.wait_ge(loaded, 32)
                with pe.Fori(0, NCH) as i:
                    if m:
                        for t in range(QC):
                            pe.wait_ge(dm[1].sem, dm[1].now(i, f"xn{t}"))
                            pe.wait_ge(am[1].sem, am[1].now(i, f"x{t - 2}") if t >= 2 else am[1].prev(i, f"x{t + 2}"))
                            for kt in range(KT):
                                last = tr(ps[:, 4 + t % 2, kt * P:(kt + 1) * P], hnm[t % 2][:, kt * P:(kt + 1) * P], ident)
                            last.then_inc(em[1].sem, em[1].did(f"x{t}"))
                        pe.wait_ge(am[1].sem, am[1].now(i, f"x{QC - 1}"))
                    for ft in range(FT):
                        pe.wait_ge(am[m].sem, am[m].now(i, f"h{ft - 2}") if ft >= 2 else am[m].prev(i, f"h{ft + 6}"))
                        for kt in range(KT):
                            last = mm(ps[:, ft % 2, :], w["wa"][:, kt, ft * P:(ft + 1) * P], cols(i, kt),
                                      start=kt == 0, stop=kt == KT - 1)
                        last.then_inc(em[m].sem, em[m].did(f"h{ft}"))
                    for t in range(QC):
                        pe.wait_ge(am[m].sem, am[m].now(i, f"h{FT - 1}"))
                        pe.wait_ge(dm[m].sem, dm[m].now(i, f"o{t - 2}") if t >= 2 else dm[m].prev(i, f"o{t + 2}"))
                        for ft in range(FT):
                            last = mm(ps[:, 2 + t % 2, 0:D], w["h"][:, ft, t * P:(t + 1) * P], w["wb"][:, ft, :],
                                      start=ft == 0, stop=ft == FT - 1)
                        last.then_inc(em[m].sem, em[m].did(f"o{t}"))

            if stop >= 2:
                pe.wait_ge(a1.sem, a1.end(B))
                pe.wait_ge(d1.sem, d1.end(B))
                mlp_products(0, m1, dma_m1, lambda i, kt: nT[:, kt, bass.ds(i * CH, CH)])

            if stop >= 3:
                pe.wait_ge(dma_w2, 16)
                pe.wait_ge(dm[0].sem, dm[0].end(NCH))
                pe.wait_ge(am[0].sem, am[0].end(NCH))
                for k, name in ((0, "wkT"), (1, "wvT")):
                    for mt in range(KT):
                        for kt in range(KT):
                            last = mm(ps[:, 2 * k + mt, :], wt(w2, W2, name)[:, kt, mt * P:(mt + 1) * P], cT[:, kt, :],
                                      start=kt == 0, stop=kt == KT - 1)
                    if k == 0:
                        last.then_inc(pe2p.sem, pe2p.did("k"))
                        pe.wait_ge(dv2p.sem, dv2p.now(0, "k"))
                        for mt in range(KT):
                            for kt in range(KT):
                                last = mm(ps[:, 4 + mt, :], wt(w2, W2, "wq")[:, kt, mt * P:(mt + 1) * P], t2[:, 0, kt, :],
                                          start=kt == 0, stop=kt == KT - 1)
                        last.then_inc(pe2p.sem, pe2p.did("kq"))
                last.then_inc(pe2p.sem, pe2p.did("v"))
                pe.wait_ge(dv2p.sem, dv2p.now(0, "v"))
                for b in range(B):
                    for kt in range(KT):
                        last = mm(ps[0:SC, 4 + b // 2, (b % 2) * D:(b % 2 + 1) * D], t2[:, 1, kt, b * SC:(b + 1) * SC],
                                  wt(w2, W2, "woT")[:, kt, :], start=kt == 0, stop=kt == KT - 1)
                last.then_inc(pe2p.sem, pe2p.did("vo"))
                pe.wait_ge(dv2p.sem, dv2p.now(0, "vo"))
                with pe.Fori(0, B) as i:
                    for t in range(2):
                        pe.wait_ge(g2.sem, g2.now(i, f"x{t}"))
                        pe.wait_ge(a2.sem, a2.prev(i, f"xt{t}"))
                        for kt in range(KT):
                            last = tr(ps[:, t, kt * P:(kt + 1) * P], x2[t][:, kt * P:(kt + 1) * P], ident)
                        last.then_inc(e2.sem, e2.did(f"xt{t}"))
                    for t in range(2):
                        pe.wait_ge(a2.sem, a2.now(i, f"xt{t}"))
                        pe.wait_ge(a2.sem, a2.prev(i, f"exp{t}"))
                        for kt in range(KT):
                            last = mm(ps[:, 2 + t, 0:SC], x2T[t][:, kt, :], k2[:, kt, bass.ds(i, 1), :],
                                      start=kt == 0, stop=kt == KT - 1)
                        last.then_inc(e2.sem, e2.did(f"s{t}"))
                    for t in range(2):
                        pe.wait_ge(a2.sem, a2.now(i, f"exp{t}"))
                        pe.wait_ge(a2.sem, a2.prev(i, f"pt{t}"))
                        settle(pe)
                        tr(ps[0:SC, 4 + t, 0:P], p2[t][:, :], ident).then_inc(e2.sem, e2.did(f"pt{t}"))
                    for t in range(2):
                        pe.wait_ge(a2.sem, a2.now(i, f"pt{t}"))
                        pe.wait_ge(d2.sem, d2.prev(i, f"y{t}"))
                        settle(pe)
                        mm(ps[:, 6 + t, 0:D], pT2[t][:, :], v2[:, bass.ds(i, 1), :], start=True,
                           stop=True).then_inc(e2.sem, e2.did(f"o{t}"))

            def head_products(a):
                with pe.Fori(0, HP) as i:
                    for t in range(2):
                        w = bun[t]
                        wk = w[:, 0:D].rearrange("p (k n) -> p k n", k=KT)
                        wqT, wo = w[:, D:2 * D], w[:, 3 * D:4 * D]
                        wv = w[:, 2 * D:3 * D].rearrange("p (k n) -> p k n", k=KT)
                        bq, bias_k, bias_v = w[:, 4 * D + 1:4 * D + 2], w[:, 4 * D + 3:4 * D + 4], w[:, 4 * D + 4:BUN]
                        older = lambda s, n: s.now(i, n + "0") if t else s.prev(i, n + "1")
                        pe.wait_ge(dma_bun[a][t], 16 * i + 16)
                        pe.wait_ge(dp[a].sem, older(dp[a], "k"))
                        for kt in range(KT):
                            last = mm(ps[:, 0, :], wk[:, kt, :], cT[:, kt, :], start=kt == 0, stop=kt == KT - 1)
                        last.then_inc(ep[a].sem, ep[a].did(f"k{t}"))
                        pe.wait_ge(dp[a].sem, dp[a].now(i, f"k{t}"))
                        pe.wait_ge(ap_[a].sem, older(ap_[a], "g"))
                        for mt in range(KT):
                            last = mm(ps[:, 1 + mt, :], wqT[:, mt * P:(mt + 1) * P], kh[:, :], start=True, stop=True)
                        last.then_inc(ep[a].sem, ep[a].did(f"g{t}"))
                        pe.wait_ge(ap_[a].sem, older(ap_[a], "b"))
                        mm(ps[0:1, 3, :], bq, kh[:, :], start=True, stop=True).then_inc(ep[a].sem, ep[a].did(f"b{t}"))
                        pe.wait_ge(ap_[a].sem, older(ap_[a], "v"))
                        for kt in range(KT):
                            last = mm(ps[:, 4, :], wv[:, kt, :], cT[:, kt, :], start=kt == 0, stop=kt == KT - 1)
                        last.then_inc(ep[a].sem, ep[a].did(f"v{t}"))
                        pe.wait_ge(ap_[a].sem, ap_[a].now(i, f"v{t}"))
                        pe.wait_ge(ap_[a].sem, older(ap_[a], "w"))
                        pe.wait_ge(dp[a].sem, older(dp[a], "w"))
                        for bp in range(4):
                            last = mm(ps[:, 5 + bp // 2, (bp % 2) * D:(bp % 2 + 1) * D], vh[:, bp * P:(bp + 1) * P], wo,
                                      start=True, stop=True)
                        last.then_inc(ep[a].sem, ep[a].did(f"w{t}"))
                        pe.wait_ge(dp[a].sem, older(dp[a], "vb"))
                        mm(ps[0:H3, 7, 0:D], bias_v, wo, start=True, stop=True)
                        for mt in range(KT):
                            mm(ps[:, 7, D + mt:D + mt + 1], wqT[:, mt * P:(mt + 1) * P], bias_k, start=True, stop=True)
                        mm(ps[0:1, 7, D + 4:D + 5], bq, bias_k, start=True, stop=True).then_inc(ep[a].sem, ep[a].did(f"r{t}"))

            def attend(a):
                with pe.Fori(0, B) as i:
                    for t in range(2):
                        pe.wait_ge(d3[a].sem, d3[a].now(i, f"hn{t}"))
                        if t:
                            pe.wait_ge(a3[a].sem, a3[a].now(i, "h0"))
                        else:
                            pe.wait_ge(d3[a].sem, d3[a].prev(i, "y0"))
                        for kt in range(KT):
                            last = tr(ps[:, 6, kt * P:(kt + 1) * P], hn[t][:, kt * P:(kt + 1) * P], ident)
                        last.then_inc(e3[a].sem, e3[a].did(f"h{t}"))
                    pe.wait_ge(a3[a].sem, a3[a].now(i, "h1"))
                    pe.wait_ge(d3[a].sem, d3[a].prev(i, "y1"))
                    for t in range(2):
                        for kt in range(KT):
                            mm(ps[:, 7, t * H3:(t + 1) * H3], hT[t][:, kt, :], gb3[:, kt, :], start=kt == 0, stop=False)
                        last = mm(ps[:, 7, t * H3:(t + 1) * H3], one3[:, :], bb3[:, :], start=False, stop=True)
                    last.then_inc(e3[a].sem, e3[a].did("sb"))
                    for t in range(2):
                        for c in range(2):
                            for kt in range(KT):
                                mm(ps[:, 2 * t + c, :], hT[t][:, kt, :], g3[:, kt, bass.ds(i, 1), c * 512:(c + 1) * 512],
                                   start=kt == 0, stop=False)
                            last = mm(ps[:, 2 * t + c, :], one3[:, :], bt3[:, bass.ds(i, 1), c * 512:(c + 1) * 512],
                                      start=False, stop=True)
                        last.then_inc(e3[a].sem, e3[a].did(f"s{t}"))
                    for t in range(2):
                        pe.wait_ge(g3s[a].sem, g3s[a].now(i, f"nrm{t}"))
                        pe.wait_ge(d3[a].sem, d3[a].now(i, f"nb{t}"))
                        for half, name in ((0, "a"), (1, "b")):
                            copied = {"a": "cc", "b": "cb"}[name]
                            older = a3[a].now(i, f"{copied}0") if t else a3[a].prev(i, f"{copied}1")
                            pe.wait_ge(a3[a].sem, older)
                            for k in range(4):
                                blk = 4 * half + k
                                last = tr(ps[:, 4 + half, k * P:(k + 1) * P], p3[t][:, blk * P:(blk + 1) * P], ident)
                            last.then_inc(e3[a].sem, e3[a].did(f"t{name}{t}"))
                        pe.wait_ge(a3[a].sem, a3[a].now(i, f"ca{t}"))
                        tr(ps[0:H3, 4, 0:P], p3[t][:, KEYS3:KEYS3 + H3], ident).then_inc(e3[a].sem, e3[a].did(f"tc{t}"))
                        pe.wait_ge(d3[a].sem, d3[a].now(i, "subb1"))
                        o = ps[:, 6 + t, 0:D]
                        for half, name in ((0, "a"), (1, "b")):
                            pe.wait_ge(a3[a].sem, a3[a].now(i, f"c{name}{t}"))
                            for k in range(4):
                                mm(o, pT3[half][:, k, :], v3[:, bass.ds(i, 1), 4 * half + k, :],
                                   start=half == 0 and k == 0, stop=False)
                        pe.wait_ge(a3[a].sem, a3[a].now(i, f"cc{t}"))
                        mm(o, pb3[:, :], vb3[:, :], start=False, stop=True).then_inc(e3[a].sem, e3[a].did(f"o{t}"))

            for a in range(2):
                if stop >= 4 + 2 * a:
                    if a == 0:
                        pe.wait_ge(d2.sem, d2.end(B))
                        pe.wait_ge(a2.sem, a2.end(B))
                    else:
                        pe.wait_ge(d3[0].sem, d3[0].end(B))
                        pe.wait_ge(a3[0].sem, a3[0].end(B))
                    head_products(a)
                if stop >= 5 + 2 * a:
                    pe.wait_ge(dp[a].sem, dp[a].end(HP))
                    pe.wait_ge(ap_[a].sem, ap_[a].end(HP))
                    attend(a)
            if stop >= 8:
                pe.wait_ge(d3[1].sem, d3[1].end(B))
                pe.wait_ge(a3[1].sem, a3[1].end(B))
                mlp_products(1, m3, dma_m3, lambda i, kt: xc3[:, kt, :])

        @block.scalar
        def _(act):
            def copy(o, x, bias=0.0, scale=1.0):
                return nc.scalar.activation(o, x, ACT.Identity, bias=bias, scale=scale)

            def exp(o, x, bias=0.0, scale=1.0):
                return nc.scalar.activation(o, x, ACT.Exp, bias=bias, scale=scale)

            for s in [a0, a1, a2] + am + ap_ + a3:
                act.sem_inc(s.sem, s.per)
            act.wait_ge(dma_k, 80)

            act.wait_ge(dma_xT, 16)
            with act.Fori(0, B) as i:
                def weights(t):
                    act.wait_ge(g0.sem, g0.now(i, f"sh{t}"))
                    exp(p0[t][:, :], p0[t][:, :]).then_inc(a0.sem, a0.did(f"exp{t}"))

                def turned(t, c, bank):
                    act.wait_ge(e0.sem, e0.now(i, f"t{t}{c}"))
                    if c >= 2:
                        act.wait_ge(e0.sem, e0.now(i, f"v{t}{c - 2}"))
                    elif t == 1:
                        act.wait_ge(e0.sem, e0.now(i, f"v0{c + 2}"))
                    else:
                        act.wait_ge(e0.sem, e0.prev(i, f"v1{c + 2}"))
                    copy(pt0[c % 2][:, :], ps[:, bank, :]).then_inc(a0.sem, a0.did(f"c{t}{c}"))

                def heads_out(t):
                    act.wait_ge(e0.sem, e0.now(i, f"aot{t}"))
                    act.wait_ge(e0.sem, e0.now(i, "out0") if t else e0.prev(i, "out1"))
                    copy(aoT0[:, 0, :], ps[:, 4, 0:P], bias=pvec("L0_bv", 0))
                    copy(aoT0[:, 1, :], ps[:, 4, P:2 * P], bias=pvec("L0_bv", 1)).then_inc(a0.sem, a0.did(f"aot{t}"))

                def x_out(t):
                    act.wait_ge(e0.sem, e0.now(i, f"xt{t}"))
                    copy(xT[:, 0, bass.ds(i * S + t * P, P)], ps[:, 5, 0:P], pvec("L0_beta", 0), pvec("L0_gamma", 0))
                    copy(xT[:, 1, bass.ds(i * S + t * P, P)], ps[:, 5, P:2 * P], pvec("L0_beta", 1),
                         pvec("L0_gamma", 1)).then_inc(a0.sem, a0.did(f"xt{t}"))

                weights(0)
                turned(0, 0, 4)
                turned(0, 1, 5)
                turned(0, 2, 4)
                turned(0, 3, 5)
                weights(1)
                turned(1, 0, 4)
                turned(1, 1, 5)
                heads_out(0)
                turned(1, 2, 5)
                turned(1, 3, 4)
                x_out(0)
                heads_out(1)
                x_out(1)

            if stop >= 1:
                act.wait_ge(d0.sem, d0.end(B))
                act.wait_ge(g0.sem, g0.end(B))
                with act.Fori(0, B) as i:
                    act.wait_ge(e1.sem, e1.now(i, "v"))
                    act.wait_ge(ppo.sem, ppo.now(0, "ones"))
                    act.wait_ge(d1.sem, d1.now(i, "q"))
                    copy(v1[:, :, :, 0:D1], ps[:, 5, :].rearrange("p (t h d) -> p t h d", t=QT_B, h=H1)
                         ).then_inc(a1.sem, a1.did("v"))

                    def weights(u):
                        act.wait_ge(d1.sem, d1.now(i, f"mx{u}"))
                        act.wait_ge(e1.sem, e1.now(i, f"t{u - 2}") if u >= 2 else e1.prev(i, f"t{u + 14}"))
                        for e in range(2):
                            last = exp(p1[u % 2][:, e * KEYS1:(e + 1) * KEYS1], ps[:, 2 * (u % 2) + e, 0:KEYS1],
                                       bias=nm1[:, u, e:e + 1])
                        last.then_inc(a1.sem, a1.did(f"e{u}"))

                    weights(0)
                    for u in range(16):
                        if u < 15:
                            weights(u + 1)
                        act.wait_ge(e1.sem, e1.now(i, f"t{u}"))
                        act.wait_ge(e1.sem, e1.now(i, f"a{u - 2}") if u >= 2 else e1.prev(i, f"a{u + 14}"))
                        copy(pc1[u % 2][:, :], ps[:, 6, 0:P]).then_inc(a1.sem, a1.did(f"c{u}"))
                        for t, at, name in ((0, 9, "aot"), (0, 13, "nt"), (1, 15, "aot"), (1, 15, "nt")):
                            if u != at:
                                continue
                            act.wait_ge(e1.sem, e1.now(i, f"{name}{t}"))
                            o = ps[:, 6, 256:512]
                            if name == "aot":
                                for kt in range(KT):
                                    last = copy(aoT1[:, kt, :], o[:, kt * P:(kt + 1) * P], bias=pvec("L1_bv", kt))
                            else:
                                for kt in range(KT):
                                    last = copy(nT[:, kt, bass.ds(i * S + t * P, P)], o[:, kt * P:(kt + 1) * P],
                                                scale=pvec("L1_norm", kt))
                            last.then_inc(a1.sem, a1.did(f"{name}{t}"))

            def mlp_gelu(m, w, func):
                with act.Fori(0, NCH) as i:
                    if m:
                        for t in range(QC):
                            act.wait_ge(em[1].sem, em[1].now(i, f"x{t}"))
                            act.wait_ge(em[1].sem, em[1].prev(i, f"h{FT - 1}"))
                            for kt in range(KT):
                                last = copy(xc3[:, kt, t * P:(t + 1) * P], ps[:, 4 + t % 2, kt * P:(kt + 1) * P],
                                            pvec("lnm_o", kt), pvec("lnm_s", kt))
                            last.then_inc(am[1].sem, am[1].did(f"x{t}"))
                    for ft in range(FT):
                        act.wait_ge(em[m].sem, em[m].now(i, f"h{ft}"))
                        nc.scalar.activation(w["h"][:, ft, :], ps[:, ft % 2, :], func, bias=fvec(m, ft)
                                             ).then_inc(am[m].sem, am[m].did(f"h{ft}"))

            if stop >= 2:
                act.wait_ge(e1.sem, e1.end(B))
                act.wait_ge(d1.sem, d1.end(B))
                mlp_gelu(0, m1, ACT.Gelu_apprx_tanh)

            if stop >= 3:
                act.wait_ge(dv2p.sem, dv2p.now(0, "vo"))
                with act.Fori(0, B) as i:
                    for t in range(2):
                        act.wait_ge(e2.sem, e2.now(i, f"xt{t}"))
                        act.wait_ge(e2.sem, e2.prev(i, f"s{t}"))
                        copy(x2T[t][:, :, :], ps[:, t, 0:D].rearrange("p (k n) -> p k n", k=KT)
                             ).then_inc(a2.sem, a2.did(f"xt{t}"))
                    for t in range(2):
                        act.wait_ge(d2.sem, d2.now(i, f"max{t}"))
                        act.wait_ge(d2.sem, d2.prev(i, f"sum{t}"))
                        act.wait_ge(e2.sem, e2.prev(i, f"pt{t}"))
                        exp(p2[t][:, :], ps[:, 2 + t, 0:SC], bias=sm2[t][:, 0:1], scale=SCALE2).then_inc(a2.sem, a2.did(f"exp{t}"))
                    for t in range(2):
                        act.wait_ge(e2.sem, e2.now(i, f"pt{t}"))
                        act.wait_ge(e2.sem, e2.prev(i, f"o{t}"))
                        copy(pT2[t][:, :], ps[0:SC, 4 + t, 0:P]).then_inc(a2.sem, a2.did(f"pt{t}"))

            def head_copies(a):
                with act.Fori(0, HP) as i:
                    for t in range(2):
                        act.wait_ge(dma_bun[a][t], 16 * i + 16)
                        act.wait_ge(ep[a].sem, ep[a].now(i, f"g{t}"))
                        for mt in range(KT):
                            last = copy(g3[:, mt, :, bass.ds(i * 2 * SC + t * SC, SC)],
                                        ps[:, 1 + mt, :].rearrange("p (b k) -> p b k", b=B))
                        last.then_inc(ap_[a].sem, ap_[a].did(f"g{t}"))
                        act.wait_ge(ep[a].sem, ep[a].now(i, f"b{t}"))
                        copy(bt3[:, :, bass.ds(i * 2 * SC + t * SC, SC)],
                             ps[0:1, 3, :].rearrange("p (b k) -> p b k", b=B)).then_inc(ap_[a].sem, ap_[a].did(f"b{t}"))
                        act.wait_ge(ep[a].sem, ep[a].now(i, f"v{t}"))
                        act.wait_ge(ep[a].sem, ep[a].now(i, "w0") if t else ep[a].prev(i, "w1"))
                        copy(vh[:, :], ps[:, 4, :], bias=bun[t][:, 4 * D + 2:4 * D + 3]).then_inc(ap_[a].sem, ap_[a].did(f"v{t}"))
                        act.wait_ge(ep[a].sem, ep[a].now(i, f"w{t}"))
                        copy(v3[HALF * t:HALF * (t + 1), 0:B:2, bass.ds(i, 1), :].rearrange("p b o n -> p b (o n)"),
                             ps[0:HALF, 5:7, :].rearrange("p k (c n) -> p (k c) n", c=2)).then_inc(ap_[a].sem, ap_[a].did(f"w{t}"))

            def attend(a):
                with act.Fori(0, B) as i:
                    for t in range(2):
                        act.wait_ge(e3[a].sem, e3[a].now(i, f"h{t}"))
                        act.wait_ge(e3[a].sem, e3[a].prev(i, f"s{t}"))
                        for kt in range(KT):
                            last = copy(hT[t][:, kt, :], ps[:, 6, kt * P:(kt + 1) * P], pvec(f"ln{a + 1}_o", kt),
                                        pvec(f"ln{a + 1}_s", kt))
                        last.then_inc(a3[a].sem, a3[a].did(f"h{t}"))
                    for t in range(2):
                        act.wait_ge(d3[a].sem, d3[a].now(i, f"subb{t}"))
                        exp(p3[t][:, :], p3[t][:, :], scale=SCALE3).then_inc(a3[a].sem, a3[a].did(f"exp{t}"))
                    for t in range(2):
                        for half, name in ((0, "a"), (1, "b")):
                            act.wait_ge(e3[a].sem, e3[a].now(i, f"t{name}{t}"))
                            act.wait_ge(e3[a].sem, e3[a].now(i, "o0") if t else e3[a].prev(i, "o1"))
                            copy(pT3[half][:, :, :], ps[:, 4 + half, :].rearrange("p (k n) -> p k n", k=4)
                                 ).then_inc(a3[a].sem, a3[a].did(f"c{name}{t}"))
                        act.wait_ge(e3[a].sem, e3[a].now(i, f"tc{t}"))
                        copy(pb3[:, :], ps[0:H3, 4, 0:P]).then_inc(a3[a].sem, a3[a].did(f"cc{t}"))

            for a in range(2):
                if stop >= 4 + 2 * a:
                    if a == 0:
                        act.wait_ge(e2.sem, e2.end(B))
                        act.wait_ge(d2.sem, d2.end(B))
                    else:
                        act.wait_ge(e3[0].sem, e3[0].end(B))
                        act.wait_ge(d3[0].sem, d3[0].end(B))
                    head_copies(a)
                if stop >= 5 + 2 * a:
                    act.wait_ge(dp[a].sem, dp[a].end(HP))
                    act.wait_ge(ep[a].sem, ep[a].end(HP))
                    attend(a)
            if stop >= 8:
                act.wait_ge(e3[1].sem, e3[1].end(B))
                act.wait_ge(d3[1].sem, d3[1].end(B))
                mlp_gelu(1, m3, ACT.Gelu)

        @block.vector
        def _(dve):
            v = nc.vector
            for s in [pdv, d0, d1, dv2p, d2] + dm + dp + d3:
                dve.sem_inc(s.sem, s.per)

            def step(s, i, name, ins):
                ins.then_inc(s.sem, s.did(name))
                dve.wait_ge(s.sem, s.now(i, name))

            step(pdv, 0, "ones", v.memset(ones[:, :], 1.0))
            dve.wait_ge(dma_k, 80)
            dve.wait_ge(ppe.sem, ppe.now(0, "k0"))
            for mt in range(KT):
                for j in range(4):
                    last = v.tensor_scalar(kbd[:, mt, :, j * SC:(j + 1) * SC], ps[:, mt, :].rearrange("p (b k) -> p b k", b=B),
                                           pvec("L0_bk", mt), const("quarter", j), ALU.add, ALU.mult)
            last.then_inc(pdv.sem, pdv.did("k0"))
            dve.wait_ge(ppe.sem, ppe.now(0, "v0"))
            for hf in range(2):
                v.tensor_scalar(vbd[:, :, hf, 0:D0], ps[:, 2, :].rearrange("p (g d) -> p g d", d=D0),
                                const("half", hf), None, ALU.mult)
                last = v.tensor_scalar(vbd[:, :, hf, D0:D0 + 1], ones[:, 0:B * G0].unsqueeze(2), const("half", hf), None, ALU.mult)
            last.then_inc(pdv.sem, pdv.did("v0"))
            dve.wait_ge(ppe.sem, ppe.now(0, "v1"))
            for e in range(2):
                heads = vc1[:, :, :, :].rearrange("p b (g e r) d -> p (b g) e r d", e=2, r=2)[:, :, e]
                v.tensor_scalar(heads[:, :, :, D1:D1 + 1], ones[:, 0:B * H1 // 2].rearrange("p (g r o) -> p g r o", r=2, o=1),
                                const("half", e), None, ALU.mult)
                last = v.tensor_scalar(heads[:, :, :, 0:D1],
                                       ps[:, 3:7, :].rearrange("p k (g e r d) -> p (k g) e r d", e=2, r=2, d=D1)[:, :, e],
                                       const("half", e), None, ALU.mult)
            last.then_inc(pdv.sem, pdv.did("v1"))
            dve.wait_ge(dma_m, 32)
            v.tensor_scalar(mask1[:, :], maski[:, :], 0.0, MASKED, ALU.is_equal, ALU.mult).then_inc(pdv.sem, pdv.did("m1"))

            with dve.Fori(0, B) as i:
                dve.wait_ge(e0.sem, e0.now(i, "q"))
                for mt in range(KT):
                    last = v.tensor_scalar(q0[:, mt, :], ps[:, 7, mt * S:(mt + 1) * S], pvec("L0_bq", mt), SCALE0, ALU.add, ALU.mult)
                last.then_inc(d0.sem, d0.did("q"))
                for t in range(2):
                    dve.wait_ge(e0.sem, e0.now(i, f"s{t}"))
                    dve.wait_ge(e0.sem, e0.prev(i, f"t{t}3"))
                    step(d0, i, f"mask{t}", v.tensor_tensor(
                        p0[t][:, :].rearrange("p (h k) -> p h k", k=SC), ps[:, 0:4, :].rearrange("p j (h k) -> p (j h) k", k=SC),
                        mask0[:, bass.ds(2 * i + t, 1), :].broadcast_to([P, H0, SC]), ALU.add))
                    dve.wait_ge(g0.sem, g0.prev(i, f"sh{t}"))
                    v.tensor_reduce(mx0[t][:, :], p0[t][:, :].rearrange("p (h k) -> p h k", k=SC), X, ALU.max
                                    ).then_inc(d0.sem, d0.did(f"max{t}"))
                for t in range(2):
                    dve.wait_ge(e0.sem, e0.now(i, f"v{t}3"))
                    av = ps[:, 6, 0:H0 * (D0 + 1)].rearrange("p (h d) -> p h d", d=D0 + 1)
                    step(d0, i, f"inv{t}", v.reciprocal(ri0[:, :].unsqueeze(2), av[:, :, D0:D0 + 1]))
                    dve.wait_ge(e0.sem, e0.now(i, "aot0") if t else e0.prev(i, "aot1"))
                    for kt in range(KT):
                        last = v.tensor_tensor(
                            ao0[:, kt * P:(kt + 1) * P].rearrange("p (j h d) -> p j h d", j=4, h=4),
                            av[:, :, 0:D0].rearrange("p (j k h) d -> p j k h d", j=4, k=2)[:, :, kt],
                            ri0[:, :].rearrange("p (j k h) -> p j k h", j=4, k=2)[:, :, kt].unsqueeze(3).broadcast_to([P, 4, 4, D0]),
                            ALU.mult)
                    last.then_inc(d0.sem, d0.did(f"ao{t}"))
                    dve.wait_ge(e0.sem, e0.now(i, f"out{t}"))
                    dve.wait_ge(g0.sem, g0.now(i, f"xb{t}"))
                    step(d0, i, f"y{t}", v.tensor_tensor(y0[:, :], ps[:, 7, 0:D], xb0[t][:, :], ALU.add))
                    step(d0, i, f"bn{t}", v.bn_stats(st0[:, :], y0[:, :]))
                    settle(dve)
                    step(d0, i, f"mv{t}", v.bn_aggr(mv0[t][:, 0:2], st0[:, :]))
                    v.tensor_scalar(mv0[t][:, 2:3], mv0[t][:, 1:2], EPS0, None, ALU.add).then_inc(d0.sem, d0.did(f"eps{t}"))
                    dve.wait_ge(g0.sem, g0.now(i, f"rs{t}"))
                    dve.wait_ge(e0.sem, e0.prev(i, f"xt{t}"))
                    dve.wait_ge(g0.sem, g0.prev(i, f"xg{t}"))
                    v.tensor_scalar(xn0[t][:, :], y0[:, :], mv0[t][:, 0:1], mv0[t][:, 3:4], ALU.subtract, ALU.mult
                                    ).then_inc(d0.sem, d0.did(f"xn{t}"))

            if stop >= 1:
                dve.wait_ge(a0.sem, a0.end(B))
                dve.wait_ge(g0.sem, g0.end(B))
                dve.wait_ge(e0.sem, e0.end(B))
                with dve.Fori(0, B) as i:
                    dve.wait_ge(e1.sem, e1.now(i, "q"))
                    for mt in range(KT):
                        last = v.tensor_scalar(q1[:, mt, :], ps[:, 4, mt * S:(mt + 1) * S], pvec("L1_bq", mt), SCALE1, ALU.add, ALU.mult)
                    last.then_inc(d1.sem, d1.did("q"))
                    dve.wait_ge(e1.sem, e1.now(i, "k"))
                    for mt in range(KT):
                        for par in range(2):
                            last = v.tensor_scalar(k1[:, mt, par, :], ps[:, mt, 0:SC + KEYS1], pvec("L1_bk", mt),
                                                   const("parity", par), ALU.add, ALU.mult)
                    last.then_inc(d1.sem, d1.did("k"))

                    def maxima(u):
                        dve.wait_ge(e1.sem, e1.now(i, f"s{u}"))
                        two_banks = ps[:, 2 * (u % 2):2 * (u % 2) + 2, :]
                        c = two_banks.rearrange("p e n -> p (e n)")[:, 256:768].rearrange("p (e n) -> p e n", e=2)[:, :, 0:SC]
                        step(d1, i, f"mk{u}", v.tensor_tensor(c, c, mask1[:, bass.ds(i * SC, SC)].unsqueeze(1).broadcast_to([P, 2, SC]), ALU.add))
                        v.tensor_reduce(nm1[:, u, :], two_banks[:, :, 0:KEYS1], X, ALU.max, negate=True
                                        ).then_inc(d1.sem, d1.did(f"mx{u}"))

                    def heads_out(t):
                        dve.wait_ge(e1.sem, e1.now(i, f"a{8 * t + 7}"))
                        av = ps[:, 7, 0:H1 * (D1 + 1)].rearrange("p (h d) -> p h d", d=D1 + 1)
                        step(d1, i, f"inv{t}", v.reciprocal(ri1[:, :].unsqueeze(2), av[:, :, D1:D1 + 1]))
                        v.tensor_tensor(ao1[:, :].rearrange("p (h d) -> p h d", h=H1), av[:, :, 0:D1],
                                        ri1[:, :].unsqueeze(2).broadcast_to([P, H1, D1]), ALU.mult).then_inc(d1.sem, d1.did(f"ao{t}"))

                    def residual(t):
                        dve.wait_ge(e1.sem, e1.now(i, f"out{t}"))
                        dve.wait_ge(g1.sem, g1.now(i, f"xb{t}"))
                        step(d1, i, f"y{t}", v.tensor_tensor(y1[t][:, :], ps[:, 6, 256:512], xb1[t][:, :], ALU.add))
                        step(d1, i, f"sq{t}", v.tensor_tensor_reduce(sq1[:, :], y1[t][:, :], y1[t][:, :], 1.0, 0.0, ALU.mult,
                                                                    ALU.add, ms1[t][:, 0:1]))
                        v.tensor_scalar(ms1[t][:, 1:2], ms1[t][:, 0:1], 1.0 / D, EPS1, ALU.mult, ALU.add).then_inc(d1.sem, d1.did(f"eps{t}"))

                    def normed(t):
                        dve.wait_ge(g1.sem, g1.now(i, f"rs{t}"))
                        dve.wait_ge(e1.sem, e1.now(i, "nt0") if t else e1.prev(i, "nt1"))
                        v.tensor_scalar(n1[:, :], y1[t][:, :], ms1[t][:, 2:3], None, ALU.mult).then_inc(d1.sem, d1.did(f"n{t}"))

                    maxima(0)
                    maxima(1)
                    for u in range(16):
                        dve.wait_ge(e1.sem, e1.now(i, f"t{u}"))
                        dve.wait_ge(e1.sem, e1.now(i, f"a{u - 2}") if u >= 2 else e1.prev(i, f"a{u + 14}"))
                        v.tensor_copy(pt1[u % 2][:, :, :], ps[:, 4 + u % 2, :].rearrange("p (k n) -> p k n", k=4)
                                      ).then_inc(d1.sem, d1.did(f"pt{u}"))
                        if u < 14:
                            maxima(u + 2)
                        if u == 8:
                            heads_out(0)
                        if u == 10:
                            residual(0)
                        if u == 12:
                            normed(0)
                    heads_out(1)
                    residual(1)
                    normed(1)

            def norm_rows(s, i, t, rows, stats, mv, rs, eps, dst, name, free):
                settle(dve)
                step(s, i, f"bn{t}", v.bn_stats(stats[:, :], rows))
                settle(dve)
                step(s, i, f"mv{t}", v.bn_aggr(mv[:, 0:2], stats[:, :]))
                v.tensor_scalar(mv[:, 2:3], mv[:, 1:2], eps, None, ALU.add).then_inc(s.sem, s.did(f"eps{t}"))
                dve.wait_ge(rs.sem, rs.now(i, f"rs{t}"))
                free()
                v.tensor_scalar(dst, rows, mv[:, 0:1], mv[:, 3:4], ALU.subtract, ALU.mult).then_inc(s.sem, s.did(f"{name}{t}"))

            def mlp_rows(m, w):
                with dve.Fori(0, NCH) as i:
                    if m:
                        for t in range(QC):
                            def free(t=t):
                                dve.wait_ge(em[1].sem, em[1].now(i, f"x{t - 2}") if t >= 2 else em[1].prev(i, f"x{t + 2}"))
                            norm_rows(dm[1], i, t, xr[:, bass.ds(i * QC + t, 1), :].rearrange("p o n -> p (o n)"), stm, mvm[t % 2],
                                      gm[1], EPS3, hnm[t % 2][:, :], "xn", free)
                    for t in range(QC):
                        dve.wait_ge(em[m].sem, em[m].now(i, f"o{t}"))
                        dve.wait_ge(gm[m].sem, gm[m].now(i, f"xb{t}"))
                        v.tensor_tensor(xr[:, bass.ds(i * QC + t, 1), :].rearrange("p o n -> p (o n)"), ps[:, 2 + t % 2, 0:D], w["xb"][t % 2][:, :], ALU.add
                                        ).then_inc(dm[m].sem, dm[m].did(f"o{t}"))

            if stop >= 2:
                mlp_rows(0, m1)

            if stop >= 3:
                dve.wait_ge(pe2p.sem, pe2p.now(0, "k"))
                for mt in range(KT):
                    last = v.tensor_copy(t2[:, 0, mt, :], ps[:, mt, :])
                last.then_inc(dv2p.sem, dv2p.did("k"))
                dve.wait_ge(pe2p.sem, pe2p.now(0, "kq"))
                for mt in range(KT):
                    last = v.tensor_copy(k2[:, mt, :, :], ps[:, 4 + mt, :].rearrange("p (b k) -> p b k", b=B))
                last.then_inc(dv2p.sem, dv2p.did("kq"))
                dve.wait_ge(pe2p.sem, pe2p.now(0, "v"))
                for mt in range(KT):
                    last = v.tensor_copy(t2[:, 1, mt, :], ps[:, 2 + mt, :])
                last.then_inc(dv2p.sem, dv2p.did("v"))
                dve.wait_ge(pe2p.sem, pe2p.now(0, "vo"))
                v.tensor_scalar(v2[:, :, :].rearrange("p b n -> p (b n)"), ps[0:SC, 4:8, :].rearrange("p k n -> p (k n)"),
                                alpha[0:SC, :], None, ALU.mult).then_inc(dv2p.sem, dv2p.did("vo"))
                with dve.Fori(0, B) as i:
                    for t in range(2):
                        dve.wait_ge(e2.sem, e2.now(i, f"s{t}"))
                        dve.wait_ge(a2.sem, a2.prev(i, f"exp{t}"))
                        dve.wait_ge(d2.sem, d2.prev(i, f"y{t}"))
                        step(d2, i, f"m{t}", v.tensor_reduce(sm2[t][:, 3:4], ps[:, 2 + t, 0:SC], X, ALU.max, negate=True))
                        v.tensor_scalar(sm2[t][:, 0:1], sm2[t][:, 3:4], SCALE2, None, ALU.mult).then_inc(d2.sem, d2.did(f"max{t}"))
                    for t in range(2):
                        dve.wait_ge(a2.sem, a2.now(i, f"exp{t}"))
                        step(d2, i, f"s{t}", v.tensor_reduce(sm2[t][:, 1:2], p2[t][:, :], X, ALU.add))
                        step(d2, i, f"sum{t}", v.reciprocal(sm2[t][:, 2:3], sm2[t][:, 1:2]))
                    for t in range(2):
                        dve.wait_ge(e2.sem, e2.now(i, f"o{t}"))
                        xq = xr[:, bass.ds(2 * i + t, 1), :].rearrange("p o n -> p (o n)")
                        v.scalar_tensor_tensor(xq, ps[:, 6 + t, 0:D], sm2[t][:, 2:3], xq, ALU.mult, ALU.add).then_inc(d2.sem, d2.did(f"y{t}"))

            def head_copies(a):
                with dve.Fori(0, HP) as i:
                    for t in range(2):
                        w = bun[t]
                        dve.wait_ge(dma_bun[a][t], 16 * i + 16)
                        dve.wait_ge(ep[a].sem, ep[a].now(i, f"k{t}"))
                        dve.wait_ge(ep[a].sem, ep[a].now(i, "b0") if t else ep[a].prev(i, "b1"))
                        v.tensor_scalar(kh[:, :], ps[:, 0, :], w[:, 4 * D:4 * D + 1], None, ALU.add).then_inc(dp[a].sem, dp[a].did(f"k{t}"))
                        dve.wait_ge(ep[a].sem, ep[a].now(i, f"w{t}"))
                        v.tensor_copy(v3[HALF * t:HALF * (t + 1), 1:B:2, bass.ds(i, 1), :].rearrange("p b o n -> p b (o n)"),
                                      ps[HALF:P, 5:7, :].rearrange("p k (c n) -> p (k c) n", c=2)).then_inc(dp[a].sem, dp[a].did(f"w{t}"))
                        dve.wait_ge(ep[a].sem, ep[a].now(i, f"r{t}"))
                        v.tensor_copy(gb3[:, :, bass.ds(2 * i + t, 1)], ps[:, 7, D:D + 2].unsqueeze(2))
                        v.tensor_copy(bb3[:, bass.ds(2 * i + t, 1)], ps[0:1, 7, D + 4:D + 5]).then_inc(dp[a].sem, dp[a].did(f"m{t}"))
                        v.tensor_tensor(vb3[:, :], vb3[:, :], ps[0:H3, 7, 0:D], ALU.add).then_inc(dp[a].sem, dp[a].did(f"vb{t}"))

            def attend(a):
                with dve.Fori(0, B) as i:
                    for t in range(2):
                        def free(t=t):
                            dve.wait_ge(e3[a].sem, e3[a].prev(i, f"h{t}"))
                        norm_rows(d3[a], i, t, xr[:, bass.ds(2 * i + t, 1), :].rearrange("p o n -> p (o n)"), st3, mv3[t],
                                  g3s[a], EPS3, hn[t][:, :], "hn", free)
                    for t in range(2):
                        dve.wait_ge(e3[a].sem, e3[a].now(i, f"s{t}"))
                        dve.wait_ge(e3[a].sem, e3[a].prev(i, f"tc{t}"))
                        sc = ps[:, 2 * t:2 * t + 2, :].rearrange("p c (h k) -> p (c h) k", k=SC)
                        sbk = ps[:, 7, t * H3:(t + 1) * H3]
                        step(d3[a], i, f"mx{t}", v.tensor_reduce(mx3[t][:, :], sc, X, ALU.max))
                        step(d3[a], i, f"mb{t}", v.tensor_tensor(mx3[t][:, :], sbk, mx3[t][:, :], ALU.max))
                        v.tensor_tensor(p3[t][:, 0:KEYS3].rearrange("p (h k) -> p h k", k=SC), sc,
                                        mx3[t][:, :].unsqueeze(2).broadcast_to([P, H3, SC]), ALU.subtract).then_inc(d3[a].sem, d3[a].did(f"sub{t}"))
                        v.tensor_tensor(p3[t][:, KEYS3:], sbk, mx3[t][:, :], ALU.subtract).then_inc(d3[a].sem, d3[a].did(f"subb{t}"))
                    for t in range(2):
                        dve.wait_ge(a3[a].sem, a3[a].now(i, f"exp{t}"))
                        dve.wait_ge(g3s[a].sem, g3s[a].prev(i, f"nrm{t}"))
                        step(d3[a], i, f"sum{t}", v.tensor_reduce(sm3[t][:, :], p3[t][:, 0:KEYS3].rearrange("p (h k) -> p h k", k=SC), X, ALU.add))
                        step(d3[a], i, f"sumb{t}", v.tensor_tensor(sm3[t][:, :], sm3[t][:, :], p3[t][:, KEYS3:], ALU.add))
                        step(d3[a], i, f"inv{t}", v.reciprocal(sm3[t][:, :], sm3[t][:, :]))
                        v.tensor_tensor(p3[t][:, KEYS3:], p3[t][:, KEYS3:], sm3[t][:, :], ALU.mult).then_inc(d3[a].sem, d3[a].did(f"nb{t}"))
                    for t in range(2):
                        dve.wait_ge(e3[a].sem, e3[a].now(i, f"o{t}"))
                        dve.wait_ge(g3s[a].sem, g3s[a].now(i, f"xb{t}"))
                        v.tensor_tensor(xr[:, bass.ds(2 * i + t, 1), :].rearrange("p o n -> p (o n)"), ps[:, 6 + t, 0:D],
                                        xb3[t][:, :], ALU.add).then_inc(d3[a].sem, d3[a].did(f"y{t}"))

            for a in range(2):
                if stop >= 4 + 2 * a:
                    if a == 1:
                        dve.wait_ge(e3[0].sem, e3[0].end(B))
                        dve.wait_ge(a3[0].sem, a3[0].end(B))
                    else:
                        dve.wait_ge(e2.sem, e2.end(B))
                        dve.wait_ge(a2.sem, a2.end(B))
                    dve.wait_ge(vbz[a], 1)
                    head_copies(a)
                if stop >= 5 + 2 * a:
                    dve.wait_ge(ap_[a].sem, ap_[a].end(HP))
                    attend(a)
            if stop >= 8:
                dve.wait_ge(e3[1].sem, e3[1].end(B))
                mlp_rows(1, m3)

        @block.gpsimd
        def _(pool):
            g = nc.gpsimd
            for s in [ppo, g0, g1, g2] + gm + g3s:
                pool.sem_inc(s.sem, s.per)
            pool.wait_ge(dma_k, 80)
            pool.wait_ge(dma_x, 16)

            def root(dst, src):
                return g.tensor_tensor(dst, src, const("minus_half"), ALU.pow)

            def xq(i, t):
                return xr[:, bass.ds(2 * i + t, 1), :].rearrange("p o n -> p (o n)")

            pool.wait_ge(pdv.sem, pdv.now(0, "v1"))
            with pool.Fori(0, B) as i:
                pool.wait_ge(e0.sem, e0.prev(i, "s1"))
                settle(pool)
                g.tensor_copy(kb0[:, :, :], kbd[:, :, bass.ds(i, 1), :].rearrange("p k o n -> p k (o n)")).then_inc(g0.sem, g0.did("kb"))
                for t in range(2):
                    pool.wait_ge(d0.sem, d0.prev(i, f"y{t}"))
                    settle(pool)
                    g.tensor_tensor(xb0[t][:, :], xq(i, t), prow("L0_bo"), ALU.add).then_inc(g0.sem, g0.did(f"xb{t}"))
                for t in range(2):
                    pool.wait_ge(d0.sem, d0.now(i, f"max{t}"))
                    p = p0[t][:, :].rearrange("p (h k) -> p h k", k=SC)
                    g.tensor_tensor(p, p, mx0[t][:, :].unsqueeze(2).broadcast_to([P, H0, SC]), ALU.subtract).then_inc(g0.sem, g0.did(f"sh{t}"))
                for t in range(2):
                    pool.wait_ge(d0.sem, d0.now(i, f"eps{t}"))
                    root(mv0[t][:, 3:4], mv0[t][:, 2:3]).then_inc(g0.sem, g0.did(f"rs{t}"))
                    pool.wait_ge(d0.sem, d0.now(i, f"xn{t}"))
                    if t:
                        pool.wait_ge(g0.sem, g0.now(i, "xr0"))
                    else:
                        pool.wait_ge(g0.sem, g0.prev(i, "xr1"))
                    g.tensor_tensor(xg0[:, :], xn0[t][:, :], prow("L0_gamma"), ALU.mult).then_inc(g0.sem, g0.did(f"xg{t}"))
                    pool.wait_ge(g0.sem, g0.now(i, f"xg{t}"))
                    settle(pool)
                    g.tensor_tensor(xq(i, t), xg0[:, :], prow("L0_beta"), ALU.add).then_inc(g0.sem, g0.did(f"xr{t}"))

            if stop >= 1:
                pool.wait_ge(a0.sem, a0.end(B))
                pool.wait_ge(d0.sem, d0.end(B))
                pool.wait_ge(e0.sem, e0.end(B))
                pool.wait_ge(g0.sem, g0.end(B))
                g.memset(v1[:, :, :, D1:D1 + 1], 1.0).then_inc(ppo.sem, ppo.did("ones"))
                with pool.Fori(0, B) as i:
                    pool.wait_ge(e1.sem, e1.prev(i, "v"))
                    settle(pool)
                    g.tensor_copy(xb1T[:, :, :], xT[:, :, bass.ds(i * S, S)]).then_inc(g1.sem, g1.did("xT"))
                    pool.wait_ge(e1.sem, e1.prev(i, "a15"))
                    settle(pool)
                    g.tensor_copy(vb1[:, :, :], vc1[:, bass.ds(i, 1), :, :].rearrange("p o h d -> p (o h) d")).then_inc(g1.sem, g1.did("vb"))
                    for t in range(2):
                        pool.wait_ge(d1.sem, d1.prev(i, f"y{t}"))
                        settle(pool)
                        g.tensor_tensor(xb1[t][:, :], xq(i, t), prow("L1_bo"), ALU.add).then_inc(g1.sem, g1.did(f"xb{t}"))
                    for t in range(2):
                        pool.wait_ge(d1.sem, d1.now(i, f"eps{t}"))
                        root(ms1[t][:, 2:3], ms1[t][:, 1:2]).then_inc(g1.sem, g1.did(f"rs{t}"))

            def mlp_bias(m, w, bias):
                with pool.Fori(0, NCH) as i:
                    if m:
                        for t in range(QC):
                            pool.wait_ge(dm[1].sem, dm[1].now(i, f"eps{t}"))
                            root(mvm[t % 2][:, 3:4], mvm[t % 2][:, 2:3]).then_inc(gm[1].sem, gm[1].did(f"rs{t}"))
                    for t in range(QC):
                        pool.wait_ge(dm[m].sem, dm[m].now(i, f"o{t - 2}") if t >= 2 else dm[m].prev(i, f"o{t + 2}"))
                        settle(pool)
                        g.tensor_tensor(w["xb"][t % 2][:, :], xr[:, bass.ds(i * QC + t, 1), :].rearrange("p o n -> p (o n)"), prow(bias), ALU.add
                                        ).then_inc(gm[m].sem, gm[m].did(f"xb{t}"))

            if stop >= 2:
                pool.wait_ge(e1.sem, e1.end(B))
                pool.wait_ge(d1.sem, d1.end(B))
                pool.wait_ge(a1.sem, a1.end(B))
                mlp_bias(0, m1, "L1_b2")

            if stop >= 3:
                pool.wait_ge(dm[0].sem, dm[0].end(NCH))
                with pool.Fori(0, B) as i:
                    for t in range(2):
                        pool.wait_ge(e2.sem, e2.prev(i, f"xt{t}"))
                        settle(pool)
                        g.tensor_copy(x2[t][:, :], xq(i, t)).then_inc(g2.sem, g2.did(f"x{t}"))

            for a in range(2):
                if stop >= 4 + 2 * a:
                    if a == 0:
                        pool.wait_ge(e2.sem, e2.end(B))
                        pool.wait_ge(d2.sem, d2.end(B))
                    else:
                        pool.wait_ge(e3[0].sem, e3[0].end(B))
                        pool.wait_ge(d3[0].sem, d3[0].end(B))
                    g.memset(one3[:, :], 1.0)
                    g.memset(vb3[:, :], 0.0).then_inc(vbz[a], 1)
                if stop >= 5 + 2 * a:
                    pool.wait_ge(dp[a].sem, dp[a].end(HP))
                    pool.wait_ge(ep[a].sem, ep[a].end(HP))
                    pool.wait_ge(ap_[a].sem, ap_[a].end(HP))
                    with pool.Fori(0, B) as i:
                        for t in range(2):
                            pool.wait_ge(d3[a].sem, d3[a].now(i, f"eps{t}"))
                            root(mv3[t][:, 3:4], mv3[t][:, 2:3]).then_inc(g3s[a].sem, g3s[a].did(f"rs{t}"))
                        for t in range(2):
                            pool.wait_ge(d3[a].sem, d3[a].prev(i, f"y{t}"))
                            settle(pool)
                            g.tensor_tensor(xb3[t][:, :], xq(i, t), prow(f"bo{a + 1}"), ALU.add).then_inc(g3s[a].sem, g3s[a].did(f"xb{t}"))
                        for t in range(2):
                            pool.wait_ge(d3[a].sem, d3[a].now(i, f"inv{t}"))
                            p = p3[t][:, 0:KEYS3].rearrange("p (h k) -> p h k", k=SC)
                            g.tensor_tensor(p, p, sm3[t][:, :].unsqueeze(2).broadcast_to([P, H3, SC]), ALU.mult
                                            ).then_inc(g3s[a].sem, g3s[a].did(f"nrm{t}"))
            if stop >= 8:
                pool.wait_ge(e3[1].sem, e3[1].end(B))
                pool.wait_ge(d3[1].sem, d3[1].end(B))
                mlp_bias(1, m3, "b_fc2")


STOP = 8


def kernel(**inputs):
    import concourse.bacc as bacc
    from concourse.bass_utils import run_bass_kernel_spmd

    a = {k: np.asarray(v) for k, v in inputs.items()}

    def tiles(w):
        return np.ascontiguousarray(w.reshape(-1, P, w.shape[1]).transpose(1, 0, 2)).reshape(P, -1)

    def column(v):
        return v.reshape(-1, P).T

    f = np.float32
    rep = lambda w: np.repeat(w.reshape(w.shape[0], G0, 1, D0), H0 // G0, 2).reshape(w.shape[0], D)
    rows = np.arange(P)
    const = np.concatenate([
        np.eye(P, dtype=f), (rows[:, None] // D0 % 4 == np.arange(4)).astype(f),
        (rows[:, None] // D1 % 2 == np.arange(2)).astype(f), (rows[:, None] // HALF == np.arange(2)).astype(f),
        np.full((P, 1), -0.5, f)], 1)
    kv, kvb = a["L1_xattn_kv_w"].reshape(D, D, 2), a["L1_xattn_kv_b"].reshape(D, 2)
    vecs = {
        "L0_bq": a["L0_xattn_bq"], "L0_bk": rep(a["L0_xattn_bk"][None])[0], "L0_bv": rep(a["L0_xattn_bv"][None])[0],
        "L0_gamma": a["L0_xattn_gamma"], "L0_beta": a["L0_xattn_beta"],
        "L1_bq": a["L1_xattn_q_b"], "L1_bk": kvb[:, 0], "L1_bv": kvb[:, 1], "L1_norm": a["L1_xattn_postnorm_w"],
        "ln1_s": a["L3_xattn_ln1_scale"], "ln1_o": a["L3_xattn_ln1_offset"],
        "ln2_s": a["L3_xattn_ln2_scale"], "ln2_o": a["L3_xattn_ln2_offset"],
        "lnm_s": a["L3_xattn_ln_mlp_scale"], "lnm_o": a["L3_xattn_ln_mlp_offset"]}
    rowv = {"L0_bo": a["L0_xattn_bo"], "L0_gamma": a["L0_xattn_gamma"], "L0_beta": a["L0_xattn_beta"],
            "L1_bo": a["L1_xattn_out_b"], "L1_b2": a["L1_xattn_mlp_b2"], "bo1": a["L3_xattn_bo1"],
            "bo2": a["L3_xattn_bo2"], "b_fc2": a["L3_xattn_b_fc2"]}

    def heads(n):
        g = lambda name: a[f"L3_xattn_{name}{n}"]
        out = np.zeros((H3, P, BUN), f)
        for h in range(H3):
            c = slice(h * D3, (h + 1) * D3)
            out[h, :, 0:D] = tiles(g("wk")[:, c])
            out[h, :, D:2 * D] = g("wq")[:, c].T
            out[h, :, 2 * D:3 * D] = tiles(g("wv")[:, c])
            out[h, :, 3 * D:4 * D] = g("wo")[c]
            for k, v in enumerate((g("bk")[c], g("bq")[c], g("bv")[c], g("bias_k")[0, 0, h])):
                out[h, :, 4 * D + k] = v
            out[h, :, 4 * D + 4 + h] = g("bias_v")[0, 0, h]
        return out

    arrays = {
        "x": a["x"], "xT": tiles(a["x"].reshape(T, D).T).reshape(P, KT, T),
        "ctxT": tiles(a["ctx_2048"].reshape(C, D).T).reshape(P, KT, C),
        "mask0": a["mask_Bx1xSxS2_ff0"], "mask1": a["mask_BxS2_ik0"].reshape(C),
        "const": const, "alpha": a["L2_xattn_alpha"].reshape(1),
        "vecs": np.concatenate([column(vecs[n]) for n in VECS] + [column(a["L1_xattn_mlp_b1"]), column(a["L3_xattn_b_fc1"])], 1),
        "rows": np.stack([rowv[n] for n in ROWS]),
        "w0": np.concatenate([tiles(a["L0_xattn_Wq"]), tiles(rep(a["L0_xattn_Wk"])), tiles(a["L0_xattn_Wo"]),
                              tiles(a["L0_xattn_Wv"])], 1),
        "w1": np.concatenate([tiles(a["L1_xattn_q_w"]), tiles(kv[:, :, 0]), tiles(kv[:, :, 1]), tiles(a["L1_xattn_out_w"])], 1),
        "w2": np.concatenate([tiles(a["L2_xattn_w_q"]), tiles(a["L2_xattn_w_k"].T), tiles(a["L2_xattn_w_v"].T),
                              tiles(a["L2_xattn_w_o"].T)], 1),
        "m1a": tiles(a["L1_xattn_mlp_w1"]).reshape(P, KT, F), "m1b": tiles(a["L1_xattn_mlp_w2"]).reshape(P, FT, D),
        "m3a": tiles(a["L3_xattn_w_fc1"]).reshape(P, KT, F), "m3b": tiles(a["L3_xattn_w_fc2"]).reshape(P, FT, D),
        "heads0": heads(1), "heads1": heads(2),
    }
    arrays = {k: np.ascontiguousarray(v) for k, v in arrays.items()}
    nc = bacc.Bacc("TRN2", target_bir_lowering=False, num_devices=1)
    io = {k: nc.dram_tensor(f"in_{k}", v.shape, mybir.dt.from_np(v.dtype), kind="ExternalInput").ap() for k, v in arrays.items()}
    out = nc.dram_tensor("out", (B, S, D), F32, kind="ExternalOutput").ap()
    build(nc, io, out, STOP)
    r = run_bass_kernel_spmd(nc, [{f"in_{k}": v for k, v in arrays.items()}], core_ids=[0])
    return r.results[0]["out"]
```

```python
from contextlib import ExitStack

import numpy as np

import concourse.bass as bass
from concourse import mybir

F32 = mybir.dt.float32
I32 = mybir.dt.int32
F32R = mybir.dt.float32r
F16 = mybir.dt.float16
BF16 = mybir.dt.bfloat16
ALU = mybir.AluOpType
ACT = mybir.ActivationFunctionType
X = mybir.AxisListType.X

PARTS = ((0, 0), (0, 1), (1, 0))

P = 128
D = 256
KT = D // P
B = 8
S = 256
SC = 64
QT_B = S // P
NQ = B * QT_B
T = B * S
C = B * SC
HALF = P // 2

H0, G0, D0 = 32, 8, 8
SCALE0 = float(1.0 / np.sqrt(np.float32(D0)))
EPS0 = 1e-6
H1, D1 = 16, 16
KEYS1 = S + SC
SCALE1 = 1.0 / D1
EPS1 = 1e-6
MASKED = -3.0e38
WHOLE = float(2 ** 15)
F = 1024
FT = F // P
CH = 512
NCH = T // CH
QC = CH // P
SCALE2 = float(1.0 / np.sqrt(np.float32(D)))
H3, D3 = 16, 128
SCALE3 = float(1.0 / np.sqrt(np.float32(D3)))
EPS3 = 1e-5
HP = H3 // 2
KEYS3 = H3 * SC

CONST = dict(ident=(0, P), quarter=(128, 4), parity=(132, 2), half=(134, 2), minus_half=(136, 1))
NCONST = 137
VECS = ["L0_bq", "L0_bk", "L0_bv", "L0_gamma", "L0_beta", "L1_bq", "L1_bk", "L1_bv", "L1_norm",
        "ln1_s", "ln1_o", "ln2_s", "ln2_o", "lnm_s", "lnm_o"]
NVEC = len(VECS) * KT + 2 * FT
ROWS = ["L0_bo", "L0_gamma", "L0_beta", "L1_bo", "L1_b2", "bo1", "bo2", "b_fc2"]
W0 = dict(wq=(0, 512), wk=(512, 512), wo=(1024, 512), wv=(1536, 128))
W1 = dict(wq=(0, 512), wk=(512, 512), wv=(1024, 512), wo=(1536, 512))
W2 = dict(wq=(0, 512), wkT=(512, 512), wvT=(1024, 512), woT=(1536, 512))
BUN = 4 * D + 4 + H3


class Steps:

    def __init__(self, sem, name, steps):
        self.sem, self.steps, self.per, self.k = sem(name), list(steps), len(steps), 0
        assert len(set(self.steps)) == self.per, name

    def now(self, i, step):
        return (i + 1) * self.per + (self.steps.index(step) + 1)

    def prev(self, i, step):
        return i * self.per + (self.steps.index(step) + 1)

    def end(self, iterations):
        return (iterations + 1) * self.per

    def did(self, step):
        assert self.steps[self.k % self.per] == step, (step, self.steps[self.k % self.per])
        self.k += 1
        return 1


class Tally:

    def __init__(self, sem, name, per, owned):
        self.sem, self.per, self.seed = sem(name), per, per + 1
        owned.append(self)

    def at(self, i, k=0):
        return i * self.per + (k + 1 + self.seed)

    def end(self, iterations):
        return self.at(iterations, -1)



def spread(lead, per_unit, extra, tail):
    out = list(lead)
    for u in range(16):
        out += per_unit(u) + extra.get(u, [])
    return out + list(tail)


def build(nc, io, out, stop=99):
    ctx = ExitStack()
    with ctx:
        def sem(name):
            return ctx.enter_context(nc.semaphore(name))

        def sb(name, shape, dt=F32, where=ctx):
            return where.enter_context(nc.sbuf_tensor(name, shape, dt))

        ps = ctx.enter_context(nc.psum_tensor("ps", [P, 8, 512], F32))

        xr = sb("xr", [P, NQ, D])
        cT = sb("cT", [P, KT, C])
        cst = sb("cst", [P, NCONST])
        vec = sb("vec", [P, NVEC])
        row3 = sb("row3", [P, 3, D])
        alpha = sb("alpha", [P, 1])
        ident = cst[:, 0:P]

        def const(name, k=0):
            return cst[:, CONST[name][0] + k:CONST[name][0] + k + 1]

        def pvec(name, kt):
            c = VECS.index(name) * KT + kt
            return vec[:, c:c + 1]

        def fvec(which, ft):
            c = len(VECS) * KT + which * FT + ft
            return vec[:, c:c + 1]

        def prow(name):
            k = ROWS.index(name)
            return row1[:, k, :] if k < len(ROWS) - 3 else row3[:, k - (len(ROWS) - 3), :]

        def wt(tile, cols, name):
            a, n = cols[name]
            return tile[:, a:a + n].rearrange("p (k n) -> p k n", k=KT)

        upto2 = ExitStack()
        w2 = sb("w2", [P, 2048], where=upto2)
        row1 = sb("row1", [P, len(ROWS) - 3, D], where=upto2)
        early = ExitStack()
        xT = sb("xT", [P, KT, T], where=early)
        nT = sb("nT", [P, KT, T], where=early)
        attn01 = ExitStack()
        w0 = sb("w0", [P, 1664], where=attn01)
        w1 = sb("w1", [P, 2048], where=attn01)
        kbd = sb("kbd", [P, KT, B, 4 * SC], where=attn01)
        vbd = sb("vbd", [P, B * G0, 2, D0 + 1], where=attn01)
        vp0 = sb("vp0", [P, 3, B * G0, 2, D0 + 1], BF16, where=attn01)
        vc1 = sb("vc1", [P, B, H1, D1 + 1], where=attn01)
        vp1 = sb("vp1", [P, 3, B, H1, D1 + 1], BF16, where=attn01)
        mask0 = sb("mask0", [P, NQ, SC], where=attn01)
        maski = sb("maski", [P, B * SC], I32, where=attn01)
        mask1 = sb("mask1", [P, B * SC], where=attn01)
        ones = sb("ones", [P, P], where=attn01)

        l0 = ExitStack()
        q0 = sb("q0", [P, KT, S], where=l0)
        qp0 = [sb(f"qp0_{n}", [P, KT, S], F32R, where=l0) for n in ("high", "low")]
        kp0 = [sb(f"kp0_{n}", [P, KT, 4 * SC], F32R, where=l0) for n in ("high", "low")]
        vb0 = sb("vb0", [P, 3, G0, 2, D0 + 1], BF16, where=l0)
        p0 = [sb(f"p0_{u}", [P, 1024], where=l0) for u in range(4)]
        mx0 = [sb(f"mx0_{u}", [P, H0 // 2], where=l0) for u in range(4)]
        ph0 = [sb(f"ph0_{t}", [P, 8, P], F16, where=l0) for t in range(2)]
        pl0 = [sb(f"pl0_{t}", [P, 8, P], F16, where=l0) for t in range(2)]
        ri0 = sb("ri0", [P, H0], where=l0)
        ao0 = sb("ao0", [P, D], where=l0)
        aoT0 = sb("aoT0", [P, KT, P], where=l0)
        xb0 = [sb(f"xb0_{t}", [P, D], where=l0) for t in range(2)]
        y0 = sb("y0", [P, D], where=l0)
        st0 = sb("st0", [P, 6], where=l0)
        mv0 = [sb(f"mv0_{t}", [P, 4], where=l0) for t in range(2)]
        xn0 = [sb(f"xn0_{t}", [P, D], where=l0) for t in range(2)]
        xg0 = sb("xg0", [P, D], where=l0)
        l0.close()

        l1 = ExitStack()
        xb1T = sb("xb1T", [P, KT, S], where=l1)
        q1 = sb("q1", [P, KT, S], where=l1)
        qp1 = [sb(f"qp1_{n}", [P, KT, 2, S], F32R, where=l1) for n in ("high", "low")]
        kp1 = [sb(f"kp1_{n}", [P, KT, SC + KEYS1], F32R, where=l1) for n in ("high", "low")]
        v1 = sb("v1", [P, 3, QT_B, H1, D1 + 1], BF16, where=l1)
        vb1 = sb("vb1", [P, 3, H1, D1 + 1], BF16, where=l1)
        vr1 = sb("vr1", [P, QT_B, H1, D1], where=l1)
        nm1 = sb("nm1", [P, 16, 2], where=l1)
        p1 = [sb(f"p1_{t}", [P, 2 * KEYS1], where=l1) for t in range(2)]
        ph1 = [sb(f"ph1_{t}", [P, 5, P], F16, where=l1) for t in range(2)]
        pl1 = [sb(f"pl1_{t}", [P, 5, P], F16, where=l1) for t in range(2)]
        ri1 = sb("ri1", [P, H1], where=l1)
        ao1 = sb("ao1", [P, D], where=l1)
        aoT1 = sb("aoT1", [P, KT, P], where=l1)
        xb1 = [sb(f"xb1_{t}", [P, D], where=l1) for t in range(2)]
        y1 = [sb(f"y1_{t}", [P, D], where=l1) for t in range(2)]
        sq1 = sb("sq1", [P, D], where=l1)
        ms1 = [sb(f"ms1_{t}", [P, 4], where=l1) for t in range(2)]
        n1 = sb("n1", [P, D], where=l1)
        l1.close()
        attn01.close()

        mlp1 = ExitStack()
        m1 = dict(wa=sb("m1a", [P, KT, F], where=mlp1), wb=sb("m1b", [P, FT, D], where=mlp1),
                  h=sb("hid1", [P, FT, CH], where=mlp1), xb=[sb(f"xbm1_{t}", [P, D], where=mlp1) for t in range(2)])
        mlp1.close()
        early.close()

        l2 = ExitStack()
        k2 = sb("k2", [P, KT, B, SC], where=l2)
        v2 = sb("v2", [SC, B, D], where=l2)
        t2 = sb("t2", [P, 2, KT, C], where=l2)
        x2 = [sb(f"x2_{t}", [P, D], where=l2) for t in range(2)]
        x2T = [sb(f"x2T{t}", [P, KT, P], where=l2) for t in range(2)]
        p2 = [sb(f"p2_{t}", [P, SC], where=l2) for t in range(2)]
        pT2 = [sb(f"pT2_{t}", [SC, P], where=l2) for t in range(2)]
        sm2 = [sb(f"sm2_{t}", [P, 4], where=l2) for t in range(2)]
        l2.close()
        upto2.close()

        late = ExitStack()
        g3 = sb("g3", [P, KT, B, KEYS3], where=late)
        v3 = sb("v3", [P, B, HP, D], where=late)
        gb3 = sb("gb3", [P, KT, H3], where=late)
        vb3 = sb("vb3", [H3, D], where=late)
        bt3 = sb("bt3", [1, B, KEYS3], where=late)
        bb3 = sb("bb3", [1, H3], where=late)
        one3 = sb("one3", [1, P], where=late)
        prep = ExitStack()
        bun = [sb(f"bun{t}", [P, BUN], where=prep) for t in range(2)]
        kh = sb("kh", [P, C], where=prep)
        vh = sb("vh", [P, C], where=prep)
        prep.close()
        at3 = ExitStack()
        hn = [sb(f"hn{t}", [P, D], where=at3) for t in range(2)]
        hT = [sb(f"hT_{t}", [P, KT, P], where=at3) for t in range(2)]
        st3 = sb("st3", [P, 6], where=at3)
        mv3 = [sb(f"mv3_{t}", [P, 4], where=at3) for t in range(2)]
        mx3 = [sb(f"mx3_{t}", [P, H3], where=at3) for t in range(2)]
        sm3 = [sb(f"sm3_{t}", [P, H3], where=at3) for t in range(2)]
        p3 = [sb(f"p3_{t}", [P, KEYS3 + H3], where=at3) for t in range(2)]
        pT3 = [sb(f"pT3_{t}", [P, 4, P], where=at3) for t in range(2)]
        pb3 = sb("pb3", [H3, P], where=at3)
        xb3 = [sb(f"xb3_{t}", [P, D], where=at3) for t in range(2)]
        at3.close()
        late.close()

        fin = ExitStack()
        m3 = dict(wa=sb("m3a", [P, KT, F], where=fin), wb=sb("m3b", [P, FT, D], where=fin),
                  h=sb("hid3", [P, FT, CH], where=fin), xb=[sb(f"xbm3_{t}", [P, D], where=fin) for t in range(2)])
        xc3 = sb("xc3", [P, KT, CH], where=fin)
        hnm = [sb(f"hnm{t}", [P, D], where=fin) for t in range(2)]
        stm = sb("stm", [P, 6], where=fin)
        mvm = [sb(f"mvm{t}", [P, 4], where=fin) for t in range(2)]
        fin.close()

        dma_x, dma_xT, dma_c, dma_w0, dma_w1, dma_w2, dma_m, dma_k, dma_m1, dma_m3 = [
            sem(f"loaded_{n}") for n in ("x", "xT", "ctx", "w0", "w1", "w2", "masks", "consts", "mlp1", "mlp3")]
        dma_bun = [[sem(f"loaded_heads{a}_{t}") for t in range(2)] for a in range(2)]
        dma_out = sem("stored_out")

        ppe = Steps(sem, "prep_pe", ["k0", "v0", "v1"])
        pdv = Steps(sem, "prep_dve", ["ones", "k0", "v0", "v1", "m1"])
        ppo = Steps(sem, "prep_pool", ["ones"])

        def tallies(stage, owned, **per):
            return {k: Tally(sem, f"{stage}_{k}", n, owned) for k, n in per.items()}

        own_pe, own_act, own_dve, own_pool = [], [], [], []
        E0 = tallies("l0_pe", own_pe, q=1, scores=4, turned_a=4, turned_b=4, heads=4, heads_turned=2, projected=2, normed_turned=2)
        A0 = tallies("l0_act", own_act, weights=4, high=4, heads_turned=2, normed_turned=2)
        D0t = tallies("l0_dve", own_dve, q=1, q_high=1, q_low=1, masked=4, maxima=4, low=4, inverse=2, heads=2, sums=2, stats=2,
                      mean=2, eps=2, normed=2)
        split0 = Tally(sem, "l0_values_split", 4, own_dve)
        G0s = tallies("l0_pool", own_pool, k_high=1, k_low=1, values=1, shifted=4, root=2, scaled=2, rows=2, bias=2)
        E1 = tallies("l1_pe", own_pe, q=1, k=1, v=1, scores=16, turned=16, turned_ctx=16, heads=16, heads_turned=2,
                     projected=2, normed_turned=2)
        A1 = tallies("l1_act", own_act, k_high=1, v_high=1, weights=16, high=16, heads_turned=2, normed_turned=2)
        D1t = tallies("l1_dve", own_dve, q=1, q_high=1, q_low=1, k_low=1, v_rest=1, masked=16, maxima=16, low=16, inverse=2, heads=2, sums=2,
                      squares=2, mean=2, normed=2, ctx_split=4)
        G1 = tallies("l1_pool", own_pool, x=1, v_ctx=1, v_mid=1, v_low=1, bias=2, root=2)

        hs, os_ = [f"h{f}" for f in range(FT)], [f"o{t}" for t in range(QC)]
        em = [Steps(sem, "mlp1_pe", hs + os_), Steps(sem, "mlp3_pe", [f"x{t}" for t in range(QC)] + hs + os_)]
        am = [Steps(sem, "mlp1_act", hs), Steps(sem, "mlp3_act", [f"x{t}" for t in range(QC)] + hs)]
        ln4 = [n % t for t in range(QC) for n in ("bn%d", "mv%d", "eps%d", "xn%d")]
        dm = [Steps(sem, "mlp1_dve", os_), Steps(sem, "mlp3_dve", ln4 + os_)]
        gm = [Steps(sem, "mlp1_pool", [f"xb{t}" for t in range(QC)]),
              Steps(sem, "mlp3_pool", [f"rs{t}" for t in range(QC)] + [f"xb{t}" for t in range(QC)])]

        pe2p = Steps(sem, "l2_prep_pe", ["k", "kq", "v", "vo"])
        dv2p = Steps(sem, "l2_prep_dve", ["k", "kq", "v", "vo"])
        two = lambda *names: [n % t for n in names for t in range(2)]
        e2 = Steps(sem, "l2_pe", two("xt%d", "s%d", "pt%d", "o%d"))
        a2 = Steps(sem, "l2_act", two("xt%d", "exp%d", "pt%d"))
        d2 = Steps(sem, "l2_dve", [n % t for t in range(2) for n in ("m%d", "max%d")]
                   + [n % t for t in range(2) for n in ("s%d", "sum%d")] + two("y%d"))
        vbz = [sem(f"bias_values_zero{a}") for a in range(2)]
        g2 = Steps(sem, "l2_pool", two("x%d"))

        ep = [Steps(sem, f"heads{a}_pe", [n % t for t in range(2) for n in ("k%d", "g%d", "b%d", "v%d", "w%d", "r%d")])
              for a in range(2)]
        dp = [Steps(sem, f"heads{a}_dve", [n % t for t in range(2) for n in ("k%d", "w%d", "m%d", "vb%d")])
              for a in range(2)]
        ap_ = [Steps(sem, f"heads{a}_act", [n % t for t in range(2) for n in ("g%d", "b%d", "v%d", "w%d")])
               for a in range(2)]

        E3 = tallies("attn_pe", own_pe, normed=2, scores=2, turned_a=2, turned_b=2, turned_bias=2, out=2)
        D3t = tallies("attn_dve", own_dve, stats=2, mean=2, eps=2, normed=2, max=2, max_bias=2, shifted=2, shifted_bias=2,
                      sum=2, sum_bias=2, inverse=2, weight_bias=2, rows=2)
        A3 = tallies("attn_act", own_act, normed=2, weights=2, copied_a=2, copied_b=2, copied_bias=2)
        G3 = tallies("attn_pool", own_pool, root=2, bias=2, weights=2)

        def attn_end(t, a):
            return t.end((a + 1) * B)

        def settle(eng):
            eng.nop(nofuse=True)

        x_rows = io["x"].rearrange("b (t p) d -> p (b t) d", p=P)
        out_rows = out.rearrange("b (t p) d -> p (b t) d", p=P)

        block = ctx.enter_context(nc.Block())

        def tail0(slot, first, after):
            if slot % 2 == 0:
                of = dict(sums=slot // 2 - 2, heads=slot // 2 - 1)
            else:
                of = dict(turned=slot // 2 - 2, projected=slot // 2 - 1)
            return {step: k for step, k in of.items() if not (first and k < 0) and not (after and k >= 0)}

        def unit1(u):
            v = u % 8
            return u // 8, v // 4, (v // 2) % 2, v % 2

        def head1(u, e):
            _, kt, par, jp = unit1(u)
            return 8 * kt + 2 * (2 * jp + e) + par

        @block.sync
        def _(sp):
            sp.dma_start(cT[:, :, :], io["ctxT"]).then_inc(dma_c, 16)
            sp.dma_start(w0[:, :], io["w0"]).then_inc(dma_w0, 16)
            sp.dma_start(cst[:, :], io["const"]).then_inc(dma_k, 16)
            sp.dma_start(vec[:, :], io["vecs"]).then_inc(dma_k, 16)
            sp.dma_start(alpha[:, :], io["alpha"].partition_broadcast(P)).then_inc(dma_k, 16)
            sp.dma_start(xT[:, :, :], io["xT"]).then_inc(dma_xT, 16)
            sp.dma_start(row1[:, :, :], io["rows"][0:len(ROWS) - 3, :].partition_broadcast(P)).then_inc(dma_k, 16)
            sp.dma_start(row3[:, :, :], io["rows"][len(ROWS) - 3:, :].partition_broadcast(P)).then_inc(dma_k, 16)
            sp.dma_start(xr[:, :, :], x_rows).then_inc(dma_x, 16)
            sp.dma_start(mask0[:, :, :], io["mask0"].rearrange("b o (t p) k -> p (b o t) k", p=P)).then_inc(dma_m, 16)
            sp.dma_start(maski[:, :], io["mask1"].partition_broadcast(P)).then_inc(dma_m, 16)
            sp.dma_start(w1[:, :], io["w1"]).then_inc(dma_w1, 16)
            sp.dma_start(w2[:, :], io["w2"]).then_inc(dma_w2, 16)
            if stop >= 2:
                sp.wait_ge(E1["normed_turned"].sem, E1["normed_turned"].end(B))
                sp.wait_ge(A1["normed_turned"].sem, A1["normed_turned"].end(B))
                sp.dma_start(m1["wa"][:, :, :], io["m1a"]).then_inc(dma_m1, 16)
                sp.dma_start(m1["wb"][:, :, :], io["m1b"]).then_inc(dma_m1, 16)
            for a in range(2):
                if stop >= 4 + 2 * a:
                    if a == 0:
                        sp.wait_ge(d2.sem, d2.end(B))
                        sp.wait_ge(e2.sem, e2.end(B))
                    else:
                        sp.wait_ge(D3t["rows"].sem, attn_end(D3t["rows"], 0))
                    with sp.Fori(0, HP) as i:
                        for t in range(2):
                            sp.wait_ge(ep[a].sem, ep[a].prev(i, f"r{t}"))
                            settle(sp)
                            sp.wait_ge(ap_[a].sem, ap_[a].prev(i, f"v{t}"))
                            settle(sp)
                            sp.dma_start(bun[t][:, :], io[f"heads{a}"][bass.ds(2 * i + t, 1), :, :].rearrange(
                                "o p n -> p (o n)")).then_inc(dma_bun[a][t], 16)
            if stop >= 8:
                sp.wait_ge(D3t["rows"].sem, attn_end(D3t["rows"], 1))
                sp.dma_start(m3["wa"][:, :, :], io["m3a"]).then_inc(dma_m3, 16)
                sp.dma_start(m3["wb"][:, :, :], io["m3b"]).then_inc(dma_m3, 16)
            last = [(G0s["rows"], B), (D1t["normed"], B), (dm[0], NCH), (d2, B), (d2, B), (D3t["rows"], B), (D3t["rows"], B), (D3t["rows"], 2 * B), (dm[1], NCH)][min(stop, 8)]
            sp.wait_ge(last[0].sem, last[0].end(last[1]))
            sp.dma_start(out_rows, xr[:, :, :]).then_inc(dma_out, 16)
            sp.wait_ge(dma_out, 16)

        @block.tensor
        def _(pe):
            mm, tr = nc.tensor.matmul, nc.tensor.transpose
            for s in [ppe, pe2p, e2] + em + ep:
                pe.sem_inc(s.sem, s.per)
            for s in own_pe:
                pe.sem_inc(s.sem, s.seed)

            pe.wait_ge(dma_c, 16)
            pe.wait_ge(dma_w0, 16)
            for mt in range(KT):
                for kt in range(KT):
                    last = mm(ps[:, mt, :], wt(w0, W0, "wk")[:, kt, mt * P:(mt + 1) * P], cT[:, kt, :],
                              start=kt == 0, stop=kt == KT - 1)
            last.then_inc(ppe.sem, ppe.did("k0"))
            for b in range(B):
                for hf in range(2):
                    for kt in range(KT):
                        last = mm(ps[HALF * hf:HALF * (hf + 1), 2, b * SC:(b + 1) * SC],
                                  cT[:, kt, b * SC:(b + 1) * SC], wt(w0, W0, "wv")[:, kt, :],
                                  start=kt == 0, stop=kt == KT - 1)
            last.then_inc(ppe.sem, ppe.did("v0"))
            pe.wait_ge(dma_w1, 16)
            for b in range(B):
                for hf in range(2):
                    for kt in range(KT):
                        last = mm(ps[HALF * hf:HALF * (hf + 1), 3 + b // 2, (b % 2) * D:(b % 2 + 1) * D],
                                  cT[:, kt, b * SC:(b + 1) * SC], wt(w1, W1, "wv")[:, kt, :],
                                  start=kt == 0, stop=kt == KT - 1)
            last.then_inc(ppe.sem, ppe.did("v1"))
            pe.wait_ge(pdv.sem, pdv.now(0, "v1"))
            pe.wait_ge(dma_k, 80)
            pe.wait_ge(dma_xT, 16)

            def wait(t, i, k=0):
                pe.wait_ge(t.sem, t.at(i, k))

            def queries0(i):
                for mt in range(KT):
                    for kt in range(KT):
                        last = mm(ps[:, 7, mt * S:(mt + 1) * S], wt(w0, W0, "wq")[:, kt, mt * P:(mt + 1) * P],
                                  xT[:, kt, bass.ds(i * S, S)], start=kt == 0, stop=kt == KT - 1)
                last.then_inc(E0["q"].sem, 1)

            def scores0(i, u):
                t, hf = u // 2, u % 2
                if u == 0:
                    wait(D0t["q_low"], i)
                    wait(G0s["k_low"], i)
                wait(D0t["masked"], i, u - 2)
                for kt in range(KT):
                    for j in (2 * hf, 2 * hf + 1):
                        for n, (a, b) in enumerate(PARTS):
                            last = mm(ps[:, j, kt * 256:(kt + 1) * 256], qp0[a][32 * j:32 * j + 32, kt, t * P:(t + 1) * P],
                                      kp0[b][32 * j:32 * j + 32, kt, :], start=n == 0, stop=n == 2)
                last.then_inc(E0["scores"].sem, 1)

            def turn0(i, u):
                wait(A0["weights"], i, u)
                wait(D0t["low"], i, u - 1)
                for half, name in ((0, "a"), (1, "b")):
                    for n in range(4):
                        blk = 4 * half + n
                        last = tr(ps[:, 4 + half, n * P:(n + 1) * P], p0[u][:, blk * P:(blk + 1) * P], ident)
                    last.then_inc(E0[f"turned_{name}"].sem, 1)

            def heads0(i, k):
                if k % 2 == 0:
                    wait(D0t["heads"], i, k // 2 - 1)
                if k == 0:
                    wait(G0s["values"], i)
                wait(D0t["low"], i, k)
                for n in range(8):
                    blk = 8 * (k % 2) + n
                    g = 4 * ((blk // 2) % 2) + blk // 4
                    for w, parts in ((ph0, 3), (pl0, 2)):
                        for c in range(parts):
                            last = mm(ps[:, 6, blk * 18:blk * 18 + 18], w[k % 2][:, n, :], vb0[:, c, g, :, :],
                                      start=w is ph0 and c == 0, stop=w is pl0 and c == 1)
                last.then_inc(E0["heads"].sem, 1)

            def turn_rows0(t, i, k, rows, ready, before):
                wait(ready, i, k)
                if before:
                    wait(before, i, k - 1)
                for kt in range(KT):
                    last = tr(ps[:, 7, kt * P:(kt + 1) * P], rows[:, kt * P:(kt + 1) * P], ident)
                last.then_inc(t.sem, 1)

            def slot0(i, u, first=False, final=False, after=False):
                k = tail0(u, first, after)
                if not after:
                    turn0(i, u)
                if "turned" in k:
                    if u == 1 and not (final or after):
                        wait(D0t["q"], i + 1)
                    turn_rows0(E0["normed_turned"], i, k["turned"], xn0[k["turned"] % 2], D0t["normed"], None)
                if not (first and u == 0) and not (after and u):
                    heads0(i, u - 1)
                if "projected" in k:
                    turn_rows0(E0["heads_turned"], i, k["projected"], ao0, D0t["heads"], A0["normed_turned"])
                if not after and not (final and u >= 1):
                    scores0(i + (u >= 1), (u + 3) % 4)
                if "projected" in k:
                    wait(A0["heads_turned"], i, k["projected"])
                    for kt in range(KT):
                        last = mm(ps[:, 7, 0:D], aoT0[:, kt, :], wt(w0, W0, "wo")[:, kt, :], start=kt == 0, stop=kt == KT - 1)
                    last.then_inc(E0["projected"].sem, 1)
                if u == 0 and not (final or after):
                    if not first:
                        wait(D0t["sums"], i, -2)
                    queries0(i + 1)

            queries0(0)
            scores0(0, 0)
            scores0(0, 1)
            scores0(0, 2)
            for u in range(4):
                slot0(0, u, first=True)
            with pe.Fori(1, B - 1) as i:
                for u in range(4):
                    slot0(i, u)
            for u in range(4):
                slot0(B - 1, u, final=True)
            for u in range(4):
                slot0(B, u, after=True)

            def keys1(i):
                wait(G1["x"], i)
                wait(A1["weights"], i, -2)
                for mt in range(KT):
                    lhs = wt(w1, W1, "wk")
                    for lo, hi, rhs in ((0, SC, None), (SC, SC + S, xb1T), (SC + S, SC + S + SC, None)):
                        for kt in range(KT):
                            r = rhs[:, kt, :] if rhs is not None else cT[:, kt, bass.ds(i * SC, SC)]
                            last = mm(ps[:, mt, lo:hi], lhs[:, kt, mt * P:(mt + 1) * P], r,
                                      start=kt == 0, stop=kt == KT - 1)
                last.then_inc(E1["k"].sem, 1)

            def queries_values1(i):
                wait(A1["weights"], i, -1)
                for mt in range(KT):
                    for kt in range(KT):
                        last = mm(ps[:, 2, mt * S:(mt + 1) * S], wt(w1, W1, "wq")[:, kt, mt * P:(mt + 1) * P],
                                  xb1T[:, kt, :], start=kt == 0, stop=kt == KT - 1)
                last.then_inc(E1["q"].sem, 1)
                for t in range(QT_B):
                    for kt in range(KT):
                        last = mm(ps[:, 3, t * D:(t + 1) * D], xb1T[:, kt, t * P:(t + 1) * P],
                                  wt(w1, W1, "wv")[:, kt, :], start=kt == 0, stop=kt == KT - 1)
                last.then_inc(E1["v"].sem, 1)

            def scores1(i, u):
                t, kt, par, jp = unit1(u)
                if u == 0:
                    wait(D1t["k_low"], i)
                    wait(D1t["q_low"], i)
                elif u == 1:
                    wait(A1["v_high"], i)
                    wait(D1t["v_rest"], i)
                else:
                    wait(A1["weights"], i, u - 2)
                for e in range(2):
                    r = 32 * (2 * jp + e)
                    first = 0 if e else SC
                    for n, (a, b) in enumerate(PARTS):
                        last = mm(ps[:, 2 * (u % 2) + e, 0:KEYS1], qp1[a][r:r + 32, kt, par, t * P:(t + 1) * P],
                                  kp1[b][r:r + 32, kt, first:first + KEYS1], start=n == 0, stop=n == 2)
                last.then_inc(E1["scores"].sem, 1)

            def bank6(i, u, tails):
                if tails:
                    wait(*tails)
                else:
                    wait(D1t["low"], i, u)

            def turn1(i, u):
                wait(A1["weights"], i, u)
                wait(D1t["low"], i, u - 2)
                for k, blk in enumerate((0, 1, 3, 4)):
                    last = tr(ps[:, 4 + u % 2, k * P:(k + 1) * P], p1[u % 2][:, blk * P:(blk + 1) * P], ident)
                last.then_inc(E1["turned"].sem, 1)

            def turn_ctx1(i, u, last_tail):
                bank6(i, u - 1, last_tail)
                tr(ps[:, 6, 0:P], p1[u % 2][:, 2 * P:3 * P], ident).then_inc(E1["turned_ctx"].sem, 1)

            def heads1(i, u):
                if u == 0:
                    wait(D1t["heads"], i, -1)
                    wait(G1["v_low"], i)
                if u == 8:
                    wait(D1t["heads"], i, 0)
                wait(D1t["low"], i, u)
                for e in range(2):
                    h = head1(u, e)
                    o = ps[:, 7, h * (D1 + 1):(h + 1) * (D1 + 1)]
                    for blk in range(3):
                        k = 4 if blk == 2 else 2 * e + blk
                        for w, parts in ((ph1, 3), (pl1, 2)):
                            for c in range(parts):
                                val = vb1[:, c, h, :] if blk == 2 else v1[:, c, blk, h, :]
                                last = mm(o, w[u % 2][:, k, :], val, start=blk == 0 and w is ph1 and c == 0,
                                          stop=blk == 2 and w is pl1 and c == 1)
                last.then_inc(E1["heads"].sem, 1)

            def turn_heads1(i, k, u):
                wait(D1t["heads"], i, k)
                wait(D1t["low"], i, u)
                for kt in range(KT):
                    last = tr(ps[:, 6, kt * P:(kt + 1) * P], ao1[:, kt * P:(kt + 1) * P], ident)
                last.then_inc(E1["heads_turned"].sem, 1)

            def project1(i, k, u):
                wait(A1["heads_turned"], i, k)
                wait(D1t["low"], i, u)
                for kt in range(KT):
                    last = mm(ps[:, 6, 0:D], aoT1[:, kt, :], wt(w1, W1, "wo")[:, kt, :], start=kt == 0, stop=kt == KT - 1)
                last.then_inc(E1["projected"].sem, 1)

            def turn_normed1(i, k, u):
                wait(D1t["normed"], i, k)
                wait(D1t["low"], i, u)
                for kt in range(KT):
                    last = tr(ps[:, 6, kt * P:(kt + 1) * P], n1[:, kt * P:(kt + 1) * P], ident)
                last.then_inc(E1["normed_turned"].sem, 1)

            def batch1(i, first=False, final=False):
                for u in range(16):
                    turn1(i, u)
                    if u + 2 < 16:
                        scores1(i, u + 2)
                    elif not final:
                        if u == 14:
                            keys1(i + 1)
                        else:
                            queries_values1(i + 1)
                    tail = None
                    for at, k in ((1, -1), (9, 0)):
                        if first and k < 0:
                            continue
                        if u == at:
                            turn_heads1(i, k, u - 1)
                            tail = (A1["heads_turned"], i, k)
                        if u == at + 1:
                            project1(i, k, u - 1)
                            tail = (D1t["sums"], i, k)
                        if u == at + 3:
                            turn_normed1(i, k, u - 1)
                            tail = (A1["normed_turned"], i, k)
                    turn_ctx1(i, u, tail)
                    if u:
                        heads1(i, u - 1)
                heads1(i, 15)
                if not final:
                    scores1(i + 1, 0)
                    scores1(i + 1, 1)

            if stop >= 1:
                pe.wait_ge(A0["normed_turned"].sem, A0["normed_turned"].end(B))
                pe.wait_ge(D0t["normed"].sem, D0t["normed"].end(B))
                pe.wait_ge(D1t["ctx_split"].sem, D1t["ctx_split"].at(0, 3))
                keys1(0)
                queries_values1(0)
                scores1(0, 0)
                scores1(0, 1)
                batch1(0, first=True)
                with pe.Fori(1, B - 1) as i:
                    batch1(i)
                batch1(B - 1, final=True)
                turn_heads1(B, -1, -1)
                wait(A1["heads_turned"], B, -1)
                project1(B, -1, -1)
                wait(D1t["sums"], B, -1)
                turn_normed1(B, -1, -1)

            def mlp_products(m, w, loaded, cols):
                pe.wait_ge(loaded, 32)
                with pe.Fori(0, NCH) as i:
                    if m:
                        for t in range(QC):
                            pe.wait_ge(dm[1].sem, dm[1].now(i, f"xn{t}"))
                            pe.wait_ge(am[1].sem, am[1].now(i, f"x{t - 2}") if t >= 2 else am[1].prev(i, f"x{t + 2}"))
                            for kt in range(KT):
                                last = tr(ps[:, 4 + t % 2, kt * P:(kt + 1) * P], hnm[t % 2][:, kt * P:(kt + 1) * P], ident)
                            last.then_inc(em[1].sem, em[1].did(f"x{t}"))
                        pe.wait_ge(am[1].sem, am[1].now(i, f"x{QC - 1}"))
                    for ft in range(FT):
                        pe.wait_ge(am[m].sem, am[m].now(i, f"h{ft - 2}") if ft >= 2 else am[m].prev(i, f"h{ft + 6}"))
                        for kt in range(KT):
                            last = mm(ps[:, ft % 2, :], w["wa"][:, kt, ft * P:(ft + 1) * P], cols(i, kt),
                                      start=kt == 0, stop=kt == KT - 1)
                        last.then_inc(em[m].sem, em[m].did(f"h{ft}"))
                    for t in range(QC):
                        pe.wait_ge(am[m].sem, am[m].now(i, f"h{FT - 1}"))
                        pe.wait_ge(dm[m].sem, dm[m].now(i, f"o{t - 2}") if t >= 2 else dm[m].prev(i, f"o{t + 2}"))
                        for ft in range(FT):
                            last = mm(ps[:, 2 + t % 2, 0:D], w["h"][:, ft, t * P:(t + 1) * P], w["wb"][:, ft, :],
                                      start=ft == 0, stop=ft == FT - 1)
                        last.then_inc(em[m].sem, em[m].did(f"o{t}"))

            if stop >= 2:
                pe.wait_ge(A1["normed_turned"].sem, A1["normed_turned"].end(B))
                pe.wait_ge(D1t["normed"].sem, D1t["normed"].end(B))
                mlp_products(0, m1, dma_m1, lambda i, kt: nT[:, kt, bass.ds(i * CH, CH)])

            if stop >= 3:
                pe.wait_ge(dma_w2, 16)
                pe.wait_ge(dm[0].sem, dm[0].end(NCH))
                pe.wait_ge(am[0].sem, am[0].end(NCH))
                for k, name in ((0, "wkT"), (1, "wvT")):
                    for mt in range(KT):
                        for kt in range(KT):
                            last = mm(ps[:, 2 * k + mt, :], wt(w2, W2, name)[:, kt, mt * P:(mt + 1) * P], cT[:, kt, :],
                                      start=kt == 0, stop=kt == KT - 1)
                    if k == 0:
                        last.then_inc(pe2p.sem, pe2p.did("k"))
                        pe.wait_ge(dv2p.sem, dv2p.now(0, "k"))
                        for mt in range(KT):
                            for kt in range(KT):
                                last = mm(ps[:, 4 + mt, :], wt(w2, W2, "wq")[:, kt, mt * P:(mt + 1) * P], t2[:, 0, kt, :],
                                          start=kt == 0, stop=kt == KT - 1)
                        last.then_inc(pe2p.sem, pe2p.did("kq"))
                last.then_inc(pe2p.sem, pe2p.did("v"))
                pe.wait_ge(dv2p.sem, dv2p.now(0, "v"))
                for b in range(B):
                    for kt in range(KT):
                        last = mm(ps[0:SC, 4 + b // 2, (b % 2) * D:(b % 2 + 1) * D], t2[:, 1, kt, b * SC:(b + 1) * SC],
                                  wt(w2, W2, "woT")[:, kt, :], start=kt == 0, stop=kt == KT - 1)
                last.then_inc(pe2p.sem, pe2p.did("vo"))
                pe.wait_ge(dv2p.sem, dv2p.now(0, "vo"))
                with pe.Fori(0, B) as i:
                    for t in range(2):
                        pe.wait_ge(g2.sem, g2.now(i, f"x{t}"))
                        pe.wait_ge(a2.sem, a2.prev(i, f"xt{t}"))
                        for kt in range(KT):
                            last = tr(ps[:, t, kt * P:(kt + 1) * P], x2[t][:, kt * P:(kt + 1) * P], ident)
                        last.then_inc(e2.sem, e2.did(f"xt{t}"))
                    for t in range(2):
                        pe.wait_ge(a2.sem, a2.now(i, f"xt{t}"))
                        pe.wait_ge(a2.sem, a2.prev(i, f"exp{t}"))
                        for kt in range(KT):
                            last = mm(ps[:, 2 + t, 0:SC], x2T[t][:, kt, :], k2[:, kt, bass.ds(i, 1), :],
                                      start=kt == 0, stop=kt == KT - 1)
                        last.then_inc(e2.sem, e2.did(f"s{t}"))
                    for t in range(2):
                        pe.wait_ge(a2.sem, a2.now(i, f"exp{t}"))
                        pe.wait_ge(a2.sem, a2.prev(i, f"pt{t}"))
                        settle(pe)
                        tr(ps[0:SC, 4 + t, 0:P], p2[t][:, :], ident).then_inc(e2.sem, e2.did(f"pt{t}"))
                    for t in range(2):
                        pe.wait_ge(a2.sem, a2.now(i, f"pt{t}"))
                        pe.wait_ge(d2.sem, d2.prev(i, f"y{t}"))
                        settle(pe)
                        mm(ps[:, 6 + t, 0:D], pT2[t][:, :], v2[:, bass.ds(i, 1), :], start=True,
                           stop=True).then_inc(e2.sem, e2.did(f"o{t}"))

            def head_products(a):
                with pe.Fori(0, HP) as i:
                    for t in range(2):
                        w = bun[t]
                        wk = w[:, 0:D].rearrange("p (k n) -> p k n", k=KT)
                        wqT, wo = w[:, D:2 * D], w[:, 3 * D:4 * D]
                        wv = w[:, 2 * D:3 * D].rearrange("p (k n) -> p k n", k=KT)
                        bq, bias_k, bias_v = w[:, 4 * D + 1:4 * D + 2], w[:, 4 * D + 3:4 * D + 4], w[:, 4 * D + 4:BUN]
                        older = lambda s, n: s.now(i, n + "0") if t else s.prev(i, n + "1")
                        pe.wait_ge(dma_bun[a][t], 16 * i + 16)
                        pe.wait_ge(dp[a].sem, older(dp[a], "k"))
                        for kt in range(KT):
                            last = mm(ps[:, 0, :], wk[:, kt, :], cT[:, kt, :], start=kt == 0, stop=kt == KT - 1)
                        last.then_inc(ep[a].sem, ep[a].did(f"k{t}"))
                        pe.wait_ge(dp[a].sem, dp[a].now(i, f"k{t}"))
                        pe.wait_ge(ap_[a].sem, older(ap_[a], "g"))
                        for mt in range(KT):
                            last = mm(ps[:, 1 + mt, :], wqT[:, mt * P:(mt + 1) * P], kh[:, :], start=True, stop=True)
                        last.then_inc(ep[a].sem, ep[a].did(f"g{t}"))
                        pe.wait_ge(ap_[a].sem, older(ap_[a], "b"))
                        mm(ps[0:1, 3, :], bq, kh[:, :], start=True, stop=True).then_inc(ep[a].sem, ep[a].did(f"b{t}"))
                        pe.wait_ge(ap_[a].sem, older(ap_[a], "v"))
                        for kt in range(KT):
                            last = mm(ps[:, 4, :], wv[:, kt, :], cT[:, kt, :], start=kt == 0, stop=kt == KT - 1)
                        last.then_inc(ep[a].sem, ep[a].did(f"v{t}"))
                        pe.wait_ge(ap_[a].sem, ap_[a].now(i, f"v{t}"))
                        pe.wait_ge(ap_[a].sem, older(ap_[a], "w"))
                        pe.wait_ge(dp[a].sem, older(dp[a], "w"))
                        for bp in range(4):
                            last = mm(ps[:, 5 + bp // 2, (bp % 2) * D:(bp % 2 + 1) * D], vh[:, bp * P:(bp + 1) * P], wo,
                                      start=True, stop=True)
                        last.then_inc(ep[a].sem, ep[a].did(f"w{t}"))
                        pe.wait_ge(dp[a].sem, older(dp[a], "vb"))
                        mm(ps[0:H3, 7, 0:D], bias_v, wo, start=True, stop=True)
                        for mt in range(KT):
                            mm(ps[:, 7, D + mt:D + mt + 1], wqT[:, mt * P:(mt + 1) * P], bias_k, start=True, stop=True)
                        mm(ps[0:1, 7, D + 4:D + 5], bq, bias_k, start=True, stop=True).then_inc(ep[a].sem, ep[a].did(f"r{t}"))

            def attend(a):
                def wait(t, i, k):
                    pe.wait_ge(t.sem, t.at(i, k + a * B * t.per))

                def turn_normed(i, k):
                    wait(D3t["normed"], i, k)
                    if k >= 2:
                        wait(D3t["shifted_bias"], i, k - 1)
                    elif k == 1:
                        wait(A3["normed"], i, 0)
                    for kt in range(KT):
                        last = tr(ps[:, 6, kt * P:(kt + 1) * P], hn[k % 2][:, kt * P:(kt + 1) * P], ident)
                    last.then_inc(E3["normed"].sem, 1)

                def scores(i, k, ahead=False):
                    t, b = k % 2, i + k // 2
                    wait(A3["normed"], i, 1 if ahead else k)
                    wait(D3t["shifted_bias"], i, k - 1)
                    for kt in range(KT):
                        mm(ps[:, 6, D:D + H3], hT[t][:, kt, :], gb3[:, kt, :], start=kt == 0, stop=False)
                    mm(ps[:, 6, D:D + H3], one3[:, :], bb3[:, :], start=False, stop=True)
                    for c in range(2):
                        for kt in range(KT):
                            mm(ps[:, 2 * t + c, :], hT[t][:, kt, :], g3[:, kt, bass.ds(b, 1), c * 512:(c + 1) * 512],
                               start=kt == 0, stop=False)
                        last = mm(ps[:, 2 * t + c, :], one3[:, :], bt3[:, bass.ds(b, 1), c * 512:(c + 1) * 512],
                                  start=False, stop=True)
                    last.then_inc(E3["scores"].sem, 1)

                def turn(i, k):
                    t = k % 2
                    wait(G3["weights"], i, k)
                    wait(D3t["weight_bias"], i, k)
                    for half, name, copied in ((0, "a", "copied_bias"), (1, "b", "copied_b")):
                        wait(A3[copied], i, k - 1)
                        for n in range(4):
                            blk = 4 * half + n
                            last = tr(ps[:, 4 + half, n * P:(n + 1) * P], p3[t][:, blk * P:(blk + 1) * P], ident)
                        last.then_inc(E3[f"turned_{name}"].sem, 1)
                    wait(A3["copied_a"], i, k)
                    tr(ps[0:H3, 4, 0:P], p3[t][:, KEYS3:KEYS3 + H3], ident).then_inc(E3["turned_bias"].sem, 1)

                def rows_out(i, k, half):
                    o = ps[:, 7, 0:D]
                    if half == 0:
                        wait(D3t["rows"], i, k - 1)
                    wait(A3["copied_" + "ab"[half]], i, k)
                    for n in range(4):
                        mm(o, pT3[half][:, n, :], v3[:, bass.ds(i, 1), 4 * half + n, :], start=half == 0 and n == 0, stop=False)
                    if half:
                        wait(A3["copied_bias"], i, k)
                        mm(o, pb3[:, :], vb3[:, :], start=False, stop=True).then_inc(E3["out"].sem, 1)

                def batch(i, final=False):
                    for k in range(2):
                        if not (final and k):
                            scores(i, k + 1)
                        turn(i, k)
                        rows_out(i, k, 0)
                        if not final:
                            turn_normed(i, k + 2)
                        rows_out(i, k, 1)

                turn_normed(0, 0)
                turn_normed(0, 1)
                scores(0, 0, ahead=True)
                with pe.Fori(0, B - 1) as i:
                    batch(i)
                batch(B - 1, final=True)

            for a in range(2):
                if stop >= 4 + 2 * a:
                    if a == 0:
                        pe.wait_ge(d2.sem, d2.end(B))
                        pe.wait_ge(a2.sem, a2.end(B))
                    else:
                        pe.wait_ge(D3t["rows"].sem, attn_end(D3t["rows"], 0))
                        pe.wait_ge(A3["copied_bias"].sem, attn_end(A3["copied_bias"], 0))
                    head_products(a)
                if stop >= 5 + 2 * a:
                    pe.wait_ge(dp[a].sem, dp[a].end(HP))
                    pe.wait_ge(ap_[a].sem, ap_[a].end(HP))
                    attend(a)
            if stop >= 8:
                pe.wait_ge(D3t["rows"].sem, attn_end(D3t["rows"], 1))
                pe.wait_ge(A3["copied_bias"].sem, attn_end(A3["copied_bias"], 1))
                mlp_products(1, m3, dma_m3, lambda i, kt: xc3[:, kt, :])

        @block.scalar
        def _(act):
            def copy(o, x, bias=0.0, scale=1.0):
                return nc.scalar.activation(o, x, ACT.Identity, bias=bias, scale=scale)

            def exp(o, x, bias=0.0, scale=1.0):
                return nc.scalar.activation(o, x, ACT.Exp, bias=bias, scale=scale)

            for s in [a2] + am + ap_:
                act.sem_inc(s.sem, s.per)
            for s in own_act:
                act.sem_inc(s.sem, s.seed)
            act.wait_ge(dma_k, 80)

            act.wait_ge(dma_xT, 16)

            def wait(t, i, k=0):
                act.wait_ge(t.sem, t.at(i, k))

            def weights0(i, u):
                wait(G0s["shifted"], i, u)
                exp(p0[u][:, :], p0[u][:, :]).then_inc(A0["weights"].sem, 1)

            def slot0(i, u, first=False, final=False, after=False):
                k = tail0(u, first, after)
                if not after:
                    wait(E0["heads"], i, u - 2)
                    for half, name in ((0, "a"), (1, "b")):
                        wait(E0[f"turned_{name}"], i, u)
                        last = copy(ph0[u % 2][:, 4 * half:4 * half + 4, :], ps[:, 4 + half, :].rearrange("p (k n) -> p k n", k=4),
                                    scale=WHOLE)
                    last.then_inc(A0["high"].sem, 1)
                if "turned" in k:
                    c = k["turned"]
                    wait(E0["normed_turned"], i, c)
                    for kt in range(KT):
                        last = copy(xT[:, kt, bass.ds(i * S + c * P, P)], ps[:, 7, kt * P:(kt + 1) * P],
                                    pvec("L0_beta", kt), pvec("L0_gamma", kt))
                    last.then_inc(A0["normed_turned"].sem, 1)
                if "projected" in k:
                    c = k["projected"]
                    wait(E0["heads_turned"], i, c)
                    wait(E0["projected"], i, c - 1)
                    for kt in range(KT):
                        last = copy(aoT0[:, kt, :], ps[:, 7, kt * P:(kt + 1) * P], bias=pvec("L0_bv", kt))
                    last.then_inc(A0["heads_turned"].sem, 1)
                if not after and not (final and u == 3):
                    weights0(i + (u == 3), (u + 1) % 4)

            weights0(0, 0)
            for u in range(4):
                slot0(0, u, first=True)
            with act.Fori(1, B - 1) as i:
                for u in range(4):
                    slot0(i, u)
            for u in range(4):
                slot0(B - 1, u, final=True)
            for u in range(4):
                slot0(B, u, after=True)

            def values_high1(i):
                wait(E1["v"], i)
                wait(E1["heads"], i, -1)
                copy(v1[:, 0, :, :, 0:D1], ps[:, 3, :].rearrange("p (t h d) -> p t h d", t=QT_B, h=H1)
                     ).then_inc(A1["v_high"].sem, 1)

            def keys_high1(i):
                wait(E1["k"], i)
                wait(E1["scores"], i, -1)
                for mt in range(KT):
                    last = copy(kp1[0][:, mt, :], ps[:, mt, 0:SC + KEYS1], bias=pvec("L1_bk", mt))
                last.then_inc(A1["k_high"].sem, 1)

            def weights1(i, u):
                wait(D1t["maxima"], i, u)
                wait(E1["turned_ctx"], i, u - 2)
                for e in range(2):
                    last = exp(p1[u % 2][:, e * KEYS1:(e + 1) * KEYS1], ps[:, 2 * (u % 2) + e, 0:KEYS1],
                               bias=nm1[:, u, e:e + 1])
                last.then_inc(A1["weights"].sem, 1)

            def high1(i, u):
                wait(E1["turned"], i, u)
                wait(E1["heads"], i, u - 2)
                copy(ph1[u % 2][:, 0:4, :], ps[:, 4 + u % 2, :].rearrange("p (k n) -> p k n", k=4), scale=WHOLE)
                wait(E1["turned_ctx"], i, u)
                copy(ph1[u % 2][:, 4, :], ps[:, 6, 0:P], scale=WHOLE).then_inc(A1["high"].sem, 1)

            def heads_turned1(i, k):
                wait(E1["heads_turned"], i, k)
                for kt in range(KT):
                    last = copy(aoT1[:, kt, :], ps[:, 6, kt * P:(kt + 1) * P], bias=pvec("L1_bv", kt))
                last.then_inc(A1["heads_turned"].sem, 1)

            def normed_turned1(i, k):
                wait(E1["normed_turned"], i, k)
                for kt in range(KT):
                    last = copy(nT[:, kt, bass.ds(i * S + k * P, P)], ps[:, 6, kt * P:(kt + 1) * P],
                                scale=pvec("L1_norm", kt))
                last.then_inc(A1["normed_turned"].sem, 1)

            def batch1(i, first=False, final=False):
                weights1(i, 0)
                for u in range(16):
                    for at, k in ((1, -1), (9, 0)):
                        if not (first and k < 0):
                            if u == at:
                                heads_turned1(i, k)
                            if u == at + 3:
                                normed_turned1(i, k)
                    if u + 1 < 16:
                        weights1(i, u + 1)
                    high1(i, u)
                    if u == 14 and not final:
                        keys_high1(i + 1)
                if not final:
                    values_high1(i + 1)

            if stop >= 1:
                act.wait_ge(D0t["normed"].sem, D0t["normed"].end(B))
                act.wait_ge(G0s["rows"].sem, G0s["rows"].end(B))
                act.wait_ge(E0["normed_turned"].sem, E0["normed_turned"].end(B))
                keys_high1(0)
                values_high1(0)
                batch1(0, first=True)
                with act.Fori(1, B - 1) as i:
                    batch1(i)
                batch1(B - 1, final=True)
                heads_turned1(B, -1)
                normed_turned1(B, -1)

            def mlp_gelu(m, w, func):
                with act.Fori(0, NCH) as i:
                    if m:
                        for t in range(QC):
                            act.wait_ge(em[1].sem, em[1].now(i, f"x{t}"))
                            act.wait_ge(em[1].sem, em[1].prev(i, f"h{FT - 1}"))
                            for kt in range(KT):
                                last = copy(xc3[:, kt, t * P:(t + 1) * P], ps[:, 4 + t % 2, kt * P:(kt + 1) * P],
                                            pvec("lnm_o", kt), pvec("lnm_s", kt))
                            last.then_inc(am[1].sem, am[1].did(f"x{t}"))
                    for ft in range(FT):
                        act.wait_ge(em[m].sem, em[m].now(i, f"h{ft}"))
                        nc.scalar.activation(w["h"][:, ft, :], ps[:, ft % 2, :], func, bias=fvec(m, ft)
                                             ).then_inc(am[m].sem, am[m].did(f"h{ft}"))

            if stop >= 2:
                act.wait_ge(E1["normed_turned"].sem, E1["normed_turned"].end(B))
                act.wait_ge(D1t["normed"].sem, D1t["normed"].end(B))
                mlp_gelu(0, m1, ACT.Gelu_apprx_tanh)

            if stop >= 3:
                act.wait_ge(dv2p.sem, dv2p.now(0, "vo"))
                with act.Fori(0, B) as i:
                    for t in range(2):
                        act.wait_ge(e2.sem, e2.now(i, f"xt{t}"))
                        act.wait_ge(e2.sem, e2.prev(i, f"s{t}"))
                        copy(x2T[t][:, :, :], ps[:, t, 0:D].rearrange("p (k n) -> p k n", k=KT)
                             ).then_inc(a2.sem, a2.did(f"xt{t}"))
                    for t in range(2):
                        act.wait_ge(d2.sem, d2.now(i, f"max{t}"))
                        act.wait_ge(d2.sem, d2.prev(i, f"sum{t}"))
                        act.wait_ge(e2.sem, e2.prev(i, f"pt{t}"))
                        exp(p2[t][:, :], ps[:, 2 + t, 0:SC], bias=sm2[t][:, 0:1], scale=SCALE2).then_inc(a2.sem, a2.did(f"exp{t}"))
                    for t in range(2):
                        act.wait_ge(e2.sem, e2.now(i, f"pt{t}"))
                        act.wait_ge(e2.sem, e2.prev(i, f"o{t}"))
                        copy(pT2[t][:, :], ps[0:SC, 4 + t, 0:P]).then_inc(a2.sem, a2.did(f"pt{t}"))

            def head_copies(a):
                with act.Fori(0, HP) as i:
                    for t in range(2):
                        act.wait_ge(dma_bun[a][t], 16 * i + 16)
                        act.wait_ge(ep[a].sem, ep[a].now(i, f"g{t}"))
                        for mt in range(KT):
                            last = copy(g3[:, mt, :, bass.ds(i * 2 * SC + t * SC, SC)],
                                        ps[:, 1 + mt, :].rearrange("p (b k) -> p b k", b=B))
                        last.then_inc(ap_[a].sem, ap_[a].did(f"g{t}"))
                        act.wait_ge(ep[a].sem, ep[a].now(i, f"b{t}"))
                        copy(bt3[:, :, bass.ds(i * 2 * SC + t * SC, SC)],
                             ps[0:1, 3, :].rearrange("p (b k) -> p b k", b=B)).then_inc(ap_[a].sem, ap_[a].did(f"b{t}"))
                        act.wait_ge(ep[a].sem, ep[a].now(i, f"v{t}"))
                        act.wait_ge(ep[a].sem, ep[a].now(i, "w0") if t else ep[a].prev(i, "w1"))
                        copy(vh[:, :], ps[:, 4, :], bias=bun[t][:, 4 * D + 2:4 * D + 3]).then_inc(ap_[a].sem, ap_[a].did(f"v{t}"))
                        act.wait_ge(ep[a].sem, ep[a].now(i, f"w{t}"))
                        copy(v3[HALF * t:HALF * (t + 1), 0:B:2, bass.ds(i, 1), :].rearrange("p b o n -> p b (o n)"),
                             ps[0:HALF, 5:7, :].rearrange("p k (c n) -> p (k c) n", c=2)).then_inc(ap_[a].sem, ap_[a].did(f"w{t}"))

            def attend(a):
                def wait(t, i, k):
                    act.wait_ge(t.sem, t.at(i, k + a * B * t.per))

                def normed(i, k):
                    wait(E3["normed"], i, k)
                    wait(E3["scores"], i, k - 2)
                    for kt in range(KT):
                        last = copy(hT[k % 2][:, kt, :], ps[:, 6, kt * P:(kt + 1) * P], pvec(f"ln{a + 1}_o", kt),
                                    pvec(f"ln{a + 1}_s", kt))
                    last.then_inc(A3["normed"].sem, 1)

                def weights(i, k):
                    wait(D3t["shifted_bias"], i, k)
                    exp(p3[k % 2][:, :], p3[k % 2][:, :], scale=SCALE3).then_inc(A3["weights"].sem, 1)

                def copied(i, k):
                    for half, name in ((0, "a"), (1, "b")):
                        wait(E3[f"turned_{name}"], i, k)
                        wait(E3["out"], i, k - 1)
                        copy(pT3[half][:, :, :], ps[:, 4 + half, :].rearrange("p (k n) -> p k n", k=4)
                             ).then_inc(A3[f"copied_{name}"].sem, 1)
                    wait(E3["turned_bias"], i, k)
                    copy(pb3[:, :], ps[0:H3, 4, 0:P]).then_inc(A3["copied_bias"].sem, 1)

                def batch(i, final=False):
                    for k in range(2):
                        copied(i, k)
                        if not (final and k):
                            weights(i, k + 1)
                        if not final:
                            normed(i, k + 2)

                normed(0, 0)
                normed(0, 1)
                weights(0, 0)
                with act.Fori(0, B - 1) as i:
                    batch(i)
                batch(B - 1, final=True)

            for a in range(2):
                if stop >= 4 + 2 * a:
                    if a == 0:
                        act.wait_ge(e2.sem, e2.end(B))
                        act.wait_ge(d2.sem, d2.end(B))
                    else:
                        act.wait_ge(E3["out"].sem, attn_end(E3["out"], 0))
                        act.wait_ge(D3t["rows"].sem, attn_end(D3t["rows"], 0))
                    head_copies(a)
                if stop >= 5 + 2 * a:
                    act.wait_ge(dp[a].sem, dp[a].end(HP))
                    act.wait_ge(ep[a].sem, ep[a].end(HP))
                    attend(a)
            if stop >= 8:
                act.wait_ge(E3["out"].sem, attn_end(E3["out"], 1))
                act.wait_ge(D3t["rows"].sem, attn_end(D3t["rows"], 1))
                mlp_gelu(1, m3, ACT.Gelu)

        @block.vector
        def _(dve):
            v = nc.vector
            for s in [pdv, dv2p, d2] + dm + dp:
                dve.sem_inc(s.sem, s.per)
            for s in own_dve:
                dve.sem_inc(s.sem, s.seed)

            def step(s, i, name, ins):
                ins.then_inc(s.sem, s.did(name))
                dve.wait_ge(s.sem, s.now(i, name))

            step(pdv, 0, "ones", v.memset(ones[:, :], 1.0))
            dve.wait_ge(dma_k, 80)
            dve.wait_ge(ppe.sem, ppe.now(0, "k0"))
            for mt in range(KT):
                for j in range(4):
                    last = v.tensor_scalar(kbd[:, mt, :, j * SC:(j + 1) * SC], ps[:, mt, :].rearrange("p (b k) -> p b k", b=B),
                                           pvec("L0_bk", mt), const("quarter", j), ALU.add, ALU.mult)
            last.then_inc(pdv.sem, pdv.did("k0"))
            dve.wait_ge(ppe.sem, ppe.now(0, "v0"))
            for hf in range(2):
                v.tensor_scalar(vbd[:, :, hf, 0:D0], ps[:, 2, :].rearrange("p (g d) -> p g d", d=D0),
                                const("half", hf), None, ALU.mult)
                last = v.tensor_scalar(vbd[:, :, hf, D0:D0 + 1], ones[:, 0:B * G0].unsqueeze(2), const("half", hf), None, ALU.mult)
            last.then_inc(pdv.sem, pdv.did("v0"))
            dve.wait_ge(ppe.sem, ppe.now(0, "v1"))
            for e in range(2):
                heads = vc1[:, :, :, :].rearrange("p b (g e r) d -> p (b g) e r d", e=2, r=2)[:, :, e]
                v.tensor_scalar(heads[:, :, :, D1:D1 + 1], ones[:, 0:B * H1 // 2].rearrange("p (g r o) -> p g r o", r=2, o=1),
                                const("half", e), None, ALU.mult)
                last = v.tensor_scalar(heads[:, :, :, 0:D1],
                                       ps[:, 3:7, :].rearrange("p k (g e r d) -> p (k g) e r d", e=2, r=2, d=D1)[:, :, e],
                                       const("half", e), None, ALU.mult)
            last.then_inc(pdv.sem, pdv.did("v1"))
            dve.wait_ge(dma_m, 32)
            v.tensor_scalar(mask1[:, :], maski[:, :], 0.0, MASKED, ALU.is_equal, ALU.mult).then_inc(pdv.sem, pdv.did("m1"))

            def wait(t, i, k=0):
                dve.wait_ge(t.sem, t.at(i, k))

            def own(t, i, k, ins):
                ins.then_inc(t.sem, 1)
                dve.wait_ge(t.sem, t.at(i, k))

            dve.wait_ge(pdv.sem, pdv.now(0, "v0"))
            for c in range(3):
                if c < 2:
                    own(split0, 0, 2 * c, v.tensor_copy(vp0[:, c, :, :, :], vbd[:, :, :, :]))
                    rest = vp0[:, 2, :, :, :] if c else vbd[:, :, :, :]
                    own(split0, 0, 2 * c + 1, v.tensor_tensor(rest, vbd[:, :, :, :], vp0[:, c, :, :, :], ALU.subtract))

            def queries0(i):
                wait(E0["q"], i)
                for mt in range(KT):
                    last = v.tensor_scalar(q0[:, mt, :], ps[:, 7, mt * S:(mt + 1) * S], pvec("L0_bq", mt), SCALE0, ALU.add, ALU.mult)
                own(D0t["q"], i, 0, last)

            def queries_parts0(i):
                wait(E0["scores"], i, -1)
                own(D0t["q_high"], i, 0, v.tensor_copy(qp0[0][:, :, :], q0[:, :, :]))
                v.tensor_tensor(qp0[1][:, :, :], q0[:, :, :], qp0[0][:, :, :].bitcast(F32), ALU.subtract).then_inc(D0t["q_low"].sem, 1)

            def maxima0(i, u):
                t, hf = u // 2, u % 2
                wait(E0["scores"], i, u)
                wait(E0["turned_b"], i, u - 4)
                p = p0[u][:, :].rearrange("p (h k) -> p h k", k=SC)
                own(D0t["masked"], i, u, v.tensor_tensor(
                    p, ps[:, 2 * hf:2 * hf + 2, :].rearrange("p j (h k) -> p (j h) k", k=SC),
                    mask0[:, bass.ds(2 * i + t, 1), :].broadcast_to([P, H0 // 2, SC]), ALU.add))
                v.tensor_reduce(mx0[u][:, :], p, X, ALU.max).then_inc(D0t["maxima"].sem, 1)

            def slot0(i, u, first=False, final=False, after=False):
                k = tail0(u, first, after)
                if u == 1 and not (final or after):
                    queries_parts0(i + 1)
                if not after and not (final and u >= 2):
                    maxima0(i + (u >= 2), (u + 2) % 4)
                if "sums" in k:
                    c = k["sums"]
                    t = c % 2
                    wait(E0["projected"], i, c)
                    wait(G0s["bias"], i, c)
                    own(D0t["sums"], i, c, v.tensor_tensor(y0[:, :], ps[:, 7, 0:D], xb0[t][:, :], ALU.add))
                    own(D0t["stats"], i, c, v.bn_stats(st0[:, :], y0[:, :]))
                    settle(dve)
                    own(D0t["mean"], i, c, v.bn_aggr(mv0[t][:, 0:2], st0[:, :]))
                    v.tensor_scalar(mv0[t][:, 2:3], mv0[t][:, 1:2], EPS0, None, ALU.add).then_inc(D0t["eps"].sem, 1)
                if not after:
                    wait(A0["high"], i, u)
                    for half in range(2):
                        last = v.scalar_tensor_tensor(pl0[u % 2][:, 4 * half:4 * half + 4, :],
                                                      ps[:, 4 + half, :].rearrange("p (k n) -> p k n", k=4), WHOLE,
                                                      ph0[u % 2][:, 4 * half:4 * half + 4, :], ALU.mult, ALU.subtract)
                    last.then_inc(D0t["low"].sem, 1)
                if "sums" in k:
                    wait(G0s["root"], i, c)
                    wait(E0["normed_turned"], i, c - 2)
                    wait(G0s["scaled"], i, c - 2)
                    v.tensor_scalar(xn0[t][:, :], y0[:, :], mv0[t][:, 0:1], mv0[t][:, 3:4], ALU.subtract, ALU.mult
                                    ).then_inc(D0t["normed"].sem, 1)
                if "heads" in k:
                    c = k["heads"]
                    wait(E0["heads"], i, 2 * c + 1)
                    av = ps[:, 6, 0:H0 * (D0 + 1)].rearrange("p (h d) -> p h d", d=D0 + 1)
                    own(D0t["inverse"], i, c, v.reciprocal(ri0[:, :].unsqueeze(2), av[:, :, D0:D0 + 1]))
                    wait(E0["heads_turned"], i, c - 1)
                    for kt in range(KT):
                        last = v.tensor_tensor(
                            ao0[:, kt * P:(kt + 1) * P].rearrange("p (j h d) -> p j h d", j=4, h=4),
                            av[:, :, 0:D0].rearrange("p (j k h) d -> p j k h d", j=4, k=2)[:, :, kt],
                            ri0[:, :].rearrange("p (j k h) -> p j k h", j=4, k=2)[:, :, kt].unsqueeze(3).broadcast_to([P, 4, 4, D0]),
                            ALU.mult)
                    last.then_inc(D0t["heads"].sem, 1)
                if u == 0 and not (final or after):
                    queries0(i + 1)

            queries0(0)
            queries_parts0(0)
            maxima0(0, 0)
            maxima0(0, 1)
            for u in range(4):
                slot0(0, u, first=True)
            with dve.Fori(1, B - 1) as i:
                for u in range(4):
                    slot0(i, u)
            for u in range(4):
                slot0(B - 1, u, final=True)
            for u in range(4):
                slot0(B, u, after=True)

            def keys1(i):
                wait(A1["k_high"], i)
                for mt in range(KT):
                    last = v.scalar_tensor_tensor(kp1[1][:, mt, :], ps[:, mt, 0:SC + KEYS1], pvec("L1_bk", mt),
                                                  kp1[0][:, mt, :].bitcast(F32), ALU.add, ALU.subtract)
                last.then_inc(D1t["k_low"].sem, 1)

            def queries1(i):
                wait(E1["q"], i)
                for mt in range(KT):
                    last = v.tensor_scalar(q1[:, mt, :], ps[:, 2, mt * S:(mt + 1) * S], pvec("L1_bq", mt), SCALE1, ALU.add, ALU.mult)
                own(D1t["q"], i, 0, last)
                wait(E1["scores"], i, -1)
                for par in range(2):
                    last = v.tensor_scalar(qp1[0][:, :, par, :], q1[:, :, :], const("parity", par), None, ALU.mult)
                own(D1t["q_high"], i, 0, last)
                for par in range(2):
                    last = v.scalar_tensor_tensor(qp1[1][:, :, par, :], q1[:, :, :], const("parity", par),
                                                  qp1[0][:, :, par, :].bitcast(F32), ALU.mult, ALU.subtract)
                last.then_inc(D1t["q_low"].sem, 1)

            def values_rest1(i):
                wait(A1["v_high"], i)
                wait(G1["v_low"], i - 1)
                v.tensor_tensor(vr1[:, :, :, :], ps[:, 3, :].rearrange("p (t h d) -> p t h d", t=QT_B, h=H1),
                                v1[:, 0, :, :, 0:D1], ALU.subtract).then_inc(D1t["v_rest"].sem, 1)

            def maxima1(i, u):
                wait(E1["scores"], i, u)
                two_banks = ps[:, 2 * (u % 2):2 * (u % 2) + 2, :]
                c = two_banks.rearrange("p e n -> p (e n)")[:, 256:768].rearrange("p (e n) -> p e n", e=2)[:, :, 0:SC]
                own(D1t["masked"], i, u, v.tensor_tensor(c, c, mask1[:, bass.ds(i * SC, SC)].unsqueeze(1).broadcast_to([P, 2, SC]), ALU.add))
                v.tensor_reduce(nm1[:, u, :], two_banks[:, :, 0:KEYS1], X, ALU.max, negate=True
                                ).then_inc(D1t["maxima"].sem, 1)

            def low1(i, u):
                wait(A1["high"], i, u)
                v.scalar_tensor_tensor(pl1[u % 2][:, 0:4, :], ps[:, 4 + u % 2, :].rearrange("p (k n) -> p k n", k=4), WHOLE,
                                       ph1[u % 2][:, 0:4, :], ALU.mult, ALU.subtract)
                v.scalar_tensor_tensor(pl1[u % 2][:, 4, :], ps[:, 6, 0:P], WHOLE, ph1[u % 2][:, 4, :], ALU.mult,
                                       ALU.subtract).then_inc(D1t["low"].sem, 1)

            def heads_out1(i, k):
                wait(E1["heads"], i, 8 * k + 7)
                av = ps[:, 7, 0:H1 * (D1 + 1)].rearrange("p (h d) -> p h d", d=D1 + 1)
                own(D1t["inverse"], i, k, v.reciprocal(ri1[:, :].unsqueeze(2), av[:, :, D1:D1 + 1]))
                wait(E1["heads_turned"], i, k - 1)
                v.tensor_tensor(ao1[:, :].rearrange("p (h d) -> p h d", h=H1), av[:, :, 0:D1],
                                ri1[:, :].unsqueeze(2).broadcast_to([P, H1, D1]), ALU.mult).then_inc(D1t["heads"].sem, 1)

            def residual1(i, k):
                t = k % 2
                wait(E1["projected"], i, k)
                wait(G1["bias"], i, k)
                own(D1t["sums"], i, k, v.tensor_tensor(y1[t][:, :], ps[:, 6, 0:D], xb1[t][:, :], ALU.add))
                own(D1t["squares"], i, k, v.tensor_tensor_reduce(sq1[:, :], y1[t][:, :], y1[t][:, :], 1.0, 0.0, ALU.mult,
                                                                 ALU.add, ms1[t][:, 0:1]))
                v.tensor_scalar(ms1[t][:, 1:2], ms1[t][:, 0:1], 1.0 / D, EPS1, ALU.mult, ALU.add).then_inc(D1t["mean"].sem, 1)

            def normed1(i, k):
                wait(G1["root"], i, k)
                wait(E1["normed_turned"], i, k - 1)
                v.tensor_scalar(n1[:, :], y1[k % 2][:, :], ms1[k % 2][:, 2:3], None, ALU.mult).then_inc(D1t["normed"].sem, 1)

            def batch1(i, first=False, final=False):
                for u in range(16):
                    for at, k in ((1, -1), (9, 0)):
                        if not (first and k < 0):
                            if u == at + 1:
                                residual1(i, k)
                            if u == at + 2:
                                normed1(i, k)
                    if u + 2 < 16:
                        maxima1(i, u + 2)
                    elif not final:
                        if u == 14:
                            keys1(i + 1)
                        else:
                            queries1(i + 1)
                    low1(i, u)
                    if u == 8:
                        heads_out1(i, 0)
                heads_out1(i, 1)
                if not final:
                    values_rest1(i + 1)
                    maxima1(i + 1, 0)
                    maxima1(i + 1, 1)

            if stop >= 1:
                dve.wait_ge(A0["normed_turned"].sem, A0["normed_turned"].end(B))
                dve.wait_ge(G0s["rows"].sem, G0s["rows"].end(B))
                dve.wait_ge(E0["normed_turned"].sem, E0["normed_turned"].end(B))
                split = D1t["ctx_split"]
                for c in range(3):
                    own(split, 0, 2 * c - (c == 2), v.tensor_copy(vp1[:, c, :, :, :], vc1[:, :, :, :])) if c < 2 else None
                    if c == 0:
                        own(split, 0, 1, v.tensor_tensor(vc1[:, :, :, :], vc1[:, :, :, :], vp1[:, 0, :, :, :], ALU.subtract))
                    elif c == 1:
                        own(split, 0, 3, v.tensor_tensor(vp1[:, 2, :, :, :], vc1[:, :, :, :], vp1[:, 1, :, :, :], ALU.subtract))
                keys1(0)
                queries1(0)
                values_rest1(0)
                maxima1(0, 0)
                maxima1(0, 1)
                batch1(0, first=True)
                with dve.Fori(1, B - 1) as i:
                    batch1(i)
                batch1(B - 1, final=True)
                residual1(B, -1)
                normed1(B, -1)

            def norm_rows(s, i, t, rows, stats, mv, rs, eps, dst, name, free):
                settle(dve)
                step(s, i, f"bn{t}", v.bn_stats(stats[:, :], rows))
                settle(dve)
                step(s, i, f"mv{t}", v.bn_aggr(mv[:, 0:2], stats[:, :]))
                v.tensor_scalar(mv[:, 2:3], mv[:, 1:2], eps, None, ALU.add).then_inc(s.sem, s.did(f"eps{t}"))
                dve.wait_ge(rs.sem, rs.now(i, f"rs{t}"))
                free()
                v.tensor_scalar(dst, rows, mv[:, 0:1], mv[:, 3:4], ALU.subtract, ALU.mult).then_inc(s.sem, s.did(f"{name}{t}"))

            def mlp_rows(m, w):
                with dve.Fori(0, NCH) as i:
                    if m:
                        for t in range(QC):
                            def free(t=t):
                                dve.wait_ge(em[1].sem, em[1].now(i, f"x{t - 2}") if t >= 2 else em[1].prev(i, f"x{t + 2}"))
                            norm_rows(dm[1], i, t, xr[:, bass.ds(i * QC + t, 1), :].rearrange("p o n -> p (o n)"), stm, mvm[t % 2],
                                      gm[1], EPS3, hnm[t % 2][:, :], "xn", free)
                    for t in range(QC):
                        dve.wait_ge(em[m].sem, em[m].now(i, f"o{t}"))
                        dve.wait_ge(gm[m].sem, gm[m].now(i, f"xb{t}"))
                        v.tensor_tensor(xr[:, bass.ds(i * QC + t, 1), :].rearrange("p o n -> p (o n)"), ps[:, 2 + t % 2, 0:D], w["xb"][t % 2][:, :], ALU.add
                                        ).then_inc(dm[m].sem, dm[m].did(f"o{t}"))

            if stop >= 2:
                mlp_rows(0, m1)

            if stop >= 3:
                dve.wait_ge(pe2p.sem, pe2p.now(0, "k"))
                for mt in range(KT):
                    last = v.tensor_copy(t2[:, 0, mt, :], ps[:, mt, :])
                last.then_inc(dv2p.sem, dv2p.did("k"))
                dve.wait_ge(pe2p.sem, pe2p.now(0, "kq"))
                for mt in range(KT):
                    last = v.tensor_copy(k2[:, mt, :, :], ps[:, 4 + mt, :].rearrange("p (b k) -> p b k", b=B))
                last.then_inc(dv2p.sem, dv2p.did("kq"))
                dve.wait_ge(pe2p.sem, pe2p.now(0, "v"))
                for mt in range(KT):
                    last = v.tensor_copy(t2[:, 1, mt, :], ps[:, 2 + mt, :])
                last.then_inc(dv2p.sem, dv2p.did("v"))
                dve.wait_ge(pe2p.sem, pe2p.now(0, "vo"))
                v.tensor_scalar(v2[:, :, :].rearrange("p b n -> p (b n)"), ps[0:SC, 4:8, :].rearrange("p k n -> p (k n)"),
                                alpha[0:SC, :], None, ALU.mult).then_inc(dv2p.sem, dv2p.did("vo"))
                with dve.Fori(0, B) as i:
                    for t in range(2):
                        dve.wait_ge(e2.sem, e2.now(i, f"s{t}"))
                        dve.wait_ge(a2.sem, a2.prev(i, f"exp{t}"))
                        dve.wait_ge(d2.sem, d2.prev(i, f"y{t}"))
                        step(d2, i, f"m{t}", v.tensor_reduce(sm2[t][:, 3:4], ps[:, 2 + t, 0:SC], X, ALU.max, negate=True))
                        v.tensor_scalar(sm2[t][:, 0:1], sm2[t][:, 3:4], SCALE2, None, ALU.mult).then_inc(d2.sem, d2.did(f"max{t}"))
                    for t in range(2):
                        dve.wait_ge(a2.sem, a2.now(i, f"exp{t}"))
                        step(d2, i, f"s{t}", v.tensor_reduce(sm2[t][:, 1:2], p2[t][:, :], X, ALU.add))
                        step(d2, i, f"sum{t}", v.reciprocal(sm2[t][:, 2:3], sm2[t][:, 1:2]))
                    for t in range(2):
                        dve.wait_ge(e2.sem, e2.now(i, f"o{t}"))
                        xq = xr[:, bass.ds(2 * i + t, 1), :].rearrange("p o n -> p (o n)")
                        v.scalar_tensor_tensor(xq, ps[:, 6 + t, 0:D], sm2[t][:, 2:3], xq, ALU.mult, ALU.add).then_inc(d2.sem, d2.did(f"y{t}"))

            def head_copies(a):
                with dve.Fori(0, HP) as i:
                    for t in range(2):
                        w = bun[t]
                        dve.wait_ge(dma_bun[a][t], 16 * i + 16)
                        dve.wait_ge(ep[a].sem, ep[a].now(i, f"k{t}"))
                        dve.wait_ge(ep[a].sem, ep[a].now(i, "b0") if t else ep[a].prev(i, "b1"))
                        v.tensor_scalar(kh[:, :], ps[:, 0, :], w[:, 4 * D:4 * D + 1], None, ALU.add).then_inc(dp[a].sem, dp[a].did(f"k{t}"))
                        dve.wait_ge(ep[a].sem, ep[a].now(i, f"w{t}"))
                        v.tensor_copy(v3[HALF * t:HALF * (t + 1), 1:B:2, bass.ds(i, 1), :].rearrange("p b o n -> p b (o n)"),
                                      ps[HALF:P, 5:7, :].rearrange("p k (c n) -> p (k c) n", c=2)).then_inc(dp[a].sem, dp[a].did(f"w{t}"))
                        dve.wait_ge(ep[a].sem, ep[a].now(i, f"r{t}"))
                        v.tensor_copy(gb3[:, :, bass.ds(2 * i + t, 1)], ps[:, 7, D:D + 2].unsqueeze(2))
                        v.tensor_copy(bb3[:, bass.ds(2 * i + t, 1)], ps[0:1, 7, D + 4:D + 5]).then_inc(dp[a].sem, dp[a].did(f"m{t}"))
                        v.tensor_tensor(vb3[:, :], vb3[:, :], ps[0:H3, 7, 0:D], ALU.add).then_inc(dp[a].sem, dp[a].did(f"vb{t}"))

            def attend(a):
                def wait(t, i, k):
                    dve.wait_ge(t.sem, t.at(i, k + a * B * t.per))

                def own3(name, i, k, ins):
                    ins.then_inc(D3t[name].sem, 1)
                    wait(D3t[name], i, k)

                def rows(i, k):
                    return xr[:, bass.ds(2 * i + k, 1), :].rearrange("p o n -> p (o n)")

                def normed(i, k):
                    mv = mv3[k % 2]
                    settle(dve)
                    own3("stats", i, k, v.bn_stats(st3[:, :], rows(i, k)))
                    settle(dve)
                    own3("mean", i, k, v.bn_aggr(mv[:, 0:2], st3[:, :]))
                    v.tensor_scalar(mv[:, 2:3], mv[:, 1:2], EPS3, None, ALU.add).then_inc(D3t["eps"].sem, 1)
                    wait(G3["root"], i, k)
                    wait(E3["normed"], i, k - 2)
                    v.tensor_scalar(hn[k % 2][:, :], rows(i, k), mv[:, 0:1], mv[:, 3:4], ALU.subtract, ALU.mult
                                    ).then_inc(D3t["normed"].sem, 1)

                def shifted(i, k):
                    t = k % 2
                    wait(E3["scores"], i, k)
                    wait(E3["turned_bias"], i, k - 2)
                    sc = ps[:, 2 * t:2 * t + 2, :].rearrange("p c (h k) -> p (c h) k", k=SC)
                    sbk = ps[:, 6, D:D + H3]
                    own3("max", i, k, v.tensor_reduce(mx3[t][:, :], sc, X, ALU.max))
                    own3("max_bias", i, k, v.tensor_tensor(mx3[t][:, :], sbk, mx3[t][:, :], ALU.max))
                    v.tensor_tensor(p3[t][:, 0:KEYS3].rearrange("p (h k) -> p h k", k=SC), sc,
                                    mx3[t][:, :].unsqueeze(2).broadcast_to([P, H3, SC]), ALU.subtract).then_inc(D3t["shifted"].sem, 1)
                    v.tensor_tensor(p3[t][:, KEYS3:], sbk, mx3[t][:, :], ALU.subtract).then_inc(D3t["shifted_bias"].sem, 1)

                def inverse(i, k):
                    t = k % 2
                    wait(A3["weights"], i, k)
                    wait(G3["weights"], i, k - 2)
                    own3("sum", i, k, v.tensor_reduce(sm3[t][:, :], p3[t][:, 0:KEYS3].rearrange("p (h k) -> p h k", k=SC), X, ALU.add))
                    own3("sum_bias", i, k, v.tensor_tensor(sm3[t][:, :], sm3[t][:, :], p3[t][:, KEYS3:], ALU.add))
                    own3("inverse", i, k, v.reciprocal(sm3[t][:, :], sm3[t][:, :]))
                    v.tensor_tensor(p3[t][:, KEYS3:], p3[t][:, KEYS3:], sm3[t][:, :], ALU.mult).then_inc(D3t["weight_bias"].sem, 1)

                def residual(i, k):
                    wait(E3["out"], i, k)
                    wait(G3["bias"], i, k)
                    v.tensor_tensor(rows(i, k), ps[:, 7, 0:D], xb3[k % 2][:, :], ALU.add).then_inc(D3t["rows"].sem, 1)

                def batch(i, final=False):
                    for k in range(2):
                        if not final:
                            normed(i, k + 2)
                        if not (final and k):
                            shifted(i, k + 1)
                            inverse(i, k + 1)
                        residual(i, k)

                normed(0, 0)
                normed(0, 1)
                shifted(0, 0)
                inverse(0, 0)
                with dve.Fori(0, B - 1) as i:
                    batch(i)
                batch(B - 1, final=True)

            for a in range(2):
                if stop >= 4 + 2 * a:
                    if a == 1:
                        dve.wait_ge(E3["out"].sem, attn_end(E3["out"], 0))
                        dve.wait_ge(A3["copied_bias"].sem, attn_end(A3["copied_bias"], 0))
                    else:
                        dve.wait_ge(e2.sem, e2.end(B))
                        dve.wait_ge(a2.sem, a2.end(B))
                    dve.wait_ge(vbz[a], 1)
                    head_copies(a)
                if stop >= 5 + 2 * a:
                    dve.wait_ge(ap_[a].sem, ap_[a].end(HP))
                    attend(a)
            if stop >= 8:
                dve.wait_ge(E3["out"].sem, attn_end(E3["out"], 1))
                mlp_rows(1, m3)

        @block.gpsimd
        def _(pool):
            g = nc.gpsimd
            for s in [ppo, g2] + gm:
                pool.sem_inc(s.sem, s.per)
            for s in own_pool:
                pool.sem_inc(s.sem, s.seed)
            pool.wait_ge(dma_k, 80)
            pool.wait_ge(dma_x, 16)

            def root(dst, src):
                return g.tensor_tensor(dst, src, const("minus_half"), ALU.pow)

            def xq(i, t):
                return xr[:, bass.ds(2 * i + t, 1), :].rearrange("p o n -> p (o n)")

            def wait(t, i, k=0):
                pool.wait_ge(t.sem, t.at(i, k))

            def keys0(i):
                wait(E0["scores"], i, -1)
                settle(pool)
                k = kbd[:, :, bass.ds(i, 1), :].rearrange("p k o n -> p k (o n)")
                g.tensor_copy(kp0[0][:, :, :], k).then_inc(G0s["k_high"].sem, 1)
                wait(G0s["k_high"], i)
                settle(pool)
                g.tensor_tensor(kp0[1][:, :, :], k, kp0[0][:, :, :].bitcast(F32), ALU.subtract).then_inc(G0s["k_low"].sem, 1)

            def shift0(i, u):
                wait(D0t["maxima"], i, u)
                p = p0[u][:, :].rearrange("p (h k) -> p h k", k=SC)
                g.tensor_tensor(p, p, mx0[u][:, :].unsqueeze(2).broadcast_to([P, H0 // 2, SC]), ALU.subtract).then_inc(G0s["shifted"].sem, 1)

            def slot0(i, u, first=False, final=False, after=False):
                k = tail0(u, first, after)
                if u == 1 and not (final or after):
                    keys0(i + 1)
                if not after and not (final and u >= 2):
                    shift0(i + (u >= 2), (u + 2) % 4)
                if "sums" in k:
                    c = k["sums"]
                    wait(D0t["eps"], i, c)
                    root(mv0[c % 2][:, 3:4], mv0[c % 2][:, 2:3]).then_inc(G0s["root"].sem, 1)
                if u == 0 and not after:
                    wait(E0["heads"], i, -1)
                    settle(pool)
                    g.tensor_copy(vb0[:, :, :, :, :].rearrange("p c g h d -> p c (g h d)"),
                                  vp0[:, :, bass.ds(i * G0, G0), :, :].rearrange("p c g h d -> p c (g h d)")
                                  ).then_inc(G0s["values"].sem, 1)
                if "turned" in k:
                    c = k["turned"]
                    wait(D0t["normed"], i, c)
                    wait(G0s["rows"], i, c - 1)
                    g.tensor_tensor(xg0[:, :], xn0[c % 2][:, :], prow("L0_gamma"), ALU.mult).then_inc(G0s["scaled"].sem, 1)
                    wait(G0s["scaled"], i, c)
                    settle(pool)
                    g.tensor_tensor(xq(i, c), xg0[:, :], prow("L0_beta"), ALU.add).then_inc(G0s["rows"].sem, 1)
                if "projected" in k:
                    c = k["projected"]
                    wait(D0t["sums"], i, c - 2)
                    settle(pool)
                    g.tensor_tensor(xb0[c % 2][:, :], xq(i, c), prow("L0_bo"), ALU.add).then_inc(G0s["bias"].sem, 1)

            pool.wait_ge(split0.sem, split0.at(0, 3))
            keys0(0)
            shift0(0, 0)
            shift0(0, 1)
            for u in range(4):
                slot0(0, u, first=True)
            with pool.Fori(1, B - 1) as i:
                for u in range(4):
                    slot0(i, u)
            for u in range(4):
                slot0(B - 1, u, final=True)
            for u in range(4):
                slot0(B, u, after=True)

            def x1(i):
                wait(E1["v"], i - 1)
                settle(pool)
                g.tensor_copy(xb1T[:, :, :], xT[:, :, bass.ds(i * S, S)]).then_inc(G1["x"].sem, 1)

            def values_mid_low1(i):
                wait(E1["heads"], i, -1)
                settle(pool)
                g.tensor_copy(vb1[:, :, :, :], vp1[:, :, bass.ds(i, 1), :, :].rearrange("p c o h d -> p c (o h) d")
                              ).then_inc(G1["v_ctx"].sem, 1)
                wait(D1t["v_rest"], i)
                settle(pool)
                g.tensor_copy(v1[:, 1, :, :, 0:D1], vr1[:, :, :, :]).then_inc(G1["v_mid"].sem, 1)
                wait(G1["v_mid"], i)
                g.tensor_tensor(v1[:, 2, :, :, 0:D1], vr1[:, :, :, :], v1[:, 1, :, :, 0:D1], ALU.subtract).then_inc(G1["v_low"].sem, 1)

            def root1(i, k):
                wait(D1t["mean"], i, k)
                root(ms1[k % 2][:, 2:3], ms1[k % 2][:, 1:2]).then_inc(G1["root"].sem, 1)

            def batch1(i, first=False, final=False):
                if not first:
                    root1(i, -1)
                if not final:
                    x1(i + 1)
                for t in range(2):
                    wait(D1t["sums"], i, t - 2)
                    settle(pool)
                    g.tensor_tensor(xb1[t][:, :], xq(i, t), prow("L1_bo"), ALU.add).then_inc(G1["bias"].sem, 1)
                root1(i, 0)
                if not final:
                    values_mid_low1(i + 1)

            if stop >= 1:
                pool.wait_ge(A0["normed_turned"].sem, A0["normed_turned"].end(B))
                pool.wait_ge(D0t["normed"].sem, D0t["normed"].end(B))
                pool.wait_ge(E0["normed_turned"].sem, E0["normed_turned"].end(B))
                pool.wait_ge(G0s["rows"].sem, G0s["rows"].end(B))
                wait(D1t["ctx_split"], 0, 3)
                x1(0)
                g.memset(v1[:, 0, :, :, D1:D1 + 1], 1.0)
                g.memset(v1[:, 1:3, :, :, D1:D1 + 1], 0.0)
                values_mid_low1(0)
                batch1(0, first=True)
                with pool.Fori(1, B - 1) as i:
                    batch1(i)
                batch1(B - 1, final=True)
                root1(B, -1)

            def mlp_bias(m, w, bias):
                with pool.Fori(0, NCH) as i:
                    if m:
                        for t in range(QC):
                            pool.wait_ge(dm[1].sem, dm[1].now(i, f"eps{t}"))
                            root(mvm[t % 2][:, 3:4], mvm[t % 2][:, 2:3]).then_inc(gm[1].sem, gm[1].did(f"rs{t}"))
                    for t in range(QC):
                        pool.wait_ge(dm[m].sem, dm[m].now(i, f"o{t - 2}") if t >= 2 else dm[m].prev(i, f"o{t + 2}"))
                        settle(pool)
                        g.tensor_tensor(w["xb"][t % 2][:, :], xr[:, bass.ds(i * QC + t, 1), :].rearrange("p o n -> p (o n)"), prow(bias), ALU.add
                                        ).then_inc(gm[m].sem, gm[m].did(f"xb{t}"))

            if stop >= 2:
                pool.wait_ge(E1["normed_turned"].sem, E1["normed_turned"].end(B))
                pool.wait_ge(D1t["normed"].sem, D1t["normed"].end(B))
                pool.wait_ge(A1["normed_turned"].sem, A1["normed_turned"].end(B))
                mlp_bias(0, m1, "L1_b2")

            if stop >= 3:
                pool.wait_ge(dm[0].sem, dm[0].end(NCH))
                with pool.Fori(0, B) as i:
                    for t in range(2):
                        pool.wait_ge(e2.sem, e2.prev(i, f"xt{t}"))
                        settle(pool)
                        g.tensor_copy(x2[t][:, :], xq(i, t)).then_inc(g2.sem, g2.did(f"x{t}"))

            def attend(a):
                def wait(t, i, k):
                    pool.wait_ge(t.sem, t.at(i, k + a * B * t.per))

                def root3(i, k):
                    wait(D3t["eps"], i, k)
                    root(mv3[k % 2][:, 3:4], mv3[k % 2][:, 2:3]).then_inc(G3["root"].sem, 1)

                def weights(i, k):
                    t = k % 2
                    wait(D3t["inverse"], i, k)
                    p = p3[t][:, 0:KEYS3].rearrange("p (h k) -> p h k", k=SC)
                    g.tensor_tensor(p, p, sm3[t][:, :].unsqueeze(2).broadcast_to([P, H3, SC]), ALU.mult
                                    ).then_inc(G3["weights"].sem, 1)

                def batch(i, final=False):
                    for k in range(2):
                        if not final:
                            root3(i, k + 2)
                        wait(D3t["rows"], i, k - 2)
                        settle(pool)
                        g.tensor_tensor(xb3[k][:, :], xq(i, k), prow(f"bo{a + 1}"), ALU.add).then_inc(G3["bias"].sem, 1)
                        if not (final and k):
                            weights(i, k + 1)

                root3(0, 0)
                root3(0, 1)
                weights(0, 0)
                with pool.Fori(0, B - 1) as i:
                    batch(i)
                batch(B - 1, final=True)

            for a in range(2):
                if stop >= 4 + 2 * a:
                    if a == 0:
                        pool.wait_ge(e2.sem, e2.end(B))
                        pool.wait_ge(d2.sem, d2.end(B))
                    else:
                        pool.wait_ge(E3["out"].sem, attn_end(E3["out"], 0))
                        pool.wait_ge(D3t["rows"].sem, attn_end(D3t["rows"], 0))
                    g.memset(one3[:, :], 1.0)
                    g.memset(vb3[:, :], 0.0).then_inc(vbz[a], 1)
                if stop >= 5 + 2 * a:
                    pool.wait_ge(dp[a].sem, dp[a].end(HP))
                    pool.wait_ge(ep[a].sem, ep[a].end(HP))
                    pool.wait_ge(ap_[a].sem, ap_[a].end(HP))
                    attend(a)
            if stop >= 8:
                pool.wait_ge(E3["out"].sem, attn_end(E3["out"], 1))
                pool.wait_ge(D3t["rows"].sem, attn_end(D3t["rows"], 1))
                mlp_bias(1, m3, "b_fc2")


STOP = 8


def kernel(**inputs):
    import concourse.bacc as bacc
    from concourse.bass_utils import run_bass_kernel_spmd

    a = {k: np.asarray(v) for k, v in inputs.items()}

    def tiles(w):
        return np.ascontiguousarray(w.reshape(-1, P, w.shape[1]).transpose(1, 0, 2)).reshape(P, -1)

    def column(v):
        return v.reshape(-1, P).T

    f = np.float32
    rep = lambda w: np.repeat(w.reshape(w.shape[0], G0, 1, D0), H0 // G0, 2).reshape(w.shape[0], D)
    rows = np.arange(P)
    const = np.concatenate([
        np.eye(P, dtype=f), (rows[:, None] // D0 % 4 == np.arange(4)).astype(f),
        (rows[:, None] // D1 % 2 == np.arange(2)).astype(f), (rows[:, None] // HALF == np.arange(2)).astype(f),
        np.full((P, 1), -0.5, f)], 1)
    kv, kvb = a["L1_xattn_kv_w"].reshape(D, D, 2), a["L1_xattn_kv_b"].reshape(D, 2)
    vecs = {
        "L0_bq": a["L0_xattn_bq"], "L0_bk": rep(a["L0_xattn_bk"][None])[0], "L0_bv": rep(a["L0_xattn_bv"][None])[0],
        "L0_gamma": a["L0_xattn_gamma"], "L0_beta": a["L0_xattn_beta"],
        "L1_bq": a["L1_xattn_q_b"], "L1_bk": kvb[:, 0], "L1_bv": kvb[:, 1], "L1_norm": a["L1_xattn_postnorm_w"],
        "ln1_s": a["L3_xattn_ln1_scale"], "ln1_o": a["L3_xattn_ln1_offset"],
        "ln2_s": a["L3_xattn_ln2_scale"], "ln2_o": a["L3_xattn_ln2_offset"],
        "lnm_s": a["L3_xattn_ln_mlp_scale"], "lnm_o": a["L3_xattn_ln_mlp_offset"]}
    rowv = {"L0_bo": a["L0_xattn_bo"], "L0_gamma": a["L0_xattn_gamma"], "L0_beta": a["L0_xattn_beta"],
            "L1_bo": a["L1_xattn_out_b"], "L1_b2": a["L1_xattn_mlp_b2"], "bo1": a["L3_xattn_bo1"],
            "bo2": a["L3_xattn_bo2"], "b_fc2": a["L3_xattn_b_fc2"]}

    def heads(n):
        g = lambda name: a[f"L3_xattn_{name}{n}"]
        out = np.zeros((H3, P, BUN), f)
        for h in range(H3):
            c = slice(h * D3, (h + 1) * D3)
            out[h, :, 0:D] = tiles(g("wk")[:, c])
            out[h, :, D:2 * D] = g("wq")[:, c].T
            out[h, :, 2 * D:3 * D] = tiles(g("wv")[:, c])
            out[h, :, 3 * D:4 * D] = g("wo")[c]
            for k, v in enumerate((g("bk")[c], g("bq")[c], g("bv")[c], g("bias_k")[0, 0, h])):
                out[h, :, 4 * D + k] = v
            out[h, :, 4 * D + 4 + h] = g("bias_v")[0, 0, h]
        return out

    arrays = {
        "x": a["x"], "xT": tiles(a["x"].reshape(T, D).T).reshape(P, KT, T),
        "ctxT": tiles(a["ctx_2048"].reshape(C, D).T).reshape(P, KT, C),
        "mask0": a["mask_Bx1xSxS2_ff0"], "mask1": a["mask_BxS2_ik0"].reshape(C),
        "const": const, "alpha": a["L2_xattn_alpha"].reshape(1),
        "vecs": np.concatenate([column(vecs[n]) for n in VECS] + [column(a["L1_xattn_mlp_b1"]), column(a["L3_xattn_b_fc1"])], 1),
        "rows": np.stack([rowv[n] for n in ROWS]),
        "w0": np.concatenate([tiles(a["L0_xattn_Wq"]), tiles(rep(a["L0_xattn_Wk"])), tiles(a["L0_xattn_Wo"]),
                              tiles(a["L0_xattn_Wv"])], 1),
        "w1": np.concatenate([tiles(a["L1_xattn_q_w"]), tiles(kv[:, :, 0]), tiles(kv[:, :, 1]), tiles(a["L1_xattn_out_w"])], 1),
        "w2": np.concatenate([tiles(a["L2_xattn_w_q"]), tiles(a["L2_xattn_w_k"].T), tiles(a["L2_xattn_w_v"].T),
                              tiles(a["L2_xattn_w_o"].T)], 1),
        "m1a": tiles(a["L1_xattn_mlp_w1"]).reshape(P, KT, F), "m1b": tiles(a["L1_xattn_mlp_w2"]).reshape(P, FT, D),
        "m3a": tiles(a["L3_xattn_w_fc1"]).reshape(P, KT, F), "m3b": tiles(a["L3_xattn_w_fc2"]).reshape(P, FT, D),
        "heads0": heads(1), "heads1": heads(2),
    }
    arrays = {k: np.ascontiguousarray(v) for k, v in arrays.items()}
    nc = bacc.Bacc("TRN2", target_bir_lowering=False, num_devices=1)
    io = {k: nc.dram_tensor(f"in_{k}", v.shape, mybir.dt.from_np(v.dtype), kind="ExternalInput").ap() for k, v in arrays.items()}
    out = nc.dram_tensor("out", (B, S, D), F32, kind="ExternalOutput").ap()
    build(nc, io, out, STOP)
    r = run_bass_kernel_spmd(nc, [{f"in_{k}": v for k, v in arrays.items()}], core_ids=[0])
    return r.results[0]["out"]
```

```python
from contextlib import ExitStack

import numpy as np

import concourse.bass as bass
from concourse import mybir

F32 = mybir.dt.float32
I32 = mybir.dt.int32
F32R = mybir.dt.float32r
F16 = mybir.dt.float16
BF16 = mybir.dt.bfloat16
ALU = mybir.AluOpType
ACT = mybir.ActivationFunctionType
X = mybir.AxisListType.X

PARTS = ((0, 0), (0, 1), (1, 0))
STACKED = ((0, 0), (0, 1), (1, 0), (1, 1), (0, 2), (2, 0))
STACK = len(STACKED)
STACK_DMAS = 2 * STACK
MASK_ROW = STACK * 16

P = 128
D = 256
KT = D // P
B = 8
S = 256
SC = 64
QT_B = S // P
NQ = B * QT_B
T = B * S
C = B * SC
HALF = P // 2

H0, G0, D0 = 32, 8, 8
SCALE0 = float(1.0 / np.sqrt(np.float32(D0)))
EPS0 = 1e-6
H1, D1 = 16, 16
KEYS1 = S + SC
SCALE1 = 1.0 / D1
EPS1 = 1e-6
MASKED = -3.0e38
WHOLE = float(2 ** 15)
F = 1024
FT = F // P
CH = 512
NCH = T // CH
QC = CH // P
SCALE2 = float(1.0 / np.sqrt(np.float32(D)))
H3, D3 = 16, 128
SCALE3 = float(1.0 / np.sqrt(np.float32(D3)))
EPS3 = 1e-5
HP = H3 // 2
KEYS3 = H3 * SC

CONST = dict(ident=(0, P), quarter=(128, 4), parity=(132, 2), half=(134, 2), minus_half=(136, 1))
NCONST = 137
VECS = ["L0_bq", "L0_bk", "L0_bv", "L0_gamma", "L0_beta", "L1_bq", "L1_bk", "L1_bv", "L1_norm",
        "ln1_s", "ln1_o", "ln2_s", "ln2_o", "lnm_s", "lnm_o"]
NVEC = len(VECS) * KT + 2 * FT
ROWS = ["L0_bo", "L0_gamma", "L0_beta", "L1_bo", "L1_b2", "bo1", "bo2", "b_fc2"]
W0 = dict(wq=(0, 512), wk=(512, 512), wo=(1024, 512), wv=(1536, 128))
W1 = dict(wq=(0, 512), wk=(512, 512), wv=(1024, 512), wo=(1536, 512))
W2 = dict(wq=(0, 512), wkT=(512, 512), wvT=(1024, 512), woT=(1536, 512))
BUN = 4 * D + 4 + H3


class Steps:

    def __init__(self, sem, name, steps):
        self.sem, self.steps, self.per, self.k = sem(name), list(steps), len(steps), 0
        assert len(set(self.steps)) == self.per, name

    def now(self, i, step):
        return (i + 1) * self.per + (self.steps.index(step) + 1)

    def prev(self, i, step):
        return i * self.per + (self.steps.index(step) + 1)

    def end(self, iterations):
        return (iterations + 1) * self.per

    def did(self, step):
        assert self.steps[self.k % self.per] == step, (step, self.steps[self.k % self.per])
        self.k += 1
        return 1


class Tally:

    def __init__(self, sem, name, per, owned):
        self.sem, self.per, self.seed = sem(name), per, per + 1
        owned.append(self)

    def at(self, i, k=0):
        return i * self.per + (k + 1 + self.seed)

    def end(self, iterations):
        return self.at(iterations, -1)



def spread(lead, per_unit, extra, tail):
    out = list(lead)
    for u in range(16):
        out += per_unit(u) + extra.get(u, [])
    return out + list(tail)


def build(nc, io, out):
    ctx = ExitStack()
    with ctx:
        def sem(name):
            return ctx.enter_context(nc.semaphore(name))

        def sb(name, shape, dt=F32, where=ctx):
            return where.enter_context(nc.sbuf_tensor(name, shape, dt))

        ps = ctx.enter_context(nc.psum_tensor("ps", [P, 8, 512], F32))

        xr = sb("xr", [P, NQ, D])
        cT = sb("cT", [P, KT, C])
        cst = sb("cst", [P, NCONST])
        vec = sb("vec", [P, NVEC])
        row3 = sb("row3", [P, 3, D])
        alpha = sb("alpha", [P, 1])
        ident = cst[:, 0:P]

        def const(name, k=0):
            return cst[:, CONST[name][0] + k:CONST[name][0] + k + 1]

        def pvec(name, kt):
            c = VECS.index(name) * KT + kt
            return vec[:, c:c + 1]

        def fvec(which, ft):
            c = len(VECS) * KT + which * FT + ft
            return vec[:, c:c + 1]

        def prow(name):
            k = ROWS.index(name)
            return row1[:, k, :] if k < len(ROWS) - 3 else row3[:, k - (len(ROWS) - 3), :]

        def wt(tile, cols, name):
            a, n = cols[name]
            return tile[:, a:a + n].rearrange("p (k n) -> p k n", k=KT)

        upto2 = ExitStack()
        w2 = sb("w2", [P, 2048], where=upto2)
        row1 = sb("row1", [P, len(ROWS) - 3, D], where=upto2)
        early = ExitStack()
        xT = sb("xT", [P, KT, T], where=early)
        nT = sb("nT", [P, KT, T], where=early)
        attn01 = ExitStack()
        w1 = sb("w1", [P, 2048], where=attn01)
        vp1 = sb("vp1", [P, 3, B, H1, D1 + 1], BF16, where=attn01)
        maski = sb("maski", [P, B * SC], I32, where=attn01)
        mask1 = sb("mask1", [P, B * SC], where=attn01)

        l0 = ExitStack()
        w0 = sb("w0", [P, 1664], where=l0)
        kbd = sb("kbd", [P, KT, B, 4 * SC], where=l0)
        vbd = sb("vbd", [P, B * G0, 2, D0 + 1], where=l0)
        vp0 = sb("vp0", [P, 3, B * G0, 2, D0 + 1], BF16, where=l0)
        vc1 = sb("vc1", [P, B, H1, D1 + 1], where=l0)
        mask0 = sb("mask0", [P, NQ, SC], where=l0)
        ones = sb("ones", [P, P], where=l0)
        q0 = sb("q0", [P, KT, S], where=l0)
        qp0 = [sb(f"qp0_{n}", [P, KT, S], F32R, where=l0) for n in ("high", "low")]
        kp0 = [sb(f"kp0_{n}", [P, KT, 4 * SC], F32R, where=l0) for n in ("high", "low")]
        vb0 = sb("vb0", [P, 3, G0, 2, D0 + 1], BF16, where=l0)
        p0 = [sb(f"p0_{u}", [P, 1024], where=l0) for u in range(4)]
        mx0 = [sb(f"mx0_{u}", [P, H0 // 2], where=l0) for u in range(4)]
        ph0 = [sb(f"ph0_{t}", [P, 8, P], F16, where=l0) for t in range(2)]
        pl0 = [sb(f"pl0_{t}", [P, 8, P], F16, where=l0) for t in range(2)]
        ri0 = sb("ri0", [P, H0], where=l0)
        ao0 = sb("ao0", [P, D], where=l0)
        aoT0 = sb("aoT0", [P, KT, P], where=l0)
        xb0 = [sb(f"xb0_{t}", [P, D], where=l0) for t in range(2)]
        y0 = sb("y0", [P, D], where=l0)
        st0 = sb("st0", [P, 6], where=l0)
        mv0 = [sb(f"mv0_{t}", [P, 4], where=l0) for t in range(2)]
        xn0 = [sb(f"xn0_{t}", [P, D], where=l0) for t in range(2)]
        xg0 = sb("xg0", [P, D], where=l0)
        l0.close()

        l1 = ExitStack()
        vall1 = sb("vall1", [P, 3, NQ, H1, D1 + 1], BF16, where=l1)
        qs1 = [sb(f"qs1_{t}", [STACK * D1 + 1, H1, S], BF16, where=l1) for t in range(2)]
        ks1 = [sb(f"ks1_{t}", [STACK * D1 + 1, H1, KEYS1], BF16, where=l1) for t in range(2)]
        vt1 = [sb(f"vt1_{t}", [P, 3, 3, H1, D1 + 1], BF16, where=l1) for t in range(2)]
        l1p = ExitStack()
        xb1T = [sb(f"xb1T_{t}", [P, KT, S], where=l1p) for t in range(2)]
        t1 = {n: [sb(f"{n}1_{t}", [P, KT, S] if n != "v" else [P, KT * S], where=l1p) for t in range(2)] for n in "qkv"}
        pt1 = {n: [sb(f"{n}p1_{t}", [P, 3, KT, w], BF16, where=l1p) for t in range(2)] for n, w in (("q", S), ("k", KEYS1))}
        tc1 = sb("tc1", [P, KT, C], where=l1p)
        pc1 = sb("pc1", [P, 3, KT, C], BF16, where=l1p)
        l1p.close()
        nm1 = sb("nm1", [P, 16, 2], where=l1)
        p1 = [sb(f"p1_{t}", [P, 2 * KEYS1], where=l1) for t in range(2)]
        ph1 = [sb(f"ph1_{t}", [P, 5, P], F16, where=l1) for t in range(2)]
        pl1 = [sb(f"pl1_{t}", [P, 5, P], F16, where=l1) for t in range(2)]
        ri1 = sb("ri1", [P, H1], where=l1)
        ao1 = sb("ao1", [P, D], where=l1)
        aoT1 = sb("aoT1", [P, KT, P], where=l1)
        xb1 = [sb(f"xb1_{t}", [P, D], where=l1) for t in range(2)]
        y1 = [sb(f"y1_{t}", [P, D], where=l1) for t in range(2)]
        sq1 = sb("sq1", [P, D], where=l1)
        ms1 = [sb(f"ms1_{t}", [P, 4], where=l1) for t in range(2)]
        n1 = sb("n1", [P, D], where=l1)
        l1.close()
        attn01.close()

        mlp1 = ExitStack()
        m1 = dict(wa=xT[:, 0, :].rearrange("p (k f) -> p k f", k=KT), wb=xT[:, 1, :].rearrange("p (f d) -> p f d", f=FT),
                  h=sb("hid1", [P, FT, CH], where=mlp1), xb=[sb(f"xbm1_{t}", [P, D], where=mlp1) for t in range(2)])
        mlp1.close()
        early.close()

        l2 = ExitStack()
        k2 = sb("k2", [P, KT, B, SC], where=l2)
        v2 = sb("v2", [SC, B, D], where=l2)
        t2 = sb("t2", [P, 2, KT, C], where=l2)
        x2 = [sb(f"x2_{t}", [P, D], where=l2) for t in range(2)]
        x2T = [sb(f"x2T{t}", [P, KT, P], where=l2) for t in range(2)]
        p2 = [sb(f"p2_{t}", [P, SC], where=l2) for t in range(2)]
        pT2 = [sb(f"pT2_{t}", [SC, P], where=l2) for t in range(2)]
        sm2 = [sb(f"sm2_{t}", [P, 4], where=l2) for t in range(2)]
        l2.close()
        upto2.close()

        late = ExitStack()
        g3 = sb("g3", [P, KT, B, KEYS3], where=late)
        v3 = sb("v3", [P, B, HP, D], where=late)
        gb3 = sb("gb3", [P, KT, H3], where=late)
        vb3 = sb("vb3", [H3, D], where=late)
        bt3 = sb("bt3", [1, B, KEYS3], where=late)
        bb3 = sb("bb3", [1, H3], where=late)
        one3 = sb("one3", [1, P], where=late)
        prep = ExitStack()
        bun = [sb(f"bun{t}", [P, BUN], where=prep) for t in range(2)]
        kh = sb("kh", [P, C], where=prep)
        vh = sb("vh", [P, C], where=prep)
        prep.close()
        at3 = ExitStack()
        hn = [sb(f"hn{t}", [P, D], where=at3) for t in range(2)]
        hT = [sb(f"hT_{t}", [P, KT, P], where=at3) for t in range(2)]
        st3 = sb("st3", [P, 6], where=at3)
        mv3 = [sb(f"mv3_{t}", [P, 4], where=at3) for t in range(2)]
        mx3 = [sb(f"mx3_{t}", [P, H3], where=at3) for t in range(2)]
        sm3 = [sb(f"sm3_{t}", [P, H3], where=at3) for t in range(2)]
        p3 = [sb(f"p3_{t}", [P, KEYS3 + H3], where=at3) for t in range(2)]
        pT3 = [sb(f"pT3_{t}", [P, 4, P], where=at3) for t in range(2)]
        pb3 = sb("pb3", [H3, P], where=at3)
        xb3 = [sb(f"xb3_{t}", [P, D], where=at3) for t in range(2)]
        at3.close()
        late.close()

        fin = ExitStack()
        m3 = dict(wa=sb("m3a", [P, KT, F], where=fin), wb=sb("m3b", [P, FT, D], where=fin),
                  h=sb("hid3", [P, FT, CH], where=fin), xb=[sb(f"xbm3_{t}", [P, D], where=fin) for t in range(2)])
        xc3 = sb("xc3", [P, KT, CH], where=fin)
        hnm = [sb(f"hnm{t}", [P, D], where=fin) for t in range(2)]
        stm = sb("stm", [P, 6], where=fin)
        mvm = [sb(f"mvm{t}", [P, 4], where=fin) for t in range(2)]
        fin.close()

        dma_x, dma_xT, dma_c, dma_w0, dma_w1, dma_w2, dma_m, dma_k, dma_m1, dma_m3 = [
            sem(f"loaded_{n}") for n in ("x", "xT", "ctx", "w0", "w1", "w2", "masks", "consts", "mlp1", "mlp3")]
        dma_bun = [[sem(f"loaded_heads{a}_{t}") for t in range(2)] for a in range(2)]
        dma_out = sem("stored_out")

        ppe = Steps(sem, "prep_pe", ["k0", "v0", "v1"])
        pdv = Steps(sem, "prep_dve", ["ones", "k0", "v0", "v1", "m1"])
        ppo = Steps(sem, "prep_pool", ["ones"])

        def tallies(stage, owned, **per):
            return {k: Tally(sem, f"{stage}_{k}", n, owned) for k, n in per.items()}

        own_pe, own_act, own_dve, own_pool = [], [], [], []
        E0 = tallies("l0_pe", own_pe, q=1, scores=4, turned_a=4, turned_b=4, heads=4, heads_turned=2, projected=2, normed_turned=2)
        A0 = tallies("l0_act", own_act, weights=4, high=4, heads_turned=2, normed_turned=2)
        D0t = tallies("l0_dve", own_dve, q=1, q_high=1, q_low=1, masked=4, maxima=4, low=4, inverse=2, heads=2, sums=2, stats=2,
                      mean=2, eps=2, normed=2)
        split0 = Tally(sem, "l0_values_split", 4, own_dve)
        G0s = tallies("l0_pool", own_pool, k_high=1, k_low=1, values=1, shifted=4, root=2, scaled=2, rows=2, bias=2)
        E1 = tallies("l1_pe", own_pe, k_ctx=1, q=1, k=1, v=1, scores=16, turned=16, turned_ctx=16, heads=16, heads_turned=2,
                     projected=2, normed_turned=2)
        A1 = tallies("l1_act", own_act, q_high=1, k_high=1, v_high=1, q_mid=1, k_mid=1, v_mid=1, weights=16, high_own=16, high=16,
                     heads_turned=2, normed_turned=2)
        D1t = tallies("l1_dve", own_dve, ctx_split=4, k_ctx=1, k_ctx_split=4, x=1, q=1, k=1, q_rest=1, k_rest=1, v_rest=1,
                      maxima=16, low=16, inverse=2, heads=2, sums=2, squares=2, mean=2, normed=2)
        G1 = tallies("l1_pool", own_pool, ones=1, rows=4, q_low=1, k_low=1, v_low=1, values=1, mask=1, bias=2, root=2)
        dma_part = [sem(f"stored_parts_{t}") for t in range(2)]
        dma_stack = [sem(f"loaded_stacks_{t}") for t in range(2)]

        hs, os_ = [f"h{f}" for f in range(FT)], [f"o{t}" for t in range(QC)]
        em = [Steps(sem, "mlp1_pe", hs + os_), Steps(sem, "mlp3_pe", [f"x{t}" for t in range(QC)] + hs + os_)]
        am = [Steps(sem, "mlp1_act", hs), Steps(sem, "mlp3_act", [f"x{t}" for t in range(QC)] + hs)]
        ln4 = [n % t for t in range(QC) for n in ("bn%d", "mv%d", "eps%d", "xn%d")]
        dm = [Steps(sem, "mlp1_dve", os_), Steps(sem, "mlp3_dve", ln4 + os_)]
        gm = [Steps(sem, "mlp1_pool", [f"xb{t}" for t in range(QC)]),
              Steps(sem, "mlp3_pool", [f"rs{t}" for t in range(QC)] + [f"xb{t}" for t in range(QC)])]

        pe2p = Steps(sem, "l2_prep_pe", ["k", "kq", "v", "vo"])
        dv2p = Steps(sem, "l2_prep_dve", ["k", "kq", "v", "vo"])
        two = lambda *names: [n % t for n in names for t in range(2)]
        e2 = Steps(sem, "l2_pe", two("xt%d", "s%d", "pt%d", "o%d"))
        a2 = Steps(sem, "l2_act", two("xt%d", "exp%d", "pt%d"))
        d2 = Steps(sem, "l2_dve", [n % t for t in range(2) for n in ("m%d", "max%d")]
                   + [n % t for t in range(2) for n in ("s%d", "sum%d")] + two("y%d"))
        vbz = [sem(f"bias_values_zero{a}") for a in range(2)]
        g2 = Steps(sem, "l2_pool", two("x%d"))

        ep = [Steps(sem, f"heads{a}_pe", [n % t for t in range(2) for n in ("k%d", "g%d", "b%d", "v%d", "w%d", "r%d")])
              for a in range(2)]
        dp = [Steps(sem, f"heads{a}_dve", [n % t for t in range(2) for n in ("k%d", "w%d", "m%d", "vb%d")])
              for a in range(2)]
        ap_ = [Steps(sem, f"heads{a}_act", [n % t for t in range(2) for n in ("g%d", "b%d", "v%d", "w%d")])
               for a in range(2)]

        E3 = tallies("attn_pe", own_pe, normed=2, scores=2, turned_a=2, turned_b=2, turned_bias=2, out=2)
        D3t = tallies("attn_dve", own_dve, stats=2, mean=2, eps=2, normed=2, max=2, max_bias=2, shifted=2, shifted_bias=2,
                      sum=2, sum_bias=2, inverse=2, weight_bias=2, rows=2)
        A3 = tallies("attn_act", own_act, normed=2, weights=2, copied_a=2, copied_b=2, copied_bias=2)
        G3 = tallies("attn_pool", own_pool, root=2, bias=2, weights=2)

        def attn_end(t, a):
            return t.end((a + 1) * B)

        def settle(eng):
            eng.nop(nofuse=True)

        q_parts = nc.dram_tensor("q_parts", (3 * KT, P, B, S), BF16, kind="Internal").ap()
        k_parts = nc.dram_tensor("k_parts", (3 * KT, P, B, KEYS1), BF16, kind="Internal").ap()

        x_rows = io["x"].rearrange("b (t p) d -> p (b t) d", p=P)
        out_rows = out.rearrange("b (t p) d -> p (b t) d", p=P)

        block = ctx.enter_context(nc.Block())

        def tail0(slot, first, after):
            if slot % 2 == 0:
                of = dict(sums=slot // 2 - 2, heads=slot // 2 - 1)
            else:
                of = dict(turned=slot // 2 - 2, projected=slot // 2 - 1)
            return {step: k for step, k in of.items() if not (first and k < 0) and not (after and k >= 0)}

        def unit1(u):
            v = u % 8
            return u // 8, v // 4, (v // 2) % 2, v % 2

        def spare1(u, kt):
            return ps[:, 2 * (u % 2) + kt, KEYS1:KEYS1 + P]

        HEADS_SLOTS = ((1, -1), (9, 0))
        TO_PROJECT, TO_NORMED = 2, 5

        def tail1(u, first):
            out = {}
            for at, k in HEADS_SLOTS:
                if not (first and k < 0):
                    out.update({"heads": k} if u == at else {"project": k} if u == at + TO_PROJECT else
                               {"free": k} if u == at + TO_PROJECT + 2 else {"normed": k} if u == at + TO_NORMED else {})
            return out

        def head1(u, e):
            _, kt, par, jp = unit1(u)
            return 8 * kt + 2 * (2 * jp + e) + par

        @block.sync
        def _(sp):
            sp.dma_start(cT[:, :, :], io["ctxT"]).then_inc(dma_c, 16)
            sp.dma_start(w0[:, :], io["w0"]).then_inc(dma_w0, 16)
            sp.dma_start(cst[:, :], io["const"]).then_inc(dma_k, 16)
            sp.dma_start(vec[:, :], io["vecs"]).then_inc(dma_k, 16)
            sp.dma_start(alpha[:, :], io["alpha"].partition_broadcast(P)).then_inc(dma_k, 16)
            sp.dma_start(xT[:, :, :], io["xT"]).then_inc(dma_xT, 16)
            sp.dma_start(row1[:, :, :], io["rows"][0:len(ROWS) - 3, :].partition_broadcast(P)).then_inc(dma_k, 16)
            sp.dma_start(row3[:, :, :], io["rows"][len(ROWS) - 3:, :].partition_broadcast(P)).then_inc(dma_k, 16)
            sp.dma_start(xr[:, :, :], x_rows).then_inc(dma_x, 16)
            sp.dma_start(mask0[:, :, :], io["mask0"].rearrange("b o (t p) k -> p (b o t) k", p=P)).then_inc(dma_m, 16)
            sp.dma_start(maski[:, :], io["mask1"].partition_broadcast(P)).then_inc(dma_m, 16)
            sp.dma_start(w1[:, :], io["w1"]).then_inc(dma_w1, 16)
            sp.dma_start(w2[:, :], io["w2"]).then_inc(dma_w2, 16)
            def wait(t, i, k=0):
                sp.wait_ge(t.sem, t.at(i, k))
                settle(sp)

            def store1(i, s):
                for kind, d, w in (("q", q_parts, S), ("k", k_parts, KEYS1)):
                    wait(G1[f"{kind}_low"], i)
                    sp.dma_start(d[:, :, bass.ds(i, 1), 0:w].rearrange("c p o n -> p c (o n)"),
                                 pt1[kind][s][:, :, :, :].rearrange("p c k n -> p (c k) n")).then_inc(dma_part[s], 16)

            def load1(i, s, j):
                wait(E1["scores"], i, -17)
                sp.wait_ge(dma_part[s], 32 * (j + 1))
                settle(sp)
                for n, (a, b) in enumerate(STACKED):
                    rows = slice(n * D1, (n + 1) * D1)
                    for o, d, c, w in ((qs1, q_parts, a, S), (ks1, k_parts, b, KEYS1)):
                        sp.dma_start(o[s][rows, :, :], d[KT * c:KT * (c + 1), :, bass.ds(i, 1), 0:w].rearrange(
                            "k (h d) o n -> d (k h) (o n)", d=D1)).then_inc(dma_stack[s], 16)

            for s in range(2):
                store1(s, s)
            for s in range(2):
                store1(2 + s, s)
            for s in range(2):
                load1(s, s, 0)
            with sp.Fori(2, B // 2) as j:
                for s in range(2):
                    store1(2 * j + s, s)
            with sp.Fori(1, B // 2) as j:
                for s in range(2):
                    load1(2 * j + s, s, j)
            for t in (E1["v"], D1t["x"]):
                sp.wait_ge(t.sem, t.end(B))
            sp.dma_start(m1["wa"][:, :, :], io["m1a"]).then_inc(dma_m1, 16)
            sp.dma_start(m1["wb"][:, :, :], io["m1b"]).then_inc(dma_m1, 16)
            for a in range(2):
                if a == 0:
                    sp.wait_ge(d2.sem, d2.end(B))
                    sp.wait_ge(e2.sem, e2.end(B))
                else:
                    sp.wait_ge(D3t["rows"].sem, attn_end(D3t["rows"], 0))
                with sp.Fori(0, HP) as i:
                    for t in range(2):
                        sp.wait_ge(ep[a].sem, ep[a].prev(i, f"r{t}"))
                        settle(sp)
                        sp.wait_ge(ap_[a].sem, ap_[a].prev(i, f"v{t}"))
                        settle(sp)
                        sp.dma_start(bun[t][:, :], io[f"heads{a}"][bass.ds(2 * i + t, 1), :, :].rearrange(
                            "o p n -> p (o n)")).then_inc(dma_bun[a][t], 16)
            sp.wait_ge(D3t["rows"].sem, attn_end(D3t["rows"], 1))
            sp.dma_start(m3["wa"][:, :, :], io["m3a"]).then_inc(dma_m3, 16)
            sp.dma_start(m3["wb"][:, :, :], io["m3b"]).then_inc(dma_m3, 16)
            sp.wait_ge(dm[1].sem, dm[1].end(NCH))
            sp.dma_start(out_rows, xr[:, :, :]).then_inc(dma_out, 16)
            sp.wait_ge(dma_out, 16)

        @block.tensor
        def _(pe):
            mm, tr = nc.tensor.matmul, nc.tensor.transpose
            for s in [ppe, pe2p, e2] + em + ep:
                pe.sem_inc(s.sem, s.per)
            for s in own_pe:
                pe.sem_inc(s.sem, s.seed)

            pe.wait_ge(dma_c, 16)
            pe.wait_ge(dma_w0, 16)
            for mt in range(KT):
                for kt in range(KT):
                    last = mm(ps[:, mt, :], wt(w0, W0, "wk")[:, kt, mt * P:(mt + 1) * P], cT[:, kt, :],
                              start=kt == 0, stop=kt == KT - 1)
            last.then_inc(ppe.sem, ppe.did("k0"))
            for b in range(B):
                for hf in range(2):
                    for kt in range(KT):
                        last = mm(ps[HALF * hf:HALF * (hf + 1), 2, b * SC:(b + 1) * SC],
                                  cT[:, kt, b * SC:(b + 1) * SC], wt(w0, W0, "wv")[:, kt, :],
                                  start=kt == 0, stop=kt == KT - 1)
            last.then_inc(ppe.sem, ppe.did("v0"))
            pe.wait_ge(dma_w1, 16)
            for b in range(B):
                for hf in range(2):
                    for kt in range(KT):
                        last = mm(ps[HALF * hf:HALF * (hf + 1), 3 + b // 2, (b % 2) * D:(b % 2 + 1) * D],
                                  cT[:, kt, b * SC:(b + 1) * SC], wt(w1, W1, "wv")[:, kt, :],
                                  start=kt == 0, stop=kt == KT - 1)
            last.then_inc(ppe.sem, ppe.did("v1"))
            pe.wait_ge(pdv.sem, pdv.now(0, "v1"))
            pe.wait_ge(dma_k, 80)
            pe.wait_ge(dma_xT, 16)

            def wait(t, i, k=0):
                pe.wait_ge(t.sem, t.at(i, k))

            def queries0(i):
                for mt in range(KT):
                    for kt in range(KT):
                        last = mm(ps[:, 7, mt * S:(mt + 1) * S], wt(w0, W0, "wq")[:, kt, mt * P:(mt + 1) * P],
                                  xT[:, kt, bass.ds(i * S, S)], start=kt == 0, stop=kt == KT - 1)
                last.then_inc(E0["q"].sem, 1)

            def scores0(i, u):
                t, hf = u // 2, u % 2
                if u == 0:
                    wait(D0t["q_low"], i)
                    wait(G0s["k_low"], i)
                wait(D0t["masked"], i, u - 2)
                for kt in range(KT):
                    for j in (2 * hf, 2 * hf + 1):
                        for n, (a, b) in enumerate(PARTS):
                            last = mm(ps[:, j, kt * 256:(kt + 1) * 256], qp0[a][32 * j:32 * j + 32, kt, t * P:(t + 1) * P],
                                      kp0[b][32 * j:32 * j + 32, kt, :], start=n == 0, stop=n == 2)
                last.then_inc(E0["scores"].sem, 1)

            def turn0(i, u):
                wait(A0["weights"], i, u)
                wait(D0t["low"], i, u - 1)
                for half, name in ((0, "a"), (1, "b")):
                    for n in range(4):
                        blk = 4 * half + n
                        last = tr(ps[:, 4 + half, n * P:(n + 1) * P], p0[u][:, blk * P:(blk + 1) * P], ident)
                    last.then_inc(E0[f"turned_{name}"].sem, 1)

            def heads0(i, k):
                if k % 2 == 0:
                    wait(D0t["heads"], i, k // 2 - 1)
                if k == 0:
                    wait(G0s["values"], i)
                wait(D0t["low"], i, k)
                for n in range(8):
                    blk = 8 * (k % 2) + n
                    g = 4 * ((blk // 2) % 2) + blk // 4
                    for w, parts in ((ph0, 3), (pl0, 2)):
                        for c in range(parts):
                            last = mm(ps[:, 6, blk * 18:blk * 18 + 18], w[k % 2][:, n, :], vb0[:, c, g, :, :],
                                      start=w is ph0 and c == 0, stop=w is pl0 and c == 1)
                last.then_inc(E0["heads"].sem, 1)

            def turn_rows0(t, i, k, rows, ready, before):
                wait(ready, i, k)
                if before:
                    wait(before, i, k - 1)
                for kt in range(KT):
                    last = tr(ps[:, 7, kt * P:(kt + 1) * P], rows[:, kt * P:(kt + 1) * P], ident)
                last.then_inc(t.sem, 1)

            def slot0(i, u, first=False, final=False, after=False):
                k = tail0(u, first, after)
                if not after:
                    turn0(i, u)
                if "turned" in k:
                    if u == 1 and not (final or after):
                        wait(D0t["q"], i + 1)
                    turn_rows0(E0["normed_turned"], i, k["turned"], xn0[k["turned"] % 2], D0t["normed"], None)
                if not (first and u == 0) and not (after and u):
                    heads0(i, u - 1)
                if "projected" in k:
                    turn_rows0(E0["heads_turned"], i, k["projected"], ao0, D0t["heads"], A0["normed_turned"])
                if not after and not (final and u >= 1):
                    scores0(i + (u >= 1), (u + 3) % 4)
                if "projected" in k:
                    wait(A0["heads_turned"], i, k["projected"])
                    for kt in range(KT):
                        last = mm(ps[:, 7, 0:D], aoT0[:, kt, :], wt(w0, W0, "wo")[:, kt, :], start=kt == 0, stop=kt == KT - 1)
                    last.then_inc(E0["projected"].sem, 1)
                if u == 0 and not (final or after):
                    if not first:
                        wait(D0t["sums"], i, -2)
                    queries0(i + 1)

            queries0(0)
            scores0(0, 0)
            scores0(0, 1)
            scores0(0, 2)
            for u in range(4):
                slot0(0, u, first=True)
            with pe.Fori(1, B - 1) as i:
                for u in range(4):
                    slot0(i, u)
            for u in range(4):
                slot0(B - 1, u, final=True)
            for u in range(4):
                slot0(B, u, after=True)

            def project1(i, s):
                def projected(name, lhs_rhs):
                    for half in range(2):
                        for kt in range(KT):
                            lhs, rhs = lhs_rhs(half, kt)
                            last = mm(ps[:, 3 * s + "qkv".index(name), half * S:(half + 1) * S], lhs, rhs,
                                      start=kt == 0, stop=kt == KT - 1)
                    last.then_inc(E1[name].sem, 1)

                own_x = lambda kt: xT[:, kt, bass.ds(i * S, S)]
                wait(D1t["q"], i, -2)
                projected("q", lambda mt, kt: (wt(w1, W1, "wq")[:, kt, mt * P:(mt + 1) * P], own_x(kt)))
                wait(D1t["k"], i, -2)
                projected("k", lambda mt, kt: (wt(w1, W1, "wk")[:, kt, mt * P:(mt + 1) * P], own_x(kt)))
                wait(D1t["v_rest"], i, -2)
                wait(D1t["x"], i)
                projected("v", lambda t, kt: (xb1T[s][:, kt, t * P:(t + 1) * P], wt(w1, W1, "wv")[:, kt, :]))

            def scores1(i, s, j, u):
                t, kt, par, jp = unit1(u)
                if u == 0:
                    pe.wait_ge(dma_stack[s], STACK_DMAS * 16 * (j + 1))
                    wait(G1["mask"], i)
                wait(A1["weights"], i, u - 2)
                for e in range(2):
                    h = head1(u, e)
                    o, q = ps[:, 2 * (u % 2) + e, :], qs1[s][:, h, t * P:(t + 1) * P]
                    if e == 0:
                        mm(o[:, 0:KEYS1], q, ks1[s][:, h, :], start=True, stop=True)
                    else:
                        mm(o[:, 0:SC], q, ks1[s][:, h, S:KEYS1], start=True, stop=True)
                        last = mm(o[:, SC:KEYS1], q, ks1[s][:, h, 0:S], start=True, stop=True)
                last.then_inc(E1["scores"].sem, 1)

            def turn1(i, u):
                wait(A1["weights"], i, u)
                wait(D1t["low"], i, u - 2)
                for k, blk in enumerate((0, 1, 3, 4)):
                    last = tr(ps[:, 4 + u % 2, k * P:(k + 1) * P], p1[u % 2][:, blk * P:(blk + 1) * P], ident)
                last.then_inc(E1["turned"].sem, 1)

            def turn_ctx1(i, u):
                wait(D1t["low"], i, u - 1)
                tr(ps[:, 6, 0:P], p1[u % 2][:, 2 * P:3 * P], ident).then_inc(E1["turned_ctx"].sem, 1)

            def heads1(i, s, u):
                if u == 0:
                    wait(D1t["heads"], i, -1)
                    wait(G1["values"], i)
                if u == 8:
                    wait(D1t["heads"], i, 0)
                wait(D1t["low"], i, u)
                for e in range(2):
                    h = head1(u, e)
                    o = ps[:, 7, h * (D1 + 1):(h + 1) * (D1 + 1)]
                    for blk in range(3):
                        k = 4 if blk == 2 else 2 * e + blk
                        for w, parts in ((ph1, 3), (pl1, 2)):
                            for c in range(parts):
                                last = mm(o, w[u % 2][:, k, :], vt1[s][:, c, blk, h, :], start=blk == 0 and w is ph1 and c == 0,
                                          stop=blk == 2 and w is pl1 and c == 1)
                last.then_inc(E1["heads"].sem, 1)

            def turn_heads1(i, k, u):
                wait(D1t["heads"], i, k)
                for kt in range(KT):
                    last = tr(spare1(u, kt), ao1[:, kt * P:(kt + 1) * P], ident)
                last.then_inc(E1["heads_turned"].sem, 1)

            def heads_projected1(i, k, u):
                wait(A1["heads_turned"], i, k)
                for half in range(KT):
                    for kt in range(KT):
                        last = mm(spare1(u, half), aoT1[:, kt, :], wt(w1, W1, "wo")[:, kt, half * P:(half + 1) * P],
                                  start=kt == 0, stop=kt == KT - 1)
                last.then_inc(E1["projected"].sem, 1)

            def turn_normed1(i, k, u):
                wait(D1t["normed"], i, k)
                for kt in range(KT):
                    last = tr(spare1(u, kt), n1[:, kt * P:(kt + 1) * P], ident)
                last.then_inc(E1["normed_turned"].sem, 1)

            def batch1(i, s, j, first=False, final=False):
                for u in range(16):
                    turn1(i, u)
                    tail = tail1(u, first)
                    if "heads" in tail:
                        turn_heads1(i, tail["heads"], u)
                    if "project" in tail:
                        heads_projected1(i, tail["project"], u)
                    if "free" in tail:
                        wait(D1t["sums"], i, tail["free"])
                    if "normed" in tail:
                        turn_normed1(i, tail["normed"], u)
                    if u + 2 < 16:
                        scores1(i, s, j, u + 2)
                    elif not final:
                        scores1(i + 1, 1 - s, j + s, u - 14)
                    turn_ctx1(i, u)
                    if u:
                        heads1(i, s, u - 1)
                heads1(i, s, 15)

            for t in (A0["normed_turned"], D0t["normed"], D0t["heads"]):
                pe.wait_ge(t.sem, t.end(B))
            for mt in range(KT):
                for kt in range(KT):
                    last = mm(ps[:, 6 + mt, :], wt(w1, W1, "wk")[:, kt, mt * P:(mt + 1) * P], cT[:, kt, :],
                              start=kt == 0, stop=kt == KT - 1)
            last.then_inc(E1["k_ctx"].sem, 1)
            with pe.Fori(0, B // 2) as j:
                for s in range(2):
                    project1(2 * j + s, s)
            for t in (D1t["v_rest"], G1["v_low"]):
                pe.wait_ge(t.sem, t.end(B))
            wait(D1t["k_ctx"], 0, 0)
            scores1(0, 0, 0, 0)
            scores1(0, 0, 0, 1)
            batch1(0, 0, 0, first=True)
            batch1(1, 1, 0)
            with pe.Fori(1, B // 2 - 1) as j:
                for s in range(2):
                    batch1(2 * j + s, s, j)
            batch1(B - 2, 0, B // 2 - 1)
            batch1(B - 1, 1, B // 2 - 1, final=True)
            turn_heads1(B, -1, 1)
            heads_projected1(B, -1, 1 + TO_PROJECT)
            turn_normed1(B, -1, 1 + TO_NORMED)

            def mlp_products(m, w, loaded, cols):
                pe.wait_ge(loaded, 32)
                with pe.Fori(0, NCH) as i:
                    if m:
                        for t in range(QC):
                            pe.wait_ge(dm[1].sem, dm[1].now(i, f"xn{t}"))
                            pe.wait_ge(am[1].sem, am[1].now(i, f"x{t - 2}") if t >= 2 else am[1].prev(i, f"x{t + 2}"))
                            for kt in range(KT):
                                last = tr(ps[:, 4 + t % 2, kt * P:(kt + 1) * P], hnm[t % 2][:, kt * P:(kt + 1) * P], ident)
                            last.then_inc(em[1].sem, em[1].did(f"x{t}"))
                        pe.wait_ge(am[1].sem, am[1].now(i, f"x{QC - 1}"))
                    for ft in range(FT):
                        pe.wait_ge(am[m].sem, am[m].now(i, f"h{ft - 2}") if ft >= 2 else am[m].prev(i, f"h{ft + 6}"))
                        for kt in range(KT):
                            last = mm(ps[:, ft % 2, :], w["wa"][:, kt, ft * P:(ft + 1) * P], cols(i, kt),
                                      start=kt == 0, stop=kt == KT - 1)
                        last.then_inc(em[m].sem, em[m].did(f"h{ft}"))
                    for t in range(QC):
                        pe.wait_ge(am[m].sem, am[m].now(i, f"h{FT - 1}"))
                        pe.wait_ge(dm[m].sem, dm[m].now(i, f"o{t - 2}") if t >= 2 else dm[m].prev(i, f"o{t + 2}"))
                        for ft in range(FT):
                            last = mm(ps[:, 2 + t % 2, 0:D], w["h"][:, ft, t * P:(t + 1) * P], w["wb"][:, ft, :],
                                      start=ft == 0, stop=ft == FT - 1)
                        last.then_inc(em[m].sem, em[m].did(f"o{t}"))

            pe.wait_ge(A1["normed_turned"].sem, A1["normed_turned"].end(B))
            pe.wait_ge(D1t["normed"].sem, D1t["normed"].end(B))
            mlp_products(0, m1, dma_m1, lambda i, kt: nT[:, kt, bass.ds(i * CH, CH)])

            pe.wait_ge(dma_w2, 16)
            pe.wait_ge(dm[0].sem, dm[0].end(NCH))
            pe.wait_ge(am[0].sem, am[0].end(NCH))
            for k, name in ((0, "wkT"), (1, "wvT")):
                for mt in range(KT):
                    for kt in range(KT):
                        last = mm(ps[:, 2 * k + mt, :], wt(w2, W2, name)[:, kt, mt * P:(mt + 1) * P], cT[:, kt, :],
                                  start=kt == 0, stop=kt == KT - 1)
                if k == 0:
                    last.then_inc(pe2p.sem, pe2p.did("k"))
                    pe.wait_ge(dv2p.sem, dv2p.now(0, "k"))
                    for mt in range(KT):
                        for kt in range(KT):
                            last = mm(ps[:, 4 + mt, :], wt(w2, W2, "wq")[:, kt, mt * P:(mt + 1) * P], t2[:, 0, kt, :],
                                      start=kt == 0, stop=kt == KT - 1)
                    last.then_inc(pe2p.sem, pe2p.did("kq"))
            last.then_inc(pe2p.sem, pe2p.did("v"))
            pe.wait_ge(dv2p.sem, dv2p.now(0, "v"))
            for b in range(B):
                for kt in range(KT):
                    last = mm(ps[0:SC, 4 + b // 2, (b % 2) * D:(b % 2 + 1) * D], t2[:, 1, kt, b * SC:(b + 1) * SC],
                              wt(w2, W2, "woT")[:, kt, :], start=kt == 0, stop=kt == KT - 1)
            last.then_inc(pe2p.sem, pe2p.did("vo"))
            pe.wait_ge(dv2p.sem, dv2p.now(0, "vo"))
            with pe.Fori(0, B) as i:
                for t in range(2):
                    pe.wait_ge(g2.sem, g2.now(i, f"x{t}"))
                    pe.wait_ge(a2.sem, a2.prev(i, f"xt{t}"))
                    for kt in range(KT):
                        last = tr(ps[:, t, kt * P:(kt + 1) * P], x2[t][:, kt * P:(kt + 1) * P], ident)
                    last.then_inc(e2.sem, e2.did(f"xt{t}"))
                for t in range(2):
                    pe.wait_ge(a2.sem, a2.now(i, f"xt{t}"))
                    pe.wait_ge(a2.sem, a2.prev(i, f"exp{t}"))
                    for kt in range(KT):
                        last = mm(ps[:, 2 + t, 0:SC], x2T[t][:, kt, :], k2[:, kt, bass.ds(i, 1), :],
                                  start=kt == 0, stop=kt == KT - 1)
                    last.then_inc(e2.sem, e2.did(f"s{t}"))
                for t in range(2):
                    pe.wait_ge(a2.sem, a2.now(i, f"exp{t}"))
                    pe.wait_ge(a2.sem, a2.prev(i, f"pt{t}"))
                    settle(pe)
                    tr(ps[0:SC, 4 + t, 0:P], p2[t][:, :], ident).then_inc(e2.sem, e2.did(f"pt{t}"))
                for t in range(2):
                    pe.wait_ge(a2.sem, a2.now(i, f"pt{t}"))
                    pe.wait_ge(d2.sem, d2.prev(i, f"y{t}"))
                    settle(pe)
                    mm(ps[:, 6 + t, 0:D], pT2[t][:, :], v2[:, bass.ds(i, 1), :], start=True,
                       stop=True).then_inc(e2.sem, e2.did(f"o{t}"))

            def head_products(a):
                with pe.Fori(0, HP) as i:
                    for t in range(2):
                        w = bun[t]
                        wk = w[:, 0:D].rearrange("p (k n) -> p k n", k=KT)
                        wqT, wo = w[:, D:2 * D], w[:, 3 * D:4 * D]
                        wv = w[:, 2 * D:3 * D].rearrange("p (k n) -> p k n", k=KT)
                        bq, bias_k, bias_v = w[:, 4 * D + 1:4 * D + 2], w[:, 4 * D + 3:4 * D + 4], w[:, 4 * D + 4:BUN]
                        older = lambda s, n: s.now(i, n + "0") if t else s.prev(i, n + "1")
                        pe.wait_ge(dma_bun[a][t], 16 * i + 16)
                        pe.wait_ge(dp[a].sem, older(dp[a], "k"))
                        for kt in range(KT):
                            last = mm(ps[:, 0, :], wk[:, kt, :], cT[:, kt, :], start=kt == 0, stop=kt == KT - 1)
                        last.then_inc(ep[a].sem, ep[a].did(f"k{t}"))
                        pe.wait_ge(dp[a].sem, dp[a].now(i, f"k{t}"))
                        pe.wait_ge(ap_[a].sem, older(ap_[a], "g"))
                        for mt in range(KT):
                            last = mm(ps[:, 1 + mt, :], wqT[:, mt * P:(mt + 1) * P], kh[:, :], start=True, stop=True)
                        last.then_inc(ep[a].sem, ep[a].did(f"g{t}"))
                        pe.wait_ge(ap_[a].sem, older(ap_[a], "b"))
                        mm(ps[0:1, 3, :], bq, kh[:, :], start=True, stop=True).then_inc(ep[a].sem, ep[a].did(f"b{t}"))
                        pe.wait_ge(ap_[a].sem, older(ap_[a], "v"))
                        for kt in range(KT):
                            last = mm(ps[:, 4, :], wv[:, kt, :], cT[:, kt, :], start=kt == 0, stop=kt == KT - 1)
                        last.then_inc(ep[a].sem, ep[a].did(f"v{t}"))
                        pe.wait_ge(ap_[a].sem, ap_[a].now(i, f"v{t}"))
                        pe.wait_ge(ap_[a].sem, older(ap_[a], "w"))
                        pe.wait_ge(dp[a].sem, older(dp[a], "w"))
                        for bp in range(4):
                            last = mm(ps[:, 5 + bp // 2, (bp % 2) * D:(bp % 2 + 1) * D], vh[:, bp * P:(bp + 1) * P], wo,
                                      start=True, stop=True)
                        last.then_inc(ep[a].sem, ep[a].did(f"w{t}"))
                        pe.wait_ge(dp[a].sem, older(dp[a], "vb"))
                        mm(ps[0:H3, 7, 0:D], bias_v, wo, start=True, stop=True)
                        for mt in range(KT):
                            mm(ps[:, 7, D + mt:D + mt + 1], wqT[:, mt * P:(mt + 1) * P], bias_k, start=True, stop=True)
                        mm(ps[0:1, 7, D + 4:D + 5], bq, bias_k, start=True, stop=True).then_inc(ep[a].sem, ep[a].did(f"r{t}"))

            def attend(a):
                def wait(t, i, k):
                    pe.wait_ge(t.sem, t.at(i, k + a * B * t.per))

                def turn_normed(i, k):
                    wait(D3t["normed"], i, k)
                    if k >= 2:
                        wait(D3t["shifted_bias"], i, k - 1)
                    elif k == 1:
                        wait(A3["normed"], i, 0)
                    for kt in range(KT):
                        last = tr(ps[:, 6, kt * P:(kt + 1) * P], hn[k % 2][:, kt * P:(kt + 1) * P], ident)
                    last.then_inc(E3["normed"].sem, 1)

                def scores(i, k, ahead=False):
                    t, b = k % 2, i + k // 2
                    wait(A3["normed"], i, 1 if ahead else k)
                    wait(D3t["shifted_bias"], i, k - 1)
                    for kt in range(KT):
                        mm(ps[:, 6, D:D + H3], hT[t][:, kt, :], gb3[:, kt, :], start=kt == 0, stop=False)
                    mm(ps[:, 6, D:D + H3], one3[:, :], bb3[:, :], start=False, stop=True)
                    for c in range(2):
                        for kt in range(KT):
                            mm(ps[:, 2 * t + c, :], hT[t][:, kt, :], g3[:, kt, bass.ds(b, 1), c * 512:(c + 1) * 512],
                               start=kt == 0, stop=False)
                        last = mm(ps[:, 2 * t + c, :], one3[:, :], bt3[:, bass.ds(b, 1), c * 512:(c + 1) * 512],
                                  start=False, stop=True)
                    last.then_inc(E3["scores"].sem, 1)

                def turn(i, k):
                    t = k % 2
                    wait(G3["weights"], i, k)
                    wait(D3t["weight_bias"], i, k)
                    for half, name, copied in ((0, "a", "copied_bias"), (1, "b", "copied_b")):
                        wait(A3[copied], i, k - 1)
                        for n in range(4):
                            blk = 4 * half + n
                            last = tr(ps[:, 4 + half, n * P:(n + 1) * P], p3[t][:, blk * P:(blk + 1) * P], ident)
                        last.then_inc(E3[f"turned_{name}"].sem, 1)
                    wait(A3["copied_a"], i, k)
                    tr(ps[0:H3, 4, 0:P], p3[t][:, KEYS3:KEYS3 + H3], ident).then_inc(E3["turned_bias"].sem, 1)

                def rows_out(i, k, half):
                    o = ps[:, 7, 0:D]
                    if half == 0:
                        wait(D3t["rows"], i, k - 1)
                    wait(A3["copied_" + "ab"[half]], i, k)
                    for n in range(4):
                        mm(o, pT3[half][:, n, :], v3[:, bass.ds(i, 1), 4 * half + n, :], start=half == 0 and n == 0, stop=False)
                    if half:
                        wait(A3["copied_bias"], i, k)
                        mm(o, pb3[:, :], vb3[:, :], start=False, stop=True).then_inc(E3["out"].sem, 1)

                def batch(i, final=False):
                    for k in range(2):
                        if not (final and k):
                            scores(i, k + 1)
                        turn(i, k)
                        rows_out(i, k, 0)
                        if not final:
                            turn_normed(i, k + 2)
                        rows_out(i, k, 1)

                turn_normed(0, 0)
                turn_normed(0, 1)
                scores(0, 0, ahead=True)
                with pe.Fori(0, B - 1) as i:
                    batch(i)
                batch(B - 1, final=True)

            for a in range(2):
                if a == 0:
                    pe.wait_ge(d2.sem, d2.end(B))
                    pe.wait_ge(a2.sem, a2.end(B))
                else:
                    pe.wait_ge(D3t["rows"].sem, attn_end(D3t["rows"], 0))
                    pe.wait_ge(A3["copied_bias"].sem, attn_end(A3["copied_bias"], 0))
                head_products(a)
                pe.wait_ge(dp[a].sem, dp[a].end(HP))
                pe.wait_ge(ap_[a].sem, ap_[a].end(HP))
                attend(a)
            pe.wait_ge(D3t["rows"].sem, attn_end(D3t["rows"], 1))
            pe.wait_ge(A3["copied_bias"].sem, attn_end(A3["copied_bias"], 1))
            mlp_products(1, m3, dma_m3, lambda i, kt: xc3[:, kt, :])

        @block.scalar
        def _(act):
            def copy(o, x, bias=0.0, scale=1.0):
                return nc.scalar.activation(o, x, ACT.Identity, bias=bias, scale=scale)

            def exp(o, x, bias=0.0, scale=1.0):
                return nc.scalar.activation(o, x, ACT.Exp, bias=bias, scale=scale)

            for s in [a2] + am + ap_:
                act.sem_inc(s.sem, s.per)
            for s in own_act:
                act.sem_inc(s.sem, s.seed)
            act.wait_ge(dma_k, 80)

            act.wait_ge(dma_xT, 16)

            def wait(t, i, k=0):
                act.wait_ge(t.sem, t.at(i, k))

            def weights0(i, u):
                wait(G0s["shifted"], i, u)
                exp(p0[u][:, :], p0[u][:, :]).then_inc(A0["weights"].sem, 1)

            def slot0(i, u, first=False, final=False, after=False):
                k = tail0(u, first, after)
                if not after:
                    wait(E0["heads"], i, u - 2)
                    for half, name in ((0, "a"), (1, "b")):
                        wait(E0[f"turned_{name}"], i, u)
                        last = copy(ph0[u % 2][:, 4 * half:4 * half + 4, :], ps[:, 4 + half, :].rearrange("p (k n) -> p k n", k=4),
                                    scale=WHOLE)
                    last.then_inc(A0["high"].sem, 1)
                if "turned" in k:
                    c = k["turned"]
                    wait(E0["normed_turned"], i, c)
                    for kt in range(KT):
                        last = copy(xT[:, kt, bass.ds(i * S + c * P, P)], ps[:, 7, kt * P:(kt + 1) * P],
                                    pvec("L0_beta", kt), pvec("L0_gamma", kt))
                    last.then_inc(A0["normed_turned"].sem, 1)
                if "projected" in k:
                    c = k["projected"]
                    wait(E0["heads_turned"], i, c)
                    wait(E0["projected"], i, c - 1)
                    for kt in range(KT):
                        last = copy(aoT0[:, kt, :], ps[:, 7, kt * P:(kt + 1) * P], bias=pvec("L0_bv", kt))
                    last.then_inc(A0["heads_turned"].sem, 1)
                if not after and not (final and u == 3):
                    weights0(i + (u == 3), (u + 1) % 4)

            weights0(0, 0)
            for u in range(4):
                slot0(0, u, first=True)
            with act.Fori(1, B - 1) as i:
                for u in range(4):
                    slot0(i, u)
            for u in range(4):
                slot0(B - 1, u, final=True)
            for u in range(4):
                slot0(B, u, after=True)

            def parts1(i, s):
                for kind in "qk":
                    wait(D1t[kind], i)
                    copy(pt1[kind][s][:, 0, :, 0:S], t1[kind][s][:, :, :]).then_inc(A1[f"{kind}_high"].sem, 1)
                wait(E1["v"], i)
                copy(vall1[:, 0, bass.ds(2 * i, 2), :, 0:D1], ps[:, 3 * s + 2, :].rearrange("p (t h d) -> p t h d", t=QT_B, h=H1)
                     ).then_inc(A1["v_high"].sem, 1)
                for kind in "qk":
                    wait(D1t[f"{kind}_rest"], i)
                    if kind == "k":
                        copy(pt1[kind][s][:, :, :, S:KEYS1].rearrange("p c k n -> p (c k) n"),
                             pc1[:, :, :, bass.ds(i * SC, SC)].rearrange("p c k n -> p (c k) n"))
                    copy(pt1[kind][s][:, 1, :, 0:S], t1[kind][s][:, :, :]).then_inc(A1[f"{kind}_mid"].sem, 1)
                wait(D1t["v_rest"], i)
                copy(vall1[:, 1, bass.ds(2 * i, 2), :, 0:D1], t1["v"][s][:, :].rearrange("p (t h d) -> p t h d", t=QT_B, h=H1)
                     ).then_inc(A1["v_mid"].sem, 1)

            def weights1(i, u):
                wait(D1t["maxima"], i, u)
                wait(E1["turned_ctx"], i, u - 2)
                for e in range(2):
                    last = exp(p1[u % 2][:, e * KEYS1:(e + 1) * KEYS1], ps[:, 2 * (u % 2) + e, 0:KEYS1],
                               bias=nm1[:, u, e:e + 1])
                last.then_inc(A1["weights"].sem, 1)

            def high1(i, u):
                wait(E1["turned"], i, u)
                wait(E1["heads"], i, u - 2)
                copy(ph1[u % 2][:, 0:4, :], ps[:, 4 + u % 2, :].rearrange("p (k n) -> p k n", k=4), scale=WHOLE
                     ).then_inc(A1["high_own"].sem, 1)
                wait(E1["turned_ctx"], i, u)
                copy(ph1[u % 2][:, 4, :], ps[:, 6, 0:P], scale=WHOLE).then_inc(A1["high"].sem, 1)

            def heads_turned1(i, k, u):
                wait(E1["heads_turned"], i, k)
                for kt in range(KT):
                    last = copy(aoT1[:, kt, :], spare1(u, kt), bias=pvec("L1_bv", kt))
                last.then_inc(A1["heads_turned"].sem, 1)

            def normed_turned1(i, k, u):
                wait(E1["normed_turned"], i, k)
                for kt in range(KT):
                    last = copy(nT[:, kt, bass.ds(i * S + k * P, P)], spare1(u, kt), scale=pvec("L1_norm", kt))
                last.then_inc(A1["normed_turned"].sem, 1)

            def batch1(i, first=False, final=False):
                for u in range(16):
                    if "project" in tail1(u - 1, first):
                        wait(D1t["sums"], i, tail1(u - 1, first)["project"])
                    if not (final and u == 15):
                        weights1(i + (u == 15), (u + 1) % 16)
                    high1(i, u)
                    tail = tail1(u, first)
                    if ("heads" in tail or "normed" in tail) and not (final and u >= 14):
                        wait(D1t["maxima"], i, u + 2)
                    if "heads" in tail:
                        heads_turned1(i, tail["heads"], u)
                    if "normed" in tail:
                        normed_turned1(i, tail["normed"], u)

            for t in (D0t["normed"], G0s["rows"], E0["normed_turned"]):
                act.wait_ge(t.sem, t.end(B))
            wait(D1t["ctx_split"], 0, 3)
            wait(G1["ones"], 0)
            wait(D1t["k_ctx_split"], 0, 3)
            parts1(0, 0)
            parts1(1, 1)
            with act.Fori(1, B // 2) as j:
                act.wait_ge(dma_part[0], 32 * j)
                parts1(2 * j, 0)
                act.wait_ge(dma_part[1], 32 * j)
                parts1(2 * j + 1, 1)
            wait(G1["v_low"], B, -1)
            for s in range(2):
                act.wait_ge(dma_part[s], 32 * (B // 2))
            weights1(0, 0)
            batch1(0, first=True)
            with act.Fori(1, B - 1) as i:
                batch1(i)
            batch1(B - 1, final=True)
            heads_turned1(B, -1, 1)
            normed_turned1(B, -1, 1 + TO_NORMED)

            def mlp_gelu(m, w, func):
                with act.Fori(0, NCH) as i:
                    if m:
                        for t in range(QC):
                            act.wait_ge(em[1].sem, em[1].now(i, f"x{t}"))
                            act.wait_ge(em[1].sem, em[1].prev(i, f"h{FT - 1}"))
                            for kt in range(KT):
                                last = copy(xc3[:, kt, t * P:(t + 1) * P], ps[:, 4 + t % 2, kt * P:(kt + 1) * P],
                                            pvec("lnm_o", kt), pvec("lnm_s", kt))
                            last.then_inc(am[1].sem, am[1].did(f"x{t}"))
                    for ft in range(FT):
                        act.wait_ge(em[m].sem, em[m].now(i, f"h{ft}"))
                        nc.scalar.activation(w["h"][:, ft, :], ps[:, ft % 2, :], func, bias=fvec(m, ft)
                                             ).then_inc(am[m].sem, am[m].did(f"h{ft}"))

            act.wait_ge(E1["normed_turned"].sem, E1["normed_turned"].end(B))
            act.wait_ge(D1t["normed"].sem, D1t["normed"].end(B))
            mlp_gelu(0, m1, ACT.Gelu_apprx_tanh)

            act.wait_ge(dv2p.sem, dv2p.now(0, "vo"))
            with act.Fori(0, B) as i:
                for t in range(2):
                    act.wait_ge(e2.sem, e2.now(i, f"xt{t}"))
                    act.wait_ge(e2.sem, e2.prev(i, f"s{t}"))
                    copy(x2T[t][:, :, :], ps[:, t, 0:D].rearrange("p (k n) -> p k n", k=KT)
                         ).then_inc(a2.sem, a2.did(f"xt{t}"))
                for t in range(2):
                    act.wait_ge(d2.sem, d2.now(i, f"max{t}"))
                    act.wait_ge(d2.sem, d2.prev(i, f"sum{t}"))
                    act.wait_ge(e2.sem, e2.prev(i, f"pt{t}"))
                    exp(p2[t][:, :], ps[:, 2 + t, 0:SC], bias=sm2[t][:, 0:1], scale=SCALE2).then_inc(a2.sem, a2.did(f"exp{t}"))
                for t in range(2):
                    act.wait_ge(e2.sem, e2.now(i, f"pt{t}"))
                    act.wait_ge(e2.sem, e2.prev(i, f"o{t}"))
                    copy(pT2[t][:, :], ps[0:SC, 4 + t, 0:P]).then_inc(a2.sem, a2.did(f"pt{t}"))

            def head_copies(a):
                with act.Fori(0, HP) as i:
                    for t in range(2):
                        act.wait_ge(dma_bun[a][t], 16 * i + 16)
                        act.wait_ge(ep[a].sem, ep[a].now(i, f"g{t}"))
                        for mt in range(KT):
                            last = copy(g3[:, mt, :, bass.ds(i * 2 * SC + t * SC, SC)],
                                        ps[:, 1 + mt, :].rearrange("p (b k) -> p b k", b=B))
                        last.then_inc(ap_[a].sem, ap_[a].did(f"g{t}"))
                        act.wait_ge(ep[a].sem, ep[a].now(i, f"b{t}"))
                        copy(bt3[:, :, bass.ds(i * 2 * SC + t * SC, SC)],
                             ps[0:1, 3, :].rearrange("p (b k) -> p b k", b=B)).then_inc(ap_[a].sem, ap_[a].did(f"b{t}"))
                        act.wait_ge(ep[a].sem, ep[a].now(i, f"v{t}"))
                        act.wait_ge(ep[a].sem, ep[a].now(i, "w0") if t else ep[a].prev(i, "w1"))
                        copy(vh[:, :], ps[:, 4, :], bias=bun[t][:, 4 * D + 2:4 * D + 3]).then_inc(ap_[a].sem, ap_[a].did(f"v{t}"))
                        act.wait_ge(ep[a].sem, ep[a].now(i, f"w{t}"))
                        copy(v3[HALF * t:HALF * (t + 1), 0:B:2, bass.ds(i, 1), :].rearrange("p b o n -> p b (o n)"),
                             ps[0:HALF, 5:7, :].rearrange("p k (c n) -> p (k c) n", c=2)).then_inc(ap_[a].sem, ap_[a].did(f"w{t}"))

            def attend(a):
                def wait(t, i, k):
                    act.wait_ge(t.sem, t.at(i, k + a * B * t.per))

                def normed(i, k):
                    wait(E3["normed"], i, k)
                    wait(E3["scores"], i, k - 2)
                    for kt in range(KT):
                        last = copy(hT[k % 2][:, kt, :], ps[:, 6, kt * P:(kt + 1) * P], pvec(f"ln{a + 1}_o", kt),
                                    pvec(f"ln{a + 1}_s", kt))
                    last.then_inc(A3["normed"].sem, 1)

                def weights(i, k):
                    wait(D3t["shifted_bias"], i, k)
                    exp(p3[k % 2][:, :], p3[k % 2][:, :], scale=SCALE3).then_inc(A3["weights"].sem, 1)

                def copied(i, k):
                    for half, name in ((0, "a"), (1, "b")):
                        wait(E3[f"turned_{name}"], i, k)
                        wait(E3["out"], i, k - 1)
                        copy(pT3[half][:, :, :], ps[:, 4 + half, :].rearrange("p (k n) -> p k n", k=4)
                             ).then_inc(A3[f"copied_{name}"].sem, 1)
                    wait(E3["turned_bias"], i, k)
                    copy(pb3[:, :], ps[0:H3, 4, 0:P]).then_inc(A3["copied_bias"].sem, 1)

                def batch(i, final=False):
                    for k in range(2):
                        copied(i, k)
                        if not (final and k):
                            weights(i, k + 1)
                        if not final:
                            normed(i, k + 2)

                normed(0, 0)
                normed(0, 1)
                weights(0, 0)
                with act.Fori(0, B - 1) as i:
                    batch(i)
                batch(B - 1, final=True)

            for a in range(2):
                if a == 0:
                    act.wait_ge(e2.sem, e2.end(B))
                    act.wait_ge(d2.sem, d2.end(B))
                else:
                    act.wait_ge(E3["out"].sem, attn_end(E3["out"], 0))
                    act.wait_ge(D3t["rows"].sem, attn_end(D3t["rows"], 0))
                head_copies(a)
                act.wait_ge(dp[a].sem, dp[a].end(HP))
                act.wait_ge(ep[a].sem, ep[a].end(HP))
                attend(a)
            act.wait_ge(E3["out"].sem, attn_end(E3["out"], 1))
            act.wait_ge(D3t["rows"].sem, attn_end(D3t["rows"], 1))
            mlp_gelu(1, m3, ACT.Gelu)

        @block.vector
        def _(dve):
            v = nc.vector
            for s in [pdv, dv2p, d2] + dm + dp:
                dve.sem_inc(s.sem, s.per)
            for s in own_dve:
                dve.sem_inc(s.sem, s.seed)

            def step(s, i, name, ins):
                ins.then_inc(s.sem, s.did(name))
                dve.wait_ge(s.sem, s.now(i, name))

            step(pdv, 0, "ones", v.memset(ones[:, :], 1.0))
            dve.wait_ge(dma_k, 80)
            dve.wait_ge(ppe.sem, ppe.now(0, "k0"))
            for mt in range(KT):
                for j in range(4):
                    last = v.tensor_scalar(kbd[:, mt, :, j * SC:(j + 1) * SC], ps[:, mt, :].rearrange("p (b k) -> p b k", b=B),
                                           pvec("L0_bk", mt), const("quarter", j), ALU.add, ALU.mult)
            last.then_inc(pdv.sem, pdv.did("k0"))
            dve.wait_ge(ppe.sem, ppe.now(0, "v0"))
            for hf in range(2):
                v.tensor_scalar(vbd[:, :, hf, 0:D0], ps[:, 2, :].rearrange("p (g d) -> p g d", d=D0),
                                const("half", hf), None, ALU.mult)
                last = v.tensor_scalar(vbd[:, :, hf, D0:D0 + 1], ones[:, 0:B * G0].unsqueeze(2), const("half", hf), None, ALU.mult)
            last.then_inc(pdv.sem, pdv.did("v0"))
            dve.wait_ge(ppe.sem, ppe.now(0, "v1"))
            for e in range(2):
                heads = vc1[:, :, :, :].rearrange("p b (g e r) d -> p (b g) e r d", e=2, r=2)[:, :, e]
                v.tensor_scalar(heads[:, :, :, D1:D1 + 1], ones[:, 0:B * H1 // 2].rearrange("p (g r o) -> p g r o", r=2, o=1),
                                const("half", e), None, ALU.mult)
                last = v.tensor_scalar(heads[:, :, :, 0:D1],
                                       ps[:, 3:7, :].rearrange("p k (g e r d) -> p (k g) e r d", e=2, r=2, d=D1)[:, :, e],
                                       const("half", e), None, ALU.mult)
            last.then_inc(pdv.sem, pdv.did("v1"))
            dve.wait_ge(dma_m, 32)
            v.tensor_scalar(mask1[:, :], maski[:, :], 0.0, MASKED, ALU.is_equal, ALU.mult).then_inc(pdv.sem, pdv.did("m1"))

            def wait(t, i, k=0):
                dve.wait_ge(t.sem, t.at(i, k))

            def own(t, i, k, ins):
                ins.then_inc(t.sem, 1)
                dve.wait_ge(t.sem, t.at(i, k))

            dve.wait_ge(pdv.sem, pdv.now(0, "v0"))
            for c in range(3):
                if c < 2:
                    own(split0, 0, 2 * c, v.tensor_copy(vp0[:, c, :, :, :], vbd[:, :, :, :]))
                    rest = vp0[:, 2, :, :, :] if c else vbd[:, :, :, :]
                    own(split0, 0, 2 * c + 1, v.tensor_tensor(rest, vbd[:, :, :, :], vp0[:, c, :, :, :], ALU.subtract))

            def queries0(i):
                wait(E0["q"], i)
                for mt in range(KT):
                    last = v.tensor_scalar(q0[:, mt, :], ps[:, 7, mt * S:(mt + 1) * S], pvec("L0_bq", mt), SCALE0, ALU.add, ALU.mult)
                own(D0t["q"], i, 0, last)

            def queries_parts0(i):
                wait(E0["scores"], i, -1)
                own(D0t["q_high"], i, 0, v.tensor_copy(qp0[0][:, :, :], q0[:, :, :]))
                v.tensor_tensor(qp0[1][:, :, :], q0[:, :, :], qp0[0][:, :, :].bitcast(F32), ALU.subtract).then_inc(D0t["q_low"].sem, 1)

            def maxima0(i, u):
                t, hf = u // 2, u % 2
                wait(E0["scores"], i, u)
                wait(E0["turned_b"], i, u - 4)
                p = p0[u][:, :].rearrange("p (h k) -> p h k", k=SC)
                own(D0t["masked"], i, u, v.tensor_tensor(
                    p, ps[:, 2 * hf:2 * hf + 2, :].rearrange("p j (h k) -> p (j h) k", k=SC),
                    mask0[:, bass.ds(2 * i + t, 1), :].broadcast_to([P, H0 // 2, SC]), ALU.add))
                v.tensor_reduce(mx0[u][:, :], p, X, ALU.max).then_inc(D0t["maxima"].sem, 1)

            def slot0(i, u, first=False, final=False, after=False):
                k = tail0(u, first, after)
                if u == 1 and not (final or after):
                    queries_parts0(i + 1)
                if not after and not (final and u >= 2):
                    maxima0(i + (u >= 2), (u + 2) % 4)
                if "sums" in k:
                    c = k["sums"]
                    t = c % 2
                    wait(E0["projected"], i, c)
                    wait(G0s["bias"], i, c)
                    own(D0t["sums"], i, c, v.tensor_tensor(y0[:, :], ps[:, 7, 0:D], xb0[t][:, :], ALU.add))
                    own(D0t["stats"], i, c, v.bn_stats(st0[:, :], y0[:, :]))
                    settle(dve)
                    own(D0t["mean"], i, c, v.bn_aggr(mv0[t][:, 0:2], st0[:, :]))
                    v.tensor_scalar(mv0[t][:, 2:3], mv0[t][:, 1:2], EPS0, None, ALU.add).then_inc(D0t["eps"].sem, 1)
                if not after:
                    wait(A0["high"], i, u)
                    for half in range(2):
                        last = v.scalar_tensor_tensor(pl0[u % 2][:, 4 * half:4 * half + 4, :],
                                                      ps[:, 4 + half, :].rearrange("p (k n) -> p k n", k=4), WHOLE,
                                                      ph0[u % 2][:, 4 * half:4 * half + 4, :], ALU.mult, ALU.subtract)
                    last.then_inc(D0t["low"].sem, 1)
                if "sums" in k:
                    wait(G0s["root"], i, c)
                    wait(E0["normed_turned"], i, c - 2)
                    wait(G0s["scaled"], i, c - 2)
                    v.tensor_scalar(xn0[t][:, :], y0[:, :], mv0[t][:, 0:1], mv0[t][:, 3:4], ALU.subtract, ALU.mult
                                    ).then_inc(D0t["normed"].sem, 1)
                if "heads" in k:
                    c = k["heads"]
                    wait(E0["heads"], i, 2 * c + 1)
                    av = ps[:, 6, 0:H0 * (D0 + 1)].rearrange("p (h d) -> p h d", d=D0 + 1)
                    own(D0t["inverse"], i, c, v.reciprocal(ri0[:, :].unsqueeze(2), av[:, :, D0:D0 + 1]))
                    wait(E0["heads_turned"], i, c - 1)
                    for kt in range(KT):
                        last = v.tensor_tensor(
                            ao0[:, kt * P:(kt + 1) * P].rearrange("p (j h d) -> p j h d", j=4, h=4),
                            av[:, :, 0:D0].rearrange("p (j k h) d -> p j k h d", j=4, k=2)[:, :, kt],
                            ri0[:, :].rearrange("p (j k h) -> p j k h", j=4, k=2)[:, :, kt].unsqueeze(3).broadcast_to([P, 4, 4, D0]),
                            ALU.mult)
                    last.then_inc(D0t["heads"].sem, 1)
                if u == 0 and not (final or after):
                    queries0(i + 1)

            queries0(0)
            queries_parts0(0)
            maxima0(0, 0)
            maxima0(0, 1)
            for u in range(4):
                slot0(0, u, first=True)
            with dve.Fori(1, B - 1) as i:
                for u in range(4):
                    slot0(i, u)
            for u in range(4):
                slot0(B - 1, u, final=True)
            for u in range(4):
                slot0(B, u, after=True)

            def x1(i, s):
                wait(E1["v"], i, -2)
                v.tensor_copy(xb1T[s][:, :, :], xT[:, :, bass.ds(i * S, S)]).then_inc(D1t["x"].sem, 1)

            def rest1(i, s):
                x1(i, s)
                for kind in "qk":
                    wait(E1[kind], i)
                    wait(G1[f"{kind}_low"], i, -2)
                    for mt in range(KT):
                        o, x = t1[kind][s][:, mt, :], ps[:, 3 * s + "qk".index(kind), mt * S:(mt + 1) * S]
                        if kind == "q":
                            last = v.tensor_scalar(o, x, pvec("L1_bq", mt), SCALE1, ALU.add, ALU.mult)
                        else:
                            last = v.tensor_scalar(o, x, pvec("L1_bk", mt), None, ALU.add)
                    last.then_inc(D1t[kind].sem, 1)
                for kind in "qk":
                    wait(A1[f"{kind}_high"], i)
                    v.tensor_tensor(t1[kind][s][:, :, :], t1[kind][s][:, :, :], pt1[kind][s][:, 0, :, 0:S], ALU.subtract
                                    ).then_inc(D1t[f"{kind}_rest"].sem, 1)
                wait(A1["v_high"], i)
                wait(G1["v_low"], i, -2)
                v.tensor_tensor(t1["v"][s][:, :].rearrange("p (t h d) -> p t h d", t=QT_B, h=H1),
                                ps[:, 3 * s + 2, :].rearrange("p (t h d) -> p t h d", t=QT_B, h=H1),
                                vall1[:, 0, bass.ds(2 * i, 2), :, 0:D1], ALU.subtract).then_inc(D1t["v_rest"].sem, 1)

            def maxima1(i, u):
                wait(E1["scores"], i, u)
                two_banks = ps[:, 2 * (u % 2):2 * (u % 2) + 2, :]
                v.tensor_reduce(nm1[:, u, :], two_banks[:, :, 0:KEYS1], X, ALU.max, negate=True
                                ).then_inc(D1t["maxima"].sem, 1)

            def low1(i, u):
                wait(A1["high_own"], i, u)
                v.scalar_tensor_tensor(pl1[u % 2][:, 0:4, :], ps[:, 4 + u % 2, :].rearrange("p (k n) -> p k n", k=4), WHOLE,
                                       ph1[u % 2][:, 0:4, :], ALU.mult, ALU.subtract)
                wait(A1["high"], i, u)
                v.scalar_tensor_tensor(pl1[u % 2][:, 4, :], ps[:, 6, 0:P], WHOLE, ph1[u % 2][:, 4, :], ALU.mult,
                                       ALU.subtract).then_inc(D1t["low"].sem, 1)

            def heads_out1(i, k):
                wait(E1["heads"], i, 8 * k + 7)
                av = ps[:, 7, 0:H1 * (D1 + 1)].rearrange("p (h d) -> p h d", d=D1 + 1)
                own(D1t["inverse"], i, k, v.reciprocal(ri1[:, :].unsqueeze(2), av[:, :, D1:D1 + 1]))
                wait(E1["heads_turned"], i, k - 1)
                v.tensor_tensor(ao1[:, :].rearrange("p (h d) -> p h d", h=H1), av[:, :, 0:D1],
                                ri1[:, :].unsqueeze(2).broadcast_to([P, H1, D1]), ALU.mult).then_inc(D1t["heads"].sem, 1)

            def residual1(i, k, u):
                t = k % 2
                wait(E1["projected"], i, k)
                wait(G1["bias"], i, k)
                own(D1t["sums"], i, k, v.tensor_tensor(
                    y1[t][:, :].rearrange("p (k n) -> p k n", k=KT), ps[:, 2 * (u % 2):2 * (u % 2) + 2, KEYS1:KEYS1 + P],
                    xb1[t][:, :].rearrange("p (k n) -> p k n", k=KT), ALU.add))

            def mean_square1(i, k):
                t = k % 2
                own(D1t["squares"], i, k, v.tensor_tensor_reduce(sq1[:, :], y1[t][:, :], y1[t][:, :], 1.0, 0.0, ALU.mult,
                                                                 ALU.add, ms1[t][:, 0:1]))
                v.tensor_scalar(ms1[t][:, 1:2], ms1[t][:, 0:1], 1.0 / D, EPS1, ALU.mult, ALU.add).then_inc(D1t["mean"].sem, 1)

            def normed1(i, k):
                wait(G1["root"], i, k)
                wait(E1["normed_turned"], i, k - 1)
                v.tensor_scalar(n1[:, :], y1[k % 2][:, :], ms1[k % 2][:, 2:3], None, ALU.mult).then_inc(D1t["normed"].sem, 1)

            def batch1(i, first=False, final=False):
                for u in range(16):
                    if not (final and u >= 14):
                        maxima1(i + (u >= 14), (u + 2) % 16)
                    tail = tail1(u, first)
                    if "project" in tail:
                        residual1(i, tail["project"], u)
                    if "free" in tail:
                        normed1(i, tail["free"])
                    low1(i, u)
                    if "project" in tail:
                        mean_square1(i, tail["project"])
                    if u == 8:
                        heads_out1(i, 0)
                heads_out1(i, 1)

            for t in (A0["normed_turned"], G0s["rows"], E0["normed_turned"]):
                dve.wait_ge(t.sem, t.end(B))
            split = D1t["ctx_split"]
            dve.wait_ge(pdv.sem, pdv.now(0, "v1"))
            own(split, 0, 0, v.tensor_copy(vp1[:, 0, :, :, :], vc1[:, :, :, :]))
            own(split, 0, 1, v.tensor_tensor(vc1[:, :, :, :], vc1[:, :, :, :], vp1[:, 0, :, :, :], ALU.subtract))
            own(split, 0, 2, v.tensor_copy(vp1[:, 1, :, :, :], vc1[:, :, :, :]))
            own(split, 0, 3, v.tensor_tensor(vp1[:, 2, :, :, :], vc1[:, :, :, :], vp1[:, 1, :, :, :], ALU.subtract))
            wait(E1["k_ctx"], 0)
            for mt in range(KT):
                last = v.tensor_scalar(tc1[:, mt, :], ps[:, 6 + mt, :], pvec("L1_bk", mt), None, ALU.add)
            own(D1t["k_ctx"], 0, 0, last)
            split = D1t["k_ctx_split"]
            own(split, 0, 0, v.tensor_copy(pc1[:, 0, :, :], tc1[:, :, :]))
            own(split, 0, 1, v.tensor_tensor(tc1[:, :, :], tc1[:, :, :], pc1[:, 0, :, :], ALU.subtract))
            own(split, 0, 2, v.tensor_copy(pc1[:, 1, :, :], tc1[:, :, :]))
            own(split, 0, 3, v.tensor_tensor(pc1[:, 2, :, :], tc1[:, :, :], pc1[:, 1, :, :], ALU.subtract))
            with dve.Fori(0, B // 2) as j:
                for s in range(2):
                    rest1(2 * j + s, s)
            wait(G1["v_low"], B, -1)
            for s in range(2):
                dve.wait_ge(dma_part[s], 32 * (B // 2))
            maxima1(0, 0)
            maxima1(0, 1)
            batch1(0, first=True)
            with dve.Fori(1, B - 1) as i:
                batch1(i)
            batch1(B - 1, final=True)
            residual1(B, -1, 1 + TO_PROJECT)
            mean_square1(B, -1)
            normed1(B, -1)

            def norm_rows(s, i, t, rows, stats, mv, rs, eps, dst, name, free):
                settle(dve)
                step(s, i, f"bn{t}", v.bn_stats(stats[:, :], rows))
                settle(dve)
                step(s, i, f"mv{t}", v.bn_aggr(mv[:, 0:2], stats[:, :]))
                v.tensor_scalar(mv[:, 2:3], mv[:, 1:2], eps, None, ALU.add).then_inc(s.sem, s.did(f"eps{t}"))
                dve.wait_ge(rs.sem, rs.now(i, f"rs{t}"))
                free()
                v.tensor_scalar(dst, rows, mv[:, 0:1], mv[:, 3:4], ALU.subtract, ALU.mult).then_inc(s.sem, s.did(f"{name}{t}"))

            def mlp_rows(m, w):
                with dve.Fori(0, NCH) as i:
                    if m:
                        for t in range(QC):
                            def free(t=t):
                                dve.wait_ge(em[1].sem, em[1].now(i, f"x{t - 2}") if t >= 2 else em[1].prev(i, f"x{t + 2}"))
                            norm_rows(dm[1], i, t, xr[:, bass.ds(i * QC + t, 1), :].rearrange("p o n -> p (o n)"), stm, mvm[t % 2],
                                      gm[1], EPS3, hnm[t % 2][:, :], "xn", free)
                    for t in range(QC):
                        dve.wait_ge(em[m].sem, em[m].now(i, f"o{t}"))
                        dve.wait_ge(gm[m].sem, gm[m].now(i, f"xb{t}"))
                        v.tensor_tensor(xr[:, bass.ds(i * QC + t, 1), :].rearrange("p o n -> p (o n)"), ps[:, 2 + t % 2, 0:D], w["xb"][t % 2][:, :], ALU.add
                                        ).then_inc(dm[m].sem, dm[m].did(f"o{t}"))

            mlp_rows(0, m1)

            dve.wait_ge(pe2p.sem, pe2p.now(0, "k"))
            for mt in range(KT):
                last = v.tensor_copy(t2[:, 0, mt, :], ps[:, mt, :])
            last.then_inc(dv2p.sem, dv2p.did("k"))
            dve.wait_ge(pe2p.sem, pe2p.now(0, "kq"))
            for mt in range(KT):
                last = v.tensor_copy(k2[:, mt, :, :], ps[:, 4 + mt, :].rearrange("p (b k) -> p b k", b=B))
            last.then_inc(dv2p.sem, dv2p.did("kq"))
            dve.wait_ge(pe2p.sem, pe2p.now(0, "v"))
            for mt in range(KT):
                last = v.tensor_copy(t2[:, 1, mt, :], ps[:, 2 + mt, :])
            last.then_inc(dv2p.sem, dv2p.did("v"))
            dve.wait_ge(pe2p.sem, pe2p.now(0, "vo"))
            v.tensor_scalar(v2[:, :, :].rearrange("p b n -> p (b n)"), ps[0:SC, 4:8, :].rearrange("p k n -> p (k n)"),
                            alpha[0:SC, :], None, ALU.mult).then_inc(dv2p.sem, dv2p.did("vo"))
            with dve.Fori(0, B) as i:
                for t in range(2):
                    dve.wait_ge(e2.sem, e2.now(i, f"s{t}"))
                    dve.wait_ge(a2.sem, a2.prev(i, f"exp{t}"))
                    dve.wait_ge(d2.sem, d2.prev(i, f"y{t}"))
                    step(d2, i, f"m{t}", v.tensor_reduce(sm2[t][:, 3:4], ps[:, 2 + t, 0:SC], X, ALU.max, negate=True))
                    v.tensor_scalar(sm2[t][:, 0:1], sm2[t][:, 3:4], SCALE2, None, ALU.mult).then_inc(d2.sem, d2.did(f"max{t}"))
                for t in range(2):
                    dve.wait_ge(a2.sem, a2.now(i, f"exp{t}"))
                    step(d2, i, f"s{t}", v.tensor_reduce(sm2[t][:, 1:2], p2[t][:, :], X, ALU.add))
                    step(d2, i, f"sum{t}", v.reciprocal(sm2[t][:, 2:3], sm2[t][:, 1:2]))
                for t in range(2):
                    dve.wait_ge(e2.sem, e2.now(i, f"o{t}"))
                    xq = xr[:, bass.ds(2 * i + t, 1), :].rearrange("p o n -> p (o n)")
                    v.scalar_tensor_tensor(xq, ps[:, 6 + t, 0:D], sm2[t][:, 2:3], xq, ALU.mult, ALU.add).then_inc(d2.sem, d2.did(f"y{t}"))

            def head_copies(a):
                with dve.Fori(0, HP) as i:
                    for t in range(2):
                        w = bun[t]
                        dve.wait_ge(dma_bun[a][t], 16 * i + 16)
                        dve.wait_ge(ep[a].sem, ep[a].now(i, f"k{t}"))
                        dve.wait_ge(ep[a].sem, ep[a].now(i, "b0") if t else ep[a].prev(i, "b1"))
                        v.tensor_scalar(kh[:, :], ps[:, 0, :], w[:, 4 * D:4 * D + 1], None, ALU.add).then_inc(dp[a].sem, dp[a].did(f"k{t}"))
                        dve.wait_ge(ep[a].sem, ep[a].now(i, f"w{t}"))
                        v.tensor_copy(v3[HALF * t:HALF * (t + 1), 1:B:2, bass.ds(i, 1), :].rearrange("p b o n -> p b (o n)"),
                                      ps[HALF:P, 5:7, :].rearrange("p k (c n) -> p (k c) n", c=2)).then_inc(dp[a].sem, dp[a].did(f"w{t}"))
                        dve.wait_ge(ep[a].sem, ep[a].now(i, f"r{t}"))
                        v.tensor_copy(gb3[:, :, bass.ds(2 * i + t, 1)], ps[:, 7, D:D + 2].unsqueeze(2))
                        v.tensor_copy(bb3[:, bass.ds(2 * i + t, 1)], ps[0:1, 7, D + 4:D + 5]).then_inc(dp[a].sem, dp[a].did(f"m{t}"))
                        v.tensor_tensor(vb3[:, :], vb3[:, :], ps[0:H3, 7, 0:D], ALU.add).then_inc(dp[a].sem, dp[a].did(f"vb{t}"))

            def attend(a):
                def wait(t, i, k):
                    dve.wait_ge(t.sem, t.at(i, k + a * B * t.per))

                def own3(name, i, k, ins):
                    ins.then_inc(D3t[name].sem, 1)
                    wait(D3t[name], i, k)

                def rows(i, k):
                    return xr[:, bass.ds(2 * i + k, 1), :].rearrange("p o n -> p (o n)")

                def normed(i, k):
                    mv = mv3[k % 2]
                    settle(dve)
                    own3("stats", i, k, v.bn_stats(st3[:, :], rows(i, k)))
                    settle(dve)
                    own3("mean", i, k, v.bn_aggr(mv[:, 0:2], st3[:, :]))
                    v.tensor_scalar(mv[:, 2:3], mv[:, 1:2], EPS3, None, ALU.add).then_inc(D3t["eps"].sem, 1)
                    wait(G3["root"], i, k)
                    wait(E3["normed"], i, k - 2)
                    v.tensor_scalar(hn[k % 2][:, :], rows(i, k), mv[:, 0:1], mv[:, 3:4], ALU.subtract, ALU.mult
                                    ).then_inc(D3t["normed"].sem, 1)

                def shifted(i, k):
                    t = k % 2
                    wait(E3["scores"], i, k)
                    wait(E3["turned_bias"], i, k - 2)
                    sc = ps[:, 2 * t:2 * t + 2, :].rearrange("p c (h k) -> p (c h) k", k=SC)
                    sbk = ps[:, 6, D:D + H3]
                    own3("max", i, k, v.tensor_reduce(mx3[t][:, :], sc, X, ALU.max))
                    own3("max_bias", i, k, v.tensor_tensor(mx3[t][:, :], sbk, mx3[t][:, :], ALU.max))
                    v.tensor_tensor(p3[t][:, 0:KEYS3].rearrange("p (h k) -> p h k", k=SC), sc,
                                    mx3[t][:, :].unsqueeze(2).broadcast_to([P, H3, SC]), ALU.subtract).then_inc(D3t["shifted"].sem, 1)
                    v.tensor_tensor(p3[t][:, KEYS3:], sbk, mx3[t][:, :], ALU.subtract).then_inc(D3t["shifted_bias"].sem, 1)

                def inverse(i, k):
                    t = k % 2
                    wait(A3["weights"], i, k)
                    wait(G3["weights"], i, k - 2)
                    own3("sum", i, k, v.tensor_reduce(sm3[t][:, :], p3[t][:, 0:KEYS3].rearrange("p (h k) -> p h k", k=SC), X, ALU.add))
                    own3("sum_bias", i, k, v.tensor_tensor(sm3[t][:, :], sm3[t][:, :], p3[t][:, KEYS3:], ALU.add))
                    own3("inverse", i, k, v.reciprocal(sm3[t][:, :], sm3[t][:, :]))
                    v.tensor_tensor(p3[t][:, KEYS3:], p3[t][:, KEYS3:], sm3[t][:, :], ALU.mult).then_inc(D3t["weight_bias"].sem, 1)

                def residual(i, k):
                    wait(E3["out"], i, k)
                    wait(G3["bias"], i, k)
                    v.tensor_tensor(rows(i, k), ps[:, 7, 0:D], xb3[k % 2][:, :], ALU.add).then_inc(D3t["rows"].sem, 1)

                def batch(i, final=False):
                    for k in range(2):
                        if not final:
                            normed(i, k + 2)
                        if not (final and k):
                            shifted(i, k + 1)
                            inverse(i, k + 1)
                        residual(i, k)

                normed(0, 0)
                normed(0, 1)
                shifted(0, 0)
                inverse(0, 0)
                with dve.Fori(0, B - 1) as i:
                    batch(i)
                batch(B - 1, final=True)

            for a in range(2):
                if a == 1:
                    dve.wait_ge(E3["out"].sem, attn_end(E3["out"], 0))
                    dve.wait_ge(A3["copied_bias"].sem, attn_end(A3["copied_bias"], 0))
                else:
                    dve.wait_ge(e2.sem, e2.end(B))
                    dve.wait_ge(a2.sem, a2.end(B))
                dve.wait_ge(vbz[a], 1)
                head_copies(a)
                dve.wait_ge(ap_[a].sem, ap_[a].end(HP))
                attend(a)
            dve.wait_ge(E3["out"].sem, attn_end(E3["out"], 1))
            mlp_rows(1, m3)

        @block.gpsimd
        def _(pool):
            g = nc.gpsimd
            for s in [ppo, g2] + gm:
                pool.sem_inc(s.sem, s.per)
            for s in own_pool:
                pool.sem_inc(s.sem, s.seed)
            pool.wait_ge(dma_k, 80)
            pool.wait_ge(dma_x, 16)

            def root(dst, src):
                return g.tensor_tensor(dst, src, const("minus_half"), ALU.pow)

            def xq(i, t):
                return xr[:, bass.ds(2 * i + t, 1), :].rearrange("p o n -> p (o n)")

            def wait(t, i, k=0):
                pool.wait_ge(t.sem, t.at(i, k))

            def keys0(i):
                wait(E0["scores"], i, -1)
                settle(pool)
                k = kbd[:, :, bass.ds(i, 1), :].rearrange("p k o n -> p k (o n)")
                g.tensor_copy(kp0[0][:, :, :], k).then_inc(G0s["k_high"].sem, 1)
                wait(G0s["k_high"], i)
                settle(pool)
                g.tensor_tensor(kp0[1][:, :, :], k, kp0[0][:, :, :].bitcast(F32), ALU.subtract).then_inc(G0s["k_low"].sem, 1)

            def shift0(i, u):
                wait(D0t["maxima"], i, u)
                p = p0[u][:, :].rearrange("p (h k) -> p h k", k=SC)
                g.tensor_tensor(p, p, mx0[u][:, :].unsqueeze(2).broadcast_to([P, H0 // 2, SC]), ALU.subtract).then_inc(G0s["shifted"].sem, 1)

            def slot0(i, u, first=False, final=False, after=False):
                k = tail0(u, first, after)
                if u == 1 and not (final or after):
                    keys0(i + 1)
                if not after and not (final and u >= 2):
                    shift0(i + (u >= 2), (u + 2) % 4)
                if "sums" in k:
                    c = k["sums"]
                    wait(D0t["eps"], i, c)
                    root(mv0[c % 2][:, 3:4], mv0[c % 2][:, 2:3]).then_inc(G0s["root"].sem, 1)
                if u == 0 and not after:
                    wait(E0["heads"], i, -1)
                    settle(pool)
                    g.tensor_copy(vb0[:, :, :, :, :].rearrange("p c g h d -> p c (g h d)"),
                                  vp0[:, :, bass.ds(i * G0, G0), :, :].rearrange("p c g h d -> p c (g h d)")
                                  ).then_inc(G0s["values"].sem, 1)
                if "turned" in k:
                    c = k["turned"]
                    wait(D0t["normed"], i, c)
                    wait(G0s["rows"], i, c - 1)
                    g.tensor_tensor(xg0[:, :], xn0[c % 2][:, :], prow("L0_gamma"), ALU.mult).then_inc(G0s["scaled"].sem, 1)
                    wait(G0s["scaled"], i, c)
                    settle(pool)
                    g.tensor_tensor(xq(i, c), xg0[:, :], prow("L0_beta"), ALU.add).then_inc(G0s["rows"].sem, 1)
                if "projected" in k:
                    c = k["projected"]
                    wait(D0t["sums"], i, c - 2)
                    settle(pool)
                    g.tensor_tensor(xb0[c % 2][:, :], xq(i, c), prow("L0_bo"), ALU.add).then_inc(G0s["bias"].sem, 1)

            pool.wait_ge(split0.sem, split0.at(0, 3))
            keys0(0)
            shift0(0, 0)
            shift0(0, 1)
            for u in range(4):
                slot0(0, u, first=True)
            with pool.Fori(1, B - 1) as i:
                for u in range(4):
                    slot0(i, u)
            for u in range(4):
                slot0(B - 1, u, final=True)
            for u in range(4):
                slot0(B, u, after=True)

            def low_parts1(i, s):
                for kind in "qk":
                    wait(A1[f"{kind}_mid"], i)
                    g.tensor_tensor(pt1[kind][s][:, 2, :, 0:S], t1[kind][s][:, :, :], pt1[kind][s][:, 1, :, 0:S], ALU.subtract
                                    ).then_inc(G1[f"{kind}_low"].sem, 1)
                wait(A1["v_mid"], i)
                settle(pool)
                g.tensor_tensor(vall1[:, 2, bass.ds(2 * i, 2), :, 0:D1], t1["v"][s][:, :].rearrange("p (t h d) -> p t h d", t=QT_B, h=H1),
                                vall1[:, 1, bass.ds(2 * i, 2), :, 0:D1], ALU.subtract).then_inc(G1["v_low"].sem, 1)

            def values1(i, s):
                wait(G1["v_low"], i)
                wait(E1["heads"], i, -17)
                settle(pool)
                g.tensor_copy(vt1[s][:, :, 0:2, :, :].rearrange("p c t h d -> p c (t h d)"),
                              vall1[:, :, bass.ds(2 * i, 2), :, :].rearrange("p c t h d -> p c (t h d)"))
                g.tensor_copy(vt1[s][:, :, 2, :, :].rearrange("p c h d -> p c (h d)"),
                              vp1[:, :, bass.ds(i, 1), :, :].rearrange("p c o h d -> p c (o h d)")).then_inc(G1["values"].sem, 1)
                wait(G1["values"], i)
                settle(pool)

            def alone1(t, i, k, ins):
                ins.then_inc(t.sem, 1)
                wait(t, i, k)
                settle(pool)

            def mask_row1(i, s):
                wait(E1["scores"], i, -17)
                settle(pool)
                alone1(G1["mask"], i, 0, g.tensor_copy(
                    ks1[s][MASK_ROW:, :, S:KEYS1],
                    mask1[MASK_ROW:MASK_ROW + 1, bass.ds(i * SC, SC)].unsqueeze(1).broadcast_to([1, H1, SC])))

            def root1(i, k):
                wait(D1t["mean"], i, k)
                root(ms1[k % 2][:, 2:3], ms1[k % 2][:, 1:2]).then_inc(G1["root"].sem, 1)

            def batch1(i, s, first=False, final=False):
                if not first:
                    root1(i, -1)
                for t in range(2):
                    wait(D1t["sums"], i, t - 2)
                    settle(pool)
                    g.tensor_tensor(xb1[t][:, :], xq(i, t), prow("L1_bo"), ALU.add).then_inc(G1["bias"].sem, 1)
                if not final:
                    values1(i + 1, 1 - s)
                    if not first:
                        mask_row1(i + 1, 1 - s)
                root1(i, 0)

            for t in (A0["normed_turned"], D0t["normed"], E0["normed_turned"], G0s["rows"]):
                pool.wait_ge(t.sem, t.end(B))
            wait(D1t["ctx_split"], 0, 3)
            pool.wait_ge(pdv.sem, pdv.now(0, "m1"))
            g.memset(vall1[:, 0, :, :, D1:D1 + 1], 1.0)
            g.memset(vall1[:, 1:3, :, :, D1:D1 + 1], 0.0).then_inc(G1["ones"].sem, 1)
            wait(G1["ones"], 0)
            for s in range(2):
                alone1(G1["rows"], 0, 2 * s, g.memset(qs1[s][MASK_ROW:, :, :], 1.0))
                alone1(G1["rows"], 0, 2 * s + 1, g.memset(ks1[s][MASK_ROW:, :, 0:S], 0.0))
            for s in range(2):
                mask_row1(s, s)
            for s in range(2):
                low_parts1(s, s)
            values1(0, 0)
            with pool.Fori(1, B // 2) as j:
                for s in range(2):
                    low_parts1(2 * j + s, s)
            for t in (G1["v_low"], D1t["v_rest"]):
                pool.wait_ge(t.sem, t.end(B))
            for s in range(2):
                pool.wait_ge(dma_part[s], 32 * (B // 2))
            batch1(0, 0, first=True)
            with pool.Fori(0, (B - 2) // 2) as j:
                for s in range(2):
                    batch1(2 * j + s + 1, 1 - s)
            batch1(B - 1, 1, final=True)
            root1(B, -1)

            def mlp_bias(m, w, bias):
                with pool.Fori(0, NCH) as i:
                    if m:
                        for t in range(QC):
                            pool.wait_ge(dm[1].sem, dm[1].now(i, f"eps{t}"))
                            root(mvm[t % 2][:, 3:4], mvm[t % 2][:, 2:3]).then_inc(gm[1].sem, gm[1].did(f"rs{t}"))
                    for t in range(QC):
                        pool.wait_ge(dm[m].sem, dm[m].now(i, f"o{t - 2}") if t >= 2 else dm[m].prev(i, f"o{t + 2}"))
                        settle(pool)
                        g.tensor_tensor(w["xb"][t % 2][:, :], xr[:, bass.ds(i * QC + t, 1), :].rearrange("p o n -> p (o n)"), prow(bias), ALU.add
                                        ).then_inc(gm[m].sem, gm[m].did(f"xb{t}"))

            pool.wait_ge(E1["normed_turned"].sem, E1["normed_turned"].end(B))
            pool.wait_ge(D1t["normed"].sem, D1t["normed"].end(B))
            pool.wait_ge(A1["normed_turned"].sem, A1["normed_turned"].end(B))
            mlp_bias(0, m1, "L1_b2")

            pool.wait_ge(dm[0].sem, dm[0].end(NCH))
            with pool.Fori(0, B) as i:
                for t in range(2):
                    pool.wait_ge(e2.sem, e2.prev(i, f"xt{t}"))
                    settle(pool)
                    g.tensor_copy(x2[t][:, :], xq(i, t)).then_inc(g2.sem, g2.did(f"x{t}"))

            def attend(a):
                def wait(t, i, k):
                    pool.wait_ge(t.sem, t.at(i, k + a * B * t.per))

                def root3(i, k):
                    wait(D3t["eps"], i, k)
                    root(mv3[k % 2][:, 3:4], mv3[k % 2][:, 2:3]).then_inc(G3["root"].sem, 1)

                def weights(i, k):
                    t = k % 2
                    wait(D3t["inverse"], i, k)
                    p = p3[t][:, 0:KEYS3].rearrange("p (h k) -> p h k", k=SC)
                    g.tensor_tensor(p, p, sm3[t][:, :].unsqueeze(2).broadcast_to([P, H3, SC]), ALU.mult
                                    ).then_inc(G3["weights"].sem, 1)

                def batch(i, final=False):
                    for k in range(2):
                        if not final:
                            root3(i, k + 2)
                        wait(D3t["rows"], i, k - 2)
                        settle(pool)
                        g.tensor_tensor(xb3[k][:, :], xq(i, k), prow(f"bo{a + 1}"), ALU.add).then_inc(G3["bias"].sem, 1)
                        if not (final and k):
                            weights(i, k + 1)

                root3(0, 0)
                root3(0, 1)
                weights(0, 0)
                with pool.Fori(0, B - 1) as i:
                    batch(i)
                batch(B - 1, final=True)

            for a in range(2):
                if a == 0:
                    pool.wait_ge(e2.sem, e2.end(B))
                    pool.wait_ge(d2.sem, d2.end(B))
                else:
                    pool.wait_ge(E3["out"].sem, attn_end(E3["out"], 0))
                    pool.wait_ge(D3t["rows"].sem, attn_end(D3t["rows"], 0))
                g.memset(one3[:, :], 1.0)
                g.memset(vb3[:, :], 0.0).then_inc(vbz[a], 1)
                pool.wait_ge(dp[a].sem, dp[a].end(HP))
                pool.wait_ge(ep[a].sem, ep[a].end(HP))
                pool.wait_ge(ap_[a].sem, ap_[a].end(HP))
                attend(a)
            pool.wait_ge(E3["out"].sem, attn_end(E3["out"], 1))
            pool.wait_ge(D3t["rows"].sem, attn_end(D3t["rows"], 1))
            mlp_bias(1, m3, "b_fc2")


def kernel(**inputs):
    import concourse.bacc as bacc
    from concourse.bass_utils import run_bass_kernel_spmd

    a = {k: np.asarray(v) for k, v in inputs.items()}

    def tiles(w):
        return np.ascontiguousarray(w.reshape(-1, P, w.shape[1]).transpose(1, 0, 2)).reshape(P, -1)

    def column(v):
        return v.reshape(-1, P).T

    f = np.float32
    rep = lambda w: np.repeat(w.reshape(w.shape[0], G0, 1, D0), H0 // G0, 2).reshape(w.shape[0], D)
    rows = np.arange(P)
    const = np.concatenate([
        np.eye(P, dtype=f), (rows[:, None] // D0 % 4 == np.arange(4)).astype(f),
        (rows[:, None] // D1 % 2 == np.arange(2)).astype(f), (rows[:, None] // HALF == np.arange(2)).astype(f),
        np.full((P, 1), -0.5, f)], 1)
    kv, kvb = a["L1_xattn_kv_w"].reshape(D, D, 2), a["L1_xattn_kv_b"].reshape(D, 2)
    vecs = {
        "L0_bq": a["L0_xattn_bq"], "L0_bk": rep(a["L0_xattn_bk"][None])[0], "L0_bv": rep(a["L0_xattn_bv"][None])[0],
        "L0_gamma": a["L0_xattn_gamma"], "L0_beta": a["L0_xattn_beta"],
        "L1_bq": a["L1_xattn_q_b"], "L1_bk": kvb[:, 0], "L1_bv": kvb[:, 1], "L1_norm": a["L1_xattn_postnorm_w"],
        "ln1_s": a["L3_xattn_ln1_scale"], "ln1_o": a["L3_xattn_ln1_offset"],
        "ln2_s": a["L3_xattn_ln2_scale"], "ln2_o": a["L3_xattn_ln2_offset"],
        "lnm_s": a["L3_xattn_ln_mlp_scale"], "lnm_o": a["L3_xattn_ln_mlp_offset"]}
    rowv = {"L0_bo": a["L0_xattn_bo"], "L0_gamma": a["L0_xattn_gamma"], "L0_beta": a["L0_xattn_beta"],
            "L1_bo": a["L1_xattn_out_b"], "L1_b2": a["L1_xattn_mlp_b2"], "bo1": a["L3_xattn_bo1"],
            "bo2": a["L3_xattn_bo2"], "b_fc2": a["L3_xattn_b_fc2"]}

    def heads(n):
        g = lambda name: a[f"L3_xattn_{name}{n}"]
        out = np.zeros((H3, P, BUN), f)
        for h in range(H3):
            c = slice(h * D3, (h + 1) * D3)
            out[h, :, 0:D] = tiles(g("wk")[:, c])
            out[h, :, D:2 * D] = g("wq")[:, c].T
            out[h, :, 2 * D:3 * D] = tiles(g("wv")[:, c])
            out[h, :, 3 * D:4 * D] = g("wo")[c]
            for k, v in enumerate((g("bk")[c], g("bq")[c], g("bv")[c], g("bias_k")[0, 0, h])):
                out[h, :, 4 * D + k] = v
            out[h, :, 4 * D + 4 + h] = g("bias_v")[0, 0, h]
        return out

    arrays = {
        "x": a["x"], "xT": tiles(a["x"].reshape(T, D).T).reshape(P, KT, T),
        "ctxT": tiles(a["ctx_2048"].reshape(C, D).T).reshape(P, KT, C),
        "mask0": a["mask_Bx1xSxS2_ff0"], "mask1": a["mask_BxS2_ik0"].reshape(C),
        "const": const, "alpha": a["L2_xattn_alpha"].reshape(1),
        "vecs": np.concatenate([column(vecs[n]) for n in VECS] + [column(a["L1_xattn_mlp_b1"]), column(a["L3_xattn_b_fc1"])], 1),
        "rows": np.stack([rowv[n] for n in ROWS]),
        "w0": np.concatenate([tiles(a["L0_xattn_Wq"]), tiles(rep(a["L0_xattn_Wk"])), tiles(a["L0_xattn_Wo"]),
                              tiles(a["L0_xattn_Wv"])], 1),
        "w1": np.concatenate([tiles(a["L1_xattn_q_w"]), tiles(kv[:, :, 0]), tiles(kv[:, :, 1]), tiles(a["L1_xattn_out_w"])], 1),
        "w2": np.concatenate([tiles(a["L2_xattn_w_q"]), tiles(a["L2_xattn_w_k"].T), tiles(a["L2_xattn_w_v"].T),
                              tiles(a["L2_xattn_w_o"].T)], 1),
        "m1a": tiles(a["L1_xattn_mlp_w1"]).reshape(P, KT, F), "m1b": tiles(a["L1_xattn_mlp_w2"]).reshape(P, FT, D),
        "m3a": tiles(a["L3_xattn_w_fc1"]).reshape(P, KT, F), "m3b": tiles(a["L3_xattn_w_fc2"]).reshape(P, FT, D),
        "heads0": heads(1), "heads1": heads(2),
    }
    arrays = {k: np.ascontiguousarray(v) for k, v in arrays.items()}
    nc = bacc.Bacc("TRN2", target_bir_lowering=False, num_devices=1)
    io = {k: nc.dram_tensor(f"in_{k}", v.shape, mybir.dt.from_np(v.dtype), kind="ExternalInput").ap() for k, v in arrays.items()}
    out = nc.dram_tensor("out", (B, S, D), F32, kind="ExternalOutput").ap()
    build(nc, io, out)
    r = run_bass_kernel_spmd(nc, [{f"in_{k}": v for k, v in arrays.items()}], core_ids=[0])
    return r.results[0]["out"]
```
